# Optimizing a Trainium2 kernel written in Bass

```python
import numpy as np
import jax
import jax.numpy as jnp

def _softmax(x, axis=-1):
    return jax.nn.softmax(x, axis=axis)

def _gelu(x):
    return jax.nn.gelu(x, approximate=True)

def _silu(x):
    return jax.nn.silu(x)

def _sigmoid(x):
    return jax.nn.sigmoid(x)

def _layernorm(x, axis=-1, eps=1e-05):
    m = jnp.mean(x, axis=axis, keepdims=True)
    v = jnp.var(x, axis=axis, keepdims=True)
    return (x - m) / jnp.sqrt(v + eps)

def _scatter_add(tgt, idx, src, axis=0):
    return tgt.at[idx].add(src)

def _segment_sum(src, seg, n):
    return jax.ops.segment_sum(src, seg, n)
kernel_name = 'mk_seq_preln_d2_jaxref_r8_9adbea'

def setup_inputs(seed: int=0):
    np.random.seed(seed)
    _w = jnp.asarray

    def _L0_attn_setup():
        import jax, jax.numpy as jnp
        import numpy as np
        D_MODEL = 128
        N_HEADS = 16
        D_HEAD = D_MODEL // N_HEADS
        EPS = 1e-06

        def _phi(x):
            return jax.nn.elu(x) + 1.0
        key = jax.random.key(seed)
        k1, k2, k3 = jax.random.split(key, 3)
        x = jax.random.normal(k1, (4, 512, D_MODEL), dtype=jnp.float32)
        s = 1.0 / np.sqrt(D_MODEL)
        w_qkv = jax.random.uniform(k2, (3 * D_MODEL, D_MODEL), minval=-s, maxval=s, dtype=jnp.float32)
        w_out = jax.random.uniform(k3, (D_MODEL, D_MODEL), minval=-s, maxval=s, dtype=jnp.float32)
        return {'x': x, 'w_qkv': w_qkv, 'w_out': w_out}
    _L0_attn_in = _L0_attn_setup()

    def _L0_ffn_setup():
        import jax, jax.numpy as jnp
        import numpy as np
        TOPK = 2
        CAPACITY_FACTOR = 1.0
        EPS = 1e-06
        B, S, D = (4, 512, 128)
        E = 8
        SUB_H = 256 // E
        key = jax.random.key(seed)
        ks = jax.random.split(key, 7)
        x = jax.random.normal(ks[0], (B, S, D), dtype=jnp.float32)
        w_gate_w = jax.random.normal(ks[1], (D, E), dtype=jnp.float32) * 0.02
        w_gate_b = jnp.zeros((E,), jnp.float32)
        W1 = jax.random.normal(ks[2], (E, D, SUB_H), dtype=jnp.float32) * 0.02
        b1 = jnp.zeros((E, SUB_H), jnp.float32)
        W2 = jax.random.normal(ks[3], (E, SUB_H, D), dtype=jnp.float32) * 0.02
        b2 = jnp.zeros((E, D), jnp.float32)
        return {'x': x, 'w_gate_w': w_gate_w, 'w_gate_b': w_gate_b, 'W1': W1, 'b1': b1, 'W2': W2, 'b2': b2}
    _L0_ffn_in = _L0_ffn_setup()

    def _L1_attn_setup():
        import jax, jax.numpy as jnp
        import numpy as np
        B, T, C = (64, 32, 128)
        N_HEAD, HEAD_SIZE, KV_RANK = (16, 64, 128)
        BLOCK_SIZE = 32
        key = jax.random.key(seed)
        ks = jax.random.split(key, 5)
        HD = N_HEAD * HEAD_SIZE

        def init(k, shape):
            fan_in = shape[0]
            bound = 1.0 / np.sqrt(fan_in)
            return jax.random.uniform(k, shape, jnp.float32, -bound, bound)
        return {'x': jax.random.normal(ks[0], (B, T, C), jnp.float32), 'w_kv_down': init(ks[1], (C, KV_RANK)), 'w_kv_up': init(ks[2], (KV_RANK, 2 * HD)), 'w_q': init(ks[3], (C, HD)), 'w_out': init(ks[4], (HD, C))}
    _L1_attn_in = _L1_attn_setup()

    def _L1_ffn_setup():
        import jax, jax.numpy as jnp
        import numpy as np
        MODEL_DIM = 128
        HIDDEN = 256
        NUM_GROUPS = 2
        EXPERTS_PER_GP = 4
        NUM_EXPERTS = NUM_GROUPS * EXPERTS_PER_GP
        TOP_K = 2
        B, T = (2, 256)

        def _swiglu(x):
            a, b = jnp.split(x, 2, axis=-1)
            return jax.nn.silu(a) * b
        key = jax.random.key(seed)
        ks = jax.random.split(key, 7)
        s = 0.02
        return {'x': jax.random.normal(ks[0], (B, T, MODEL_DIM), jnp.float32), 'w_in': jax.random.normal(ks[1], (HIDDEN * 2, MODEL_DIM), jnp.float32) * s, 'w_out': jax.random.normal(ks[2], (MODEL_DIM, HIDDEN), jnp.float32) * s, 'w1': jax.random.normal(ks[3], (HIDDEN * 2, MODEL_DIM), jnp.float32) * s, 'w2': jax.random.normal(ks[4], (NUM_EXPERTS, MODEL_DIM, HIDDEN), jnp.float32) * s, 'wg': jax.random.normal(ks[5], (NUM_GROUPS, MODEL_DIM), jnp.float32) * s, 'we': jax.random.normal(ks[6], (NUM_EXPERTS, MODEL_DIM), jnp.float32) * s, 'gb': jnp.zeros((NUM_GROUPS,), jnp.float32), 'eb': jnp.zeros((NUM_EXPERTS,), jnp.float32)}
    _L1_ffn_in = _L1_ffn_setup()
    _d = {'L0_attn_x': _L0_attn_in['x'], 'L0_attn_w_qkv': _L0_attn_in['w_qkv'], 'L0_attn_w_out': _L0_attn_in['w_out'], 'L0_ffn_w_gate_w': _L0_ffn_in['w_gate_w'], 'L0_ffn_w_gate_b': _L0_ffn_in['w_gate_b'], 'L0_ffn_W1': _L0_ffn_in['W1'], 'L0_ffn_b1': _L0_ffn_in['b1'], 'L0_ffn_W2': _L0_ffn_in['W2'], 'L0_ffn_b2': _L0_ffn_in['b2'], 'L1_attn_w_kv_down': _L1_attn_in['w_kv_down'], 'L1_attn_w_kv_up': _L1_attn_in['w_kv_up'], 'L1_attn_w_q': _L1_attn_in['w_q'], 'L1_attn_w_out': _L1_attn_in['w_out'], 'L1_ffn_w_in': _L1_ffn_in['w_in'], 'L1_ffn_w_out': _L1_ffn_in['w_out'], 'L1_ffn_w1': _L1_ffn_in['w1'], 'L1_ffn_w2': _L1_ffn_in['w2'], 'L1_ffn_wg': _L1_ffn_in['wg'], 'L1_ffn_we': _L1_ffn_in['we'], 'L1_ffn_gb': _L1_ffn_in['gb'], 'L1_ffn_eb': _L1_ffn_in['eb']}
    _x0 = _d['L0_attn_x']
    _d['L0_attn_x'] = jax.random.normal(jax.random.fold_in(jax.random.key(seed), 1), (8, 256, 128), dtype=_x0.dtype)
    del _x0
    return _d

def reference(L0_attn_x, L0_attn_w_qkv, L0_attn_w_out, L0_ffn_w_gate_w, L0_ffn_w_gate_b, L0_ffn_W1, L0_ffn_b1, L0_ffn_W2, L0_ffn_b2, L1_attn_w_kv_down, L1_attn_w_kv_up, L1_attn_w_q, L1_attn_w_out, L1_ffn_w_in, L1_ffn_w_out, L1_ffn_w1, L1_ffn_w2, L1_ffn_wg, L1_ffn_we, L1_ffn_gb, L1_ffn_eb):

    def _L0_attn_ref(x, w_qkv, w_out):
        import jax, jax.numpy as jnp
        import numpy as np
        D_MODEL = 128
        N_HEADS = 16
        D_HEAD = D_MODEL // N_HEADS
        EPS = 1e-06

        def _phi(x):
            return jax.nn.elu(x) + 1.0
        B, L, D = x.shape
        H, dh = (N_HEADS, D_HEAD)
        qkv = jnp.einsum('bld,ed->ble', x, w_qkv)
        qkv = qkv.reshape(B, L, 3, H, dh).transpose(2, 0, 3, 1, 4)
        q, k, v = (_phi(qkv[0]), _phi(qkv[1]), qkv[2])
        qT = q.transpose(2, 0, 1, 3)
        kT = k.transpose(2, 0, 1, 3)
        vT = v.transpose(2, 0, 1, 3)
        S0 = jnp.zeros((B, H, dh, dh), dtype=x.dtype)
        z0 = jnp.zeros((B, H, dh), dtype=x.dtype)

        def step(carry, inp):
            S, z = carry
            q_t, k_t, v_t = inp
            S = S + k_t[..., :, None] * v_t[..., None, :]
            z = z + k_t
            num = jnp.einsum('bhde,bhd->bhe', S, q_t)
            den = jnp.maximum(jnp.sum(z * q_t, axis=-1, keepdims=True), EPS)
            return ((S, z), num / den)
        _, out = jax.lax.scan(step, (S0, z0), (qT, kT, vT))
        out = out.transpose(1, 0, 2, 3).reshape(B, L, D)
        return jnp.einsum('bld,ed->ble', out, w_out)

    def _L0_ffn_ref(x, w_gate_w, w_gate_b, W1, b1, W2, b2):
        import jax, jax.numpy as jnp
        import numpy as np
        TOPK = 2
        CAPACITY_FACTOR = 1.0
        EPS = 1e-06
        B, S, D = (4, 512, 128)
        E = 8
        SUB_H = 256 // E
        Bx, Sx, Dx = x.shape
        Ex = w_gate_b.shape[0]
        K = Sx // 2
        capacity = int(CAPACITY_FACTOR * Bx)
        gate_scores = jax.nn.softmax(x @ w_gate_w + w_gate_b, axis=-1)
        _, top_idx = jax.lax.top_k(gate_scores, TOPK)
        mask = jax.nn.one_hot(top_idx, Ex, dtype=gate_scores.dtype).sum(axis=-2)
        masked = gate_scores * mask
        denom = masked.sum(axis=0, keepdims=True) + EPS
        route = masked / denom * capacity
        route_eb = jnp.transpose(route, (2, 0, 1))
        _, seq_ids = jax.lax.top_k(route_eb, K)
        seq_ids = jnp.sort(seq_ids, axis=-1)
        xg = jax.vmap(lambda idx: jnp.take_along_axis(x, idx[..., None], axis=1))(seq_ids)
        h = jnp.einsum('ebkd,edh->ebkh', xg, W1) + b1[:, None, None, :]
        h = jax.nn.gelu(h, approximate=False)
        o = jnp.einsum('ebkh,ehd->ebkd', h, W2) + b2[:, None, None, :]
        flat_ids = (jnp.arange(Bx)[None, :, None] * Sx + seq_ids).reshape(-1)
        outs = jnp.zeros((Bx * Sx, Dx), x.dtype).at[flat_ids].add(o.reshape(-1, Dx))
        return outs.reshape(Bx, Sx, Dx)

    def _L1_attn_ref(x, w_kv_down, w_kv_up, w_q, w_out):
        import jax, jax.numpy as jnp
        import numpy as np
        B, T, C = (64, 32, 128)
        N_HEAD, HEAD_SIZE, KV_RANK = (16, 64, 128)
        BLOCK_SIZE = 32
        Bx, Tx, Cx = x.shape
        HD = N_HEAD * HEAD_SIZE
        latent_kv = x @ w_kv_down
        kv = latent_kv @ w_kv_up
        k, v = (kv[..., :HD], kv[..., HD:])
        k = k.reshape(Bx, Tx, N_HEAD, HEAD_SIZE)
        v = v.reshape(Bx, Tx, N_HEAD, HEAD_SIZE)
        q = (x @ w_q).reshape(Bx, Tx, N_HEAD, HEAD_SIZE)
        scale = HEAD_SIZE ** (-0.5)
        att = jnp.einsum('bqhd,bkhd->bhqk', q, k) * scale
        causal = jnp.tril(jnp.ones((Tx, Tx), dtype=bool))
        att = jnp.where(causal, att, -jnp.inf)
        att = jax.nn.softmax(att, axis=-1)
        y = jnp.einsum('bhqk,bkhd->bqhd', att, v)
        y = y.reshape(Bx, Tx, HD)
        return y @ w_out

    def _L1_ffn_ref(x, w_in, w_out, w1, w2, wg, we, gb, eb):
        import jax, jax.numpy as jnp
        import numpy as np
        MODEL_DIM = 128
        HIDDEN = 256
        NUM_GROUPS = 2
        EXPERTS_PER_GP = 4
        NUM_EXPERTS = NUM_GROUPS * EXPERTS_PER_GP
        TOP_K = 2
        B, T = (2, 256)

        def _swiglu(x):
            a, b = jnp.split(x, 2, axis=-1)
            return jax.nn.silu(a) * b
        Bs, Ts, C = x.shape
        S = Bs * Ts
        flat = x.reshape(S, C)
        shared = _swiglu(flat @ w_in.T) @ w_out.T
        g_probs = jax.nn.softmax(flat @ wg.T + gb, axis=-1)
        g_idx = jnp.argmax(g_probs, axis=-1)
        e_logits = flat @ we.T + eb
        egid = jnp.arange(NUM_EXPERTS) // EXPERTS_PER_GP
        masked = jnp.where(g_idx[:, None] == egid[None, :], e_logits, -jnp.inf)
        e_probs = jax.nn.softmax(masked, axis=-1)
        g_prob = jnp.take_along_axis(g_probs, g_idx[:, None], axis=1)
        p_expert = e_probs * g_prob
        topv, topi = jax.lax.top_k(p_expert, TOP_K)
        w_se = jnp.zeros((S, NUM_EXPERTS), x.dtype).at[jnp.arange(S)[:, None], topi].add(topv)
        h = _swiglu(flat @ w1.T)
        routed = jnp.zeros_like(shared)
        for e in range(NUM_EXPERTS):
            routed = routed + h * w_se[:, e:e + 1] @ w2[e].T
        return (shared + routed).reshape(Bs, Ts, C)
    x = L0_attn_x
    x = x + _L0_attn_ref(_layernorm(x, axis=-1), L0_attn_w_qkv, L0_attn_w_out)
    x = x + _L0_ffn_ref(_layernorm(x, axis=-1), L0_ffn_w_gate_w, L0_ffn_w_gate_b, L0_ffn_W1, L0_ffn_b1, L0_ffn_W2, L0_ffn_b2)
    x = x + _L1_attn_ref(_layernorm(x, axis=-1), L1_attn_w_kv_down, L1_attn_w_kv_up, L1_attn_w_q, L1_attn_w_out)
    x = x + _L1_ffn_ref(_layernorm(x, axis=-1), L1_ffn_w_in, L1_ffn_w_out, L1_ffn_w1, L1_ffn_w2, L1_ffn_wg, L1_ffn_we, L1_ffn_gb, L1_ffn_eb)
    return x

_drawn_inputs = setup_inputs


def setup_inputs(seed=0):
    import zlib

    import numpy as np

    out = dict(_drawn_inputs(seed))
    spreads = {'L0_ffn_w_gate_b': (0.0, 0.1),
     'L0_ffn_b1': (0.0, 0.683),
     'L0_ffn_b2': (0.0, 0.1),
     'L1_ffn_gb': (0.0, 0.8),
     'L1_ffn_eb': (0.0, 0.8)}
    factors = {'L1_attn_w_q': 8.0,
     'L1_ffn_w_in': 6.568,
     'L1_ffn_w_out': 6.278,
     'L1_ffn_w1': 8.0,
     'L1_ffn_w2': 8.0,
     'L1_ffn_wg': 8.0,
     'L1_ffn_we': 8.0}
    for name, (base, spread) in spreads.items():
        noise = np.random.default_rng([zlib.crc32(name.encode()), seed]).standard_normal(out[name].shape)
        drawn = base * np.exp(spread * noise) if base else spread * noise
        out[name] = jnp.asarray(drawn.astype(out[name].dtype))
    for name, factor in factors.items():
        out[name] = (out[name] * factor).astype(out[name].dtype)
    return out
```

```python
from contextlib import ExitStack

import concourse.bass as bass
from concourse import mybir

F32 = mybir.dt.float32
F32R = mybir.dt.float32r
BF16 = mybir.dt.bfloat16
ALU = mybir.AluOpType
ACT = mybir.ActivationFunctionType
AX_X = mybir.AxisListType.X

B, S, D = 8, 256, 128
C = S // 128
NT = B * C
LH, LD = 16, 8
E = 8
SUB = 32
K_TOP = S // 2
NH, HD = 16, 64
NP = NH // 2
HID = 256
LN_EPS = 1e-5
EPS = 1e-6
LAG = 6


def build(nc, x_in, wqkv0, wout0, wgate0, bgate0, w1_0, b1_0, w2_0, b2_0, wdown, wkup, wvup, wq1, wout1,
          win1, w1_1, wff1, wexp1, wgate1, bgate1, c_ident, c_identb, c_causal, c_maskneg, c_mask4,
          c_block, c_expand, c_sel2, c_desc, out):
    with ExitStack() as ctx:
        def sb(name, shape, dt=F32):
            return ctx.enter_context(nc.sbuf_tensor(name, shape, dt))

        def sem(name):
            return ctx.enter_context(nc.semaphore(name))

        X = sb("X", [128, NT, D])
        wqkv = sb("wqkv", [128, 3 * D])
        wo0 = sb("wo0", [128, D])
        wg0 = sb("wg0", [128, E])
        bg0 = sb("bg0", [128, E])
        w1a = sb("w1a", [128, 2, 128])
        b1a = sb("b1a", [128, 2])
        w2a = sb("w2a", [128, 2, D])
        b2a = sb("b2a", [E, D])
        wstage = sb("wstage", [128, 2, 1024])
        wd_hi, wd_lo = sb("wd_hi", [128, 128], F32R), sb("wd_lo", [128, 128], F32R)
        wk_hi, wk_lo = sb("wk_hi", [128, 1024], F32R), sb("wk_lo", [128, 1024], F32R)
        wv_hi, wv_lo = sb("wv_hi", [128, 1024], F32R), sb("wv_lo", [128, 1024], F32R)
        wq_hi, wq_lo = sb("wq_hi", [128, 1024], F32R), sb("wq_lo", [128, 1024], F32R)
        wo_hi, wo_lo = sb("wo_hi", [128, 1024], F32R), sb("wo_lo", [128, 1024], F32R)
        wh_hi, wh_lo = sb("wh_hi", [128, 1024], F32R), sb("wh_lo", [128, 1024], F32R)
        we_hi, we_lo = sb("we_hi", [128, 2048], F32R), sb("we_lo", [128, 2048], F32R)
        wf_hi, wf_lo = sb("wf_hi", [128, 256], F32R), sb("wf_lo", [128, 256], F32R)
        wg1 = sb("wg1", [128, 10])
        bg1 = sb("bg1", [128, 10])
        ident = sb("ident", [128, 128])
        identb = sb("identb", [128, 128], BF16)
        causal = sb("causal", [128, 128])
        maskneg = sb("maskneg", [128, 128], BF16)
        mask4 = sb("mask4", [128, 4])
        block9 = sb("block9", [128, LH, LD + 1])
        expand = sb("expand", [E, 2, 128], BF16)
        sel2 = sb("sel2", [2, 2, 128])
        sel2r = sb("sel2r", [2, 2, 128], F32R)
        desc = sb("desc", [128, E])

        stats = sb("stats", [128, C, 6])
        mv = sb("mv", [128, C, 2])
        veps = sb("veps", [128, C])
        rstd = sb("rstd", [128, C])
        neghalf = sb("neghalf", [128, C])
        xn = sb("xn", [128, C, D])
        xT = sb("xT", [128, S])
        qkm = sb("qkm", [128, 2, S])
        qk = sb("qk", [128, 2, S])
        v9 = sb("v9", [128, C, LH, LD + 1])
        mid = sb("mid", [128, 2 * 2 * 512])
        qblk = mid[:, 0:4 * S].rearrange("p (j t) -> p j t", j=4)
        k0 = sb("k0", [128, 128])
        state = sb("state", [128, LH, LD + 1])
        early = sb("early", [128, 2 * C * NH * (HD + 1)])
        sm = early[:, B * S:B * S + LH * 128].rearrange("p (h t) -> p h t", h=LH)
        den0 = sb("den0", [128, LH, 1])
        rden0 = sb("rden0", [128, LH, 1])
        o0 = sb("o0", [128, C, D])
        oT = sb("oT", [128, S])
        x1T = early[:, 0:B * S].rearrange("p (b t) -> p b t", b=B)
        gate = sb("gate", [128, NT, E])
        ga, gb_, gc, gd = (sb(f"g{i}", [128, NT, E]) for i in range(4))
        gm = sb("gm", [128, NT, 1])
        gs = sb("gs", [128, NT, 1])
        dsum = sb("dsum", [128, C * E])
        route = sb("route", [128, C, B, E])
        rank = [sb(f"rank{i}", [B * E, S]) for i in range(2)]
        top8 = sb("top8", [B * E, 8])
        selb = sb("selb", [B * E, S], BF16)
        sele = sb("sele", [E, B, S], BF16)
        selc = sb("selc", [E, S])
        hs = mid[:, 4 * S:6 * S].rearrange("p (n t) -> p n t", n=2)
        hm = mid[:, 6 * S:8 * S].rearrange("p (n t) -> p n t", n=2)
        x2_hi, x2_lo = sb("x2_hi", [128, B, S], F32R), sb("x2_lo", [128, B, S], F32R)
        lat_hi, lat_lo = sb("lat_hi", [128, B, S], F32R), sb("lat_lo", [128, B, S], F32R)
        ls_hi, ls_lo = sb("ls_hi", [128, S], F32R), sb("ls_lo", [128, S], F32R)
        q_hi, q_lo = sb("q_hi", [128, NP, S], F32R), sb("q_lo", [128, NP, S], F32R)
        k_hi, k_lo = sb("k_hi", [128, NP, S], F32R), sb("k_lo", [128, NP, S], F32R)
        v65 = early[:, :].rearrange("p (n c h d) -> p n c h d", n=2, c=C, h=NH)
        negm = sb("negm", [128, 2, C, 2])
        negc = sb("negc", [2, 2, S], F32R)
        pT = mid[:, :].rearrange("p (n h t) -> p n h t", n=2, h=2)
        rden = sb("rden", [128, 2, C, 2, 1])
        yn = sb("yn", [128, 2, C, 2, HD])
        y_hi, y_lo = sb("y_hi", [128, S], F32R), sb("y_lo", [128, S], F32R)
        x3_hi, x3_lo = x2_hi, x2_lo
        th = early[:, 2080:3104].rearrange("p (n t) -> p n t", n=4)
        hg = early[:, 3104:4128].rearrange("p (n t) -> p n t", n=4)
        hT_hi, hT_lo = k_hi[:, 0:4, :], k_lo[:, 0:4, :]
        wide = v65[:, 0, :, :, :].rearrange("p a b c -> p (a b c)")
        prod = wide[:, 0:1024].rearrange("p (e d) -> p e d", e=E)
        acc4 = wide[:, 1024:1536].rearrange("p (e d) -> p e d", e=4)
        acc2 = wide[:, 1536:1792].rearrange("p (e d) -> p e d", e=2)
        PS = ctx.enter_context(nc.psum_tensor("PS", [128, 8, 512], F32))

        block = ctx.enter_context(nc.Block())

        names = """ld_x ld_c1 ld_w0 ld_w1 ld_st0 ld_st1 st_free ones w_split w_hi out_done
            s1_va s1_rs s3_va s3_rs s5_va s5_rs nh s1_xn s1_xT s1_xTs s1_qk s1_v s1_min s1_exp s1_phi s1_vs s1_blk s1_kT s1_k0 s1_st s1_stm
            s1_sc s1_sm s1_pv s1_o s1_oT s1_oTs s1_pr s1_xn1 s1_x1T s1_x1s s1_lg s1_lgs s1_vec
            s2_vec s2_d s2_e s2_rt s2_rT s2_rTs s2_sel s2_dma
            s3_selc s3_h s3_g s3_m s3_hm s3_o s3_xn s3_xT s3_hi s3_lo s3_lat s3_lhi s3_llo s3_vec
            a_proj a_qhi a_khi a_qlo a_klo a_s a_max a_c a_cs a_st a_exp a_msk a_y a_yn a_yT a_yhi a_ylo
            a_o a_x a_ls a_v a_vs a_rec
            s5_xn s5_xT s5_xTs s5_hi s5_lo s5_lg s5_lgs s5_vec s5g_vec s5g_d s5g_e s5g_e2
            f_ha f_hb f_th f_g f_ghi f_glo f_sh f_ex f_pr f_ad f_y f_vec f_fr""".split()
        s = {n: sem(n) for n in names}

        apart_regs = []

        def wait_apart(eng, name, value):
            if not isinstance(value, int):
                own = eng.alloc_register(f"apart{len(apart_regs)}")
                apart_regs.append(own)
                eng.reg_mov(own, value)
                value = own
            eng.wait_ge(s["ld_x"], 16)
            eng.wait_ge(s[name], value)

        def chain(eng, name, base=0):
            count = [0]

            def link(ins, start=None, apart=False):
                count[0] += 1
                ins.then_inc(s[name], 1)
                value = (0 if start is None else start) + base + count[0]
                if apart:
                    wait_apart(eng, name, value)
                else:
                    eng.wait_ge(s[name], value)
            return link, count

        def mm3(pe, dst, w, m, start=True, stop=True, skip=False):
            pe.matmul(dst, w[0], m[1], start=start, stop=False, skip_group_check=skip)
            pe.matmul(dst, w[1], m[0], start=False, stop=False, skip_group_check=skip)
            return pe.matmul(dst, w[0], m[0], start=False, stop=stop, skip_group_check=skip)

        def c1024(w):
            return w
        cut = [(wdown, wd_hi[:], wd_lo[:], 128), (wkup, wk_hi[:], wk_lo[:], 1024),
               (wvup, wv_hi[:], wv_lo[:], 1024), (wq1, wq_hi[:], wq_lo[:], 1024),
               (wout1, wo_hi[:], wo_lo[:], 1024), (win1, wh_hi[:, 0:512], wh_lo[:, 0:512], 512),
               (w1_1, wh_hi[:, 512:1024], wh_lo[:, 512:1024], 512),
               (wexp1[:, 0:1024], we_hi[:, 0:1024], we_lo[:, 0:1024], 1024),
               (wexp1[:, 1024:2048], we_hi[:, 1024:2048], we_lo[:, 1024:2048], 1024),
               (wff1, wf_hi[:], wf_lo[:], 256)]

        @block.sync
        def _(sp):
            sp.dma_start(X[:], x_in).then_inc(s["ld_x"], 16)
            for dst, src in ((ident, c_ident), (wqkv, wqkv0), (mask4, c_mask4), (causal, c_causal),
                             (block9, c_block), (wo0, wout0), (wg0, wgate0)):
                sp.dma_start(dst[:], src).then_inc(s["ld_w0"], 16)
            for dst, src in ((bg0, bgate0), (w1a, w1_0), (b1a, b1_0), (w2a, w2_0), (b2a, b2_0),
                             (expand, c_expand), (identb, c_identb), (maskneg, c_maskneg),
                             (sel2, c_sel2), (desc, c_desc), (wg1, wgate1), (bg1, bgate1)):
                sp.dma_start(dst[:], src).then_inc(s["ld_w1"], 16)
            for n, (src, _, _, cols) in enumerate(cut):
                if n >= 2:
                    sp.wait_ge(s["w_split"], n - 1)
                sp.dma_start(wstage[:, n % 2, 0:cols], src).then_inc(s[f"ld_st{n % 2}"], 16)
            sp.wait_ge(s["s2_sel"], 1)
            for b in range(B):
                sp.dma_start(sele[:, b, :], selb[E * b:E * b + E, :]).then_inc(s["s2_dma"], 16)
            with sp.Fori(0, B) as b:
                sp.wait_ge(s["f_y"], b + 1)
                sp.dma_start(out[:, b, :, :], X[:, :, :].rearrange("p (b c) d -> p b c d", c=C)[:, b, :, :]).then_inc(s["out_done"], 16)
            sp.wait_ge(s["out_done"], 16 * B)

        Xb = X[:, :, :].rearrange("p (b c) d -> p b c d", c=C)
        gateb = gate[:, :, :].rearrange("p (b c) e -> p b c e", c=C)

        @block.gpsimd
        def _(pool):
            pool.memset(v9[:, :, :, LD:LD + 1], 1.0).then_inc(s["ones"], 1)
            pool.memset(neghalf[:], -0.5).then_inc(s["nh"], 1)
            pool.wait_ge(s["nh"], 1)

            def root(stage, n):
                pool.wait_ge(s[stage + "_va"], n)
                pool.tensor_tensor(rstd[:], veps[:], neghalf[:], ALU.pow).then_inc(s[stage + "_rs"], 1)

            def split(n):
                _, hi, lo, cols = cut[n]
                pool.wait_ge(s[f"ld_st{n % 2}"], 16 * (n // 2 + 1))
                pool.tensor_copy(hi, wstage[:, n % 2, 0:cols]).then_inc(s["w_hi"], 1)
                pool.wait_ge(s["w_hi"], n + 1)
                pool.tensor_tensor(lo, wstage[:, n % 2, 0:cols], hi.bitcast(F32), ALU.subtract).then_inc(s["w_split"], 1)

            pool.wait_ge(s["ld_w0"], 16 * 7)
            with pool.Fori(0, B) as b:
                root("s1", 2 * b + 1)
                pool.wait_ge(s["s1_phi"], b + 1)
                pool.tensor_tensor(qblk, qk[:, 0:1, :].broadcast_to([128, 4, S]),
                                   mask4[:, :, None].broadcast_to([128, 4, S]), ALU.mult).then_inc(s["s1_blk"], 1)
                root("s1", 2 * b + 2)
            for n in range(len(cut)):
                split(n)
            pool.wait_ge(s["ld_w1"], 16 * 12)
            pool.tensor_copy(sel2r[:], sel2[:]).then_inc(s["w_hi"], 1)
            pool.wait_ge(s["s2_dma"], 16 * B)
            with pool.Fori(0, B) as b:
                pool.tensor_copy(selc[:], sele[:, b, :]).then_inc(s["s3_selc"], 1)
                pool.wait_ge(s["s3_o"], b + 1)
                root("s3", b + 1)

            pool.wait_ge(s["s3_h"], B)
            pool.memset(v65[:, :, :, :, HD:HD + 1], 1.0).then_inc(s["ones"], 1)

            def masks(k, p):
                wait_apart(pool, "a_exp", k + 1)
                blk = pT[:, p % 2, :, :].rearrange("s h (b t) -> s (h b) t", t=256)[:, :, 0:128]
                pool.affine_select(out=blk, in_=blk, compare_op=ALU.is_ge, fill=0.0, base=0,
                                   pattern=[[0, 4], [1, 128]], channel_multiplier=-1).then_inc(s["a_msk"], 1)

            def latents(b):
                pool.tensor_copy(ls_hi[:], lat_hi[:, b, :]).then_inc(s["a_ls"], 1)
                pool.tensor_copy(ls_lo[:], lat_lo[:, b, :]).then_inc(s["a_ls"], 1)

            def body(b, first, last):
                if not last:
                    if first:
                        pool.wait_ge(s["s3_llo"], B)
                    else:
                        pool.wait_ge(s["a_v"], 4 * b)
                    latents(b)
                for p in range(NP if not last else LAG):
                    if first and p < 3:
                        continue
                    if last and p >= 3:
                        continue
                    kk = p - 3
                    masks(NP * b + kk, kk)
            body(0, True, False)
            with pool.Fori(1, B) as b:
                body(b, False, False)
            body(B, False, True)

            with pool.Fori(0, B) as b:
                root("s5", b + 1)
            with pool.Fori(0, NT) as n:
                pool.wait_ge(s["f_pr"], n + 1)
                pool.tensor_tensor(acc4, prod[:, 0:4, :], prod[:, 4:8, :], ALU.add).then_inc(s["f_ad"], 1)
                pool.wait_ge(s["f_ad"], 2 * n + 1)
                pool.tensor_tensor(acc2, acc4[:, 0:2, :], acc4[:, 2:4, :], ALU.add).then_inc(s["f_ad"], 1)

        @block.scalar
        def _(act):
            act.wait_ge(s["ones"], 1)
            with act.Fori(0, B) as b:
                act.wait_ge(s["s1_xT"], b + 1)
                act.copy(xT[:], PS[:, 0, 0:S]).then_inc(s["s1_xTs"], 1)
                act.wait_ge(s["s1_v"], b + 1)
                act.copy(v9[:, :, :, 0:LD], PS[:, 2, 0:S].rearrange("p (c h d) -> p c h d", c=C, h=LH)).then_inc(s["s1_vs"], 1)
                act.wait_ge(s["s1_min"], b + 1)
                act.activation(qkm[:], qkm[:], ACT.Exp).then_inc(s["s1_exp"], 1)
                act.wait_ge(s["s1_kT"], b + 1)
                act.copy(k0[:], PS[:, 2, 0:128]).then_inc(s["s1_k0"], 1)
                act.wait_ge(s["s1_oT"], b + 1)
                act.copy(oT[:], PS[:, 0, 0:S]).then_inc(s["s1_oTs"], 1)
                act.wait_ge(s["s1_x1T"], b + 1)
                act.copy(xT[:], PS[:, 0, 0:S]).then_inc(s["s1_x1s"], 1)
                act.copy(x1T[:, b, :], PS[:, 0, 0:S]).then_inc(s["s1_x1s"], 1)
            act.wait_ge(s["s2_d"], 1)
            act.activation(gb_[:], ga[:], ACT.Exp).then_inc(s["s2_e"], 1)
            act.wait_ge(s["ld_w1"], 16 * 12)
            with act.Fori(0, B) as b:
                act.wait_ge(s["s3_h"], b + 1)
                for half in range(2):
                    act.activation(hs[:, half, :], PS[:, 0, S * half:S * half + S], ACT.Gelu,
                                   bias=b1a[:, half:half + 1]).then_inc(s["s3_g"], 1)
                act.wait_ge(s["s3_xT"], b + 1)
                act.copy(x2_hi[:, b, :], PS[:, 3, 0:S]).then_inc(s["s3_hi"], 1)
                act.wait_ge(s["s3_lat"], b + 1)
                act.copy(lat_hi[:, b, :], PS[:, 4, 0:S]).then_inc(s["s3_lhi"], 1)

            act.wait_ge(s["ones"], 2)

            def proj_hi(k, p):
                act.wait_ge(s["a_proj"], k + 1)
                act.activation(q_hi[:, p, :], PS[:, 0, 0:S], ACT.Copy, scale=float(HD) ** -0.5).then_inc(s["a_qhi"], 1)
                act.copy(k_hi[:, p, :], PS[:, 0, S:2 * S]).then_inc(s["a_khi"], 1)

            def exps(k, p):
                act.wait_ge(s["a_st"], k + 1)
                if not (isinstance(k, int) and k < 2):
                    act.wait_ge(s["a_y"], k - 1)
                act.activation(pT[:, p % 2, :, 0:384], PS[:, 3:5, 0:384], ACT.Exp).then_inc(s["a_exp"], 1)

            def yt_hi(k, p):
                act.wait_ge(s["a_yT"], k + 1)
                if not (isinstance(k, int) and k < 1):
                    act.wait_ge(s["a_o"], k)
                act.copy(y_hi[:], PS[:, 6, 0:S]).then_inc(s["a_yhi"], 1)

            def values(b, g):
                act.wait_ge(s["a_v"], 4 * b + g + 1)
                h0 = 8 * (g % 2)
                act.copy(v65[:, b % 2, g // 2, h0:h0 + 8, 0:HD],
                         PS[:, 0, :].rearrange("p (h d) -> p h d", h=8)).then_inc(s["a_vs"], 1)

            def cast_c(k, p):
                act.wait_ge(s["a_c"], k + 1)
                act.copy(negc[:, p % 2, :].rearrange("h (c t) -> h c t", c=C), PS[0:2, 3:5, 384:512]).then_inc(s["a_cs"], 1)

            def body(b, first, last):
                if not last:
                    for g in range(4):
                        values(b, g)
                for p in range(NP if not last else LAG):
                    if not last:
                        proj_hi(NP * b + p, p)
                    for lag, stage in ((2, cast_c), (3, exps), (5, yt_hi)):
                        kk = p - lag
                        if (first and kk < 0) or (last and kk >= 0):
                            continue
                        stage(NP * b + kk, kk % NP)
            body(0, True, False)
            with act.Fori(1, B) as b:
                body(b, False, False)
            body(B, False, True)

            with act.Fori(0, B) as b:
                act.wait_ge(s["s5_xT"], b + 1)
                act.copy(xT[:], PS[:, 0, 0:S]).then_inc(s["s5_xTs"], 1)
                act.copy(x3_hi[:, b, :], PS[:, 0, 0:S]).then_inc(s["s5_hi"], 1)
            act.wait_ge(s["s5g_d"], 1)
            act.activation(gb_[:], ga[:], ACT.Exp).then_inc(s["s5g_e"], 1)
            act.wait_ge(s["s5g_d"], 2)
            act.activation(gd[:], ga[:], ACT.Exp).then_inc(s["s5g_e2"], 1)
            with act.Fori(0, B) as b:
                act.wait_ge(s["f_ha"], b + 1)
                act.activation(th, PS[:, 0:2, :].rearrange("p n (m t) -> p (n m) t", m=2), ACT.Tanh, scale=0.5).then_inc(s["f_th"], 1)
                act.wait_ge(s["f_g"], b + 1)
                act.copy(hT_hi, hg).then_inc(s["f_ghi"], 1)

        @block.vector
        def _(v):
            v.wait_ge(s["ld_x"], 16)
            v.wait_ge(s["ld_w0"], 16 * 7)

            def layernorm(b, link, start, stage, n):
                for c in range(C):
                    last = v.bn_stats(stats[:, c, :], Xb[:, b, c, :])
                link(last, start, apart=True)
                for c in range(C):
                    last = v.bn_aggr(mv[:, c, :], stats[:, c, :])
                link(last, start)
                v.tensor_scalar(veps[:], mv[:, :, 1], LN_EPS, None, ALU.add).then_inc(s[stage + "_va"], 1)
                v.wait_ge(s[stage + "_rs"], n)
                for c in range(C):
                    last = v.tensor_scalar(xn[:, c, :], Xb[:, b, c, :], mv[:, c, 0:1], rstd[:, c:c + 1],
                                           ALU.subtract, ALU.mult)
                return last

            V1 = 9
            with v.Fori(0, B) as b:
                link, count = chain(v, "s1_vec")
                st = b * V1
                layernorm(b, link, st, "s1", 2 * b + 1).then_inc(s["s1_xn"], 1)
                v.wait_ge(s["s1_qk"], b + 1)
                v.tensor_scalar(qkm[:], PS[:, 1, :].rearrange("p (n t) -> p n t", n=2), 0.0, None, ALU.min).then_inc(s["s1_min"], 1)
                v.wait_ge(s["s1_exp"], b + 1)
                v.scalar_tensor_tensor(out=qk[:], in0=PS[:, 1, :].rearrange("p (n t) -> p n t", n=2), scalar=0.0,
                                       in1=qkm[:], op0=ALU.max, op1=ALU.add).then_inc(s["s1_phi"], 1)
                v.wait_ge(s["s1_st"], b + 1)
                v.tensor_tensor(state[:], PS[:, 2, 128:272].rearrange("p (h d) -> p h d", h=LH), block9[:], ALU.mult).then_inc(s["s1_stm"], 1)
                for c in range(C):
                    v.wait_ge(s["s1_sc"], b * C + c + 1)
                    if c:
                        v.wait_ge(s["s1_pv"], b * C + c)
                    v.tensor_tensor(sm, PS[:, 3:7, :].rearrange("p g (j t) -> p (g j) t", j=4),
                                    causal[:, None, :].broadcast_to([128, LH, 128]), ALU.mult).then_inc(s["s1_sm"], 1)
                    v.wait_ge(s["s1_pv"], b * C + c + 1)
                    pv = PS[:, 7, 0:144].rearrange("p (h d) -> p h d", h=LH)
                    link(v.tensor_scalar(den0[:], pv[:, :, LD:LD + 1], EPS, None, ALU.max), st)
                    link(v.reciprocal(rden0[:], den0[:]), st)
                    v.tensor_tensor(o0[:, c, :].rearrange("p (h d) -> p h d", h=LH), pv[:, :, 0:LD],
                                    rden0[:].broadcast_to([128, LH, LD]), ALU.mult).then_inc(s["s1_o"], 1)
                v.wait_ge(s["s1_pr"], b + 1)
                link(v.tensor_tensor(Xb[:, b, :, :], Xb[:, b, :, :], PS[:, 1, 0:S].rearrange("p (c d) -> p c d", c=C), ALU.add), st, apart=True)
                layernorm(b, link, st, "s1", 2 * b + 2).then_inc(s["s1_xn1"], 1)
                wait_apart(v, "s1_lg", b + 1)
                v.tensor_copy(gateb[:, b, :, :], PS[:, 7, 256:256 + C * E].rearrange("p (c e) -> p c e", c=C)).then_inc(s["s1_lgs"], 1)
                N1 = count[0]
            assert N1 == V1, N1

            link, _ = chain(v, "s2_vec")
            v.wait_ge(s["s1_lgs"], B)
            v.wait_ge(s["ld_w1"], 16 * 12)
            wideE = [128, NT, E]

            def over(t):
                return t[:].broadcast_to(wideE)
            descb = desc[:, None, :].broadcast_to(wideE)

            def first_max(link, vals, onehot, scratch):
                link(v.tensor_reduce(gm[:], vals, AX_X, ALU.max))
                link(v.tensor_tensor(scratch, vals, over(gm), ALU.is_equal))
                link(v.tensor_tensor(scratch, scratch, descb, ALU.mult))
                link(v.tensor_reduce(gs[:], scratch, AX_X, ALU.max))
                link(v.tensor_tensor(onehot, scratch, over(gs), ALU.is_equal))

            link(v.tensor_tensor(gate[:], gate[:], bg0[:, None, :].broadcast_to(wideE), ALU.add))
            link(v.tensor_reduce(gm[:], gate[:], AX_X, ALU.max))
            v.tensor_tensor(ga[:], gate[:], over(gm), ALU.subtract).then_inc(s["s2_d"], 1)
            v.wait_ge(s["s2_e"], 1)
            link(v.tensor_reduce(gs[:], gb_[:], AX_X, ALU.add))
            link(v.reciprocal(gs[:], gs[:]))
            link(v.tensor_tensor(gate[:], gb_[:], over(gs), ALU.mult))
            first_max(link, gate[:], gb_[:], ga[:])
            link(v.scalar_tensor_tensor(out=gc[:], in0=gb_[:], scalar=-2.0, in1=gate[:], op0=ALU.mult, op1=ALU.add))
            first_max(link, gc[:], gd[:], ga[:])
            link(v.tensor_tensor(gb_[:], gb_[:], gd[:], ALU.add))
            link(v.tensor_tensor(gate[:], gate[:], gb_[:], ALU.mult))
            link(v.tensor_reduce(dsum[:], gate[:].rearrange("p (b c) e -> p (c e) b", c=C), AX_X, ALU.add))
            link(v.tensor_scalar(dsum[:], dsum[:], EPS, None, ALU.add))
            link(v.reciprocal(dsum[:], dsum[:]))
            link(v.tensor_tensor(route[:], gate[:].rearrange("p (b c) e -> p c b e", c=C),
                                 dsum[:].rearrange("p (c e) -> p c e", c=C)[:, :, None, :].broadcast_to([128, C, B, E]), ALU.mult))
            v.tensor_scalar(route[:], route[:], float(B), None, ALU.mult).then_inc(s["s2_rt"], 1)
            v.wait_ge(s["s2_rT"], 1)
            v.wait_ge(s["s1_x1s"], 2 * B)
            link(v.tensor_copy(rank[0][:], PS[0:B * E, 0, 0:S]))
            for r in range(K_TOP // 8):
                link(v.max(top8[:], rank[r % 2][:]))
                link(v.match_replace(rank[(r + 1) % 2][:], top8[:], rank[r % 2][:], -1.0))
            v.tensor_scalar(selb[:], rank[(K_TOP // 8) % 2][:], 0.0, None, ALU.is_lt).then_inc(s["s2_sel"], 1)

            V3 = 3
            with v.Fori(0, B) as b:
                link, count = chain(v, "s3_vec")
                st = b * V3
                v.wait_ge(s["s3_g"], 2 * b + 2)
                v.wait_ge(s["s3_m"], b + 1)
                v.tensor_tensor(hm, PS[:, 1, :].rearrange("p (n t) -> p n t", n=2), hs, ALU.mult).then_inc(s["s3_hm"], 1)
                v.wait_ge(s["s3_o"], b + 1)
                link(v.tensor_tensor(Xb[:, b, :, :], Xb[:, b, :, :], PS[:, 2, 0:S].rearrange("p (c d) -> p c d", c=C), ALU.add), st, apart=True)
                layernorm(b, link, st, "s3", b + 1).then_inc(s["s3_xn"], 1)
                v.wait_ge(s["s3_hi"], b + 1)
                v.tensor_tensor(x2_lo[:, b, :], PS[:, 3, 0:S], x2_hi[:, b, :].bitcast(F32), ALU.subtract).then_inc(s["s3_lo"], 1)
                v.wait_ge(s["s3_lhi"], b + 1)
                v.tensor_tensor(lat_lo[:, b, :], PS[:, 4, 0:S], lat_hi[:, b, :].bitcast(F32), ALU.subtract).then_inc(s["s3_llo"], 1)
                assert count[0] == V3

            def proj_lo(k, p):
                v.wait_ge(s["a_khi"], k + 1)
                v.scalar_tensor_tensor(out=q_lo[:, p, :], in0=PS[:, 0, 0:S], scalar=float(HD) ** -0.5,
                                       in1=q_hi[:, p, :].bitcast(F32), op0=ALU.mult, op1=ALU.subtract).then_inc(s["a_qlo"], 1)
                v.tensor_tensor(k_lo[:, p, :], PS[:, 0, S:2 * S], k_hi[:, p, :].bitcast(F32), ALU.subtract).then_inc(s["a_klo"], 1)

            def row_max(k, p):
                v.wait_ge(s["a_s"], k + 1)
                if not (isinstance(k, int) and k < 2):
                    v.wait_ge(s["a_c"], k - 1)
                v.tensor_reduce(negm[:, p % 2, 0, :], PS[:, 1:3, 0:128], AX_X, ALU.max, negate=True).then_inc(s["a_max"], 1)
                v.tensor_reduce(negm[:, p % 2, 1, :], PS[:, 1:3, 128:384], AX_X, ALU.max, negate=True).then_inc(s["a_max"], 1)

            def normalise(k, p):
                v.wait_ge(s["a_y"], k + 1)
                if not (isinstance(k, int) and k < 2):
                    v.wait_ge(s["a_yT"], k - 1)
                y = PS[:, 5, 0:C * 2 * (HD + 1)].rearrange("p (c h d) -> p c h d", c=C, h=2)
                v.reciprocal(rden[:, p % 2], y[:, :, :, HD:HD + 1]).then_inc(s["a_rec"], 1)
                v.wait_ge(s["a_rec"], k + 1)
                v.tensor_tensor(yn[:, p % 2], y[:, :, :, 0:HD], rden[:, p % 2].broadcast_to([128, C, 2, HD]),
                                ALU.mult).then_inc(s["a_yn"], 1)

            def yt_lo(k, p):
                v.wait_ge(s["a_yhi"], k + 1)
                v.tensor_tensor(y_lo[:], PS[:, 6, 0:S], y_hi[:].bitcast(F32), ALU.subtract).then_inc(s["a_ylo"], 1)

            def residual(k, p, b):
                if p != NP - 1:
                    return
                v.wait_ge(s["a_o"], k + 1)
                v.tensor_tensor(Xb[:, b, :, :], Xb[:, b, :, :], PS[:, 7, 0:S].rearrange("p (c d) -> p c d", c=C), ALU.add).then_inc(s["a_x"], 1)

            def body(b, first, last):
                for p in range(NP if not last else LAG + 1):
                    if not last:
                        proj_lo(NP * b + p, p)
                    for lag, stage in ((1, row_max), (4, normalise), (5, yt_lo), (6, residual)):
                        kk = p - lag
                        if (first and kk < 0) or (last and kk >= 0):
                            continue
                        if lag == 6:
                            residual(NP * b + kk, kk % NP, b - 1 if kk < 0 else b)
                        else:
                            stage(NP * b + kk, kk % NP)
            body(0, True, False)
            with v.Fori(1, B) as b:
                body(b, False, False)
            body(B, False, True)
            v.wait_ge(s["a_x"], B)

            V5 = 2
            with v.Fori(0, B) as b:
                link, count = chain(v, "s5_vec")
                layernorm(b, link, b * V5, "s5", b + 1).then_inc(s["s5_xn"], 1)
                v.wait_ge(s["s5_hi"], b + 1)
                v.tensor_tensor(x3_lo[:, b, :], PS[:, 0, 0:S], x3_hi[:, b, :].bitcast(F32), ALU.subtract).then_inc(s["s5_lo"], 1)
                wait_apart(v, "s5_lg", b + 1)
                lg = PS[:, 1, 0:C * 10].rearrange("p (c e) -> p c e", c=C)
                v.tensor_copy(gateb[:, b, :, :], lg[:, :, 2:10]).then_inc(s["s5_lgs"], 1)
                v.tensor_copy(gc[:, :, :].rearrange("p (b c) e -> p b c e", c=C)[:, b, :, 0:2], lg[:, :, 0:2]).then_inc(s["s5_lgs"], 1)
                assert count[0] == V5
            v.wait_ge(s["s5_lgs"], 2 * B)
            link, _ = chain(v, "s5g_vec")
            link(v.tensor_tensor(gc[:, :, 0:2], gc[:, :, 0:2], bg1[:, None, 0:2].broadcast_to([128, NT, 2]), ALU.add))
            link(v.tensor_tensor(gate[:], gate[:], bg1[:, None, 2:10].broadcast_to(wideE), ALU.add))
            link(v.tensor_reduce(gm[:], gc[:, :, 0:2], AX_X, ALU.max))
            link(v.memset(ga[:], 0.0))
            v.tensor_tensor(ga[:, :, 0:2], gc[:, :, 0:2], gm[:].broadcast_to([128, NT, 2]), ALU.subtract).then_inc(s["s5g_d"], 1)
            v.wait_ge(s["s5g_e"], 1)
            g01 = gb_[:, :, 0:2]
            link(v.tensor_reduce(gs[:], g01, AX_X, ALU.add))
            link(v.reciprocal(gs[:], gs[:]))
            link(v.tensor_tensor(gc[:, :, 2:4], g01, gs[:].broadcast_to([128, NT, 2]), ALU.mult))
            link(v.tensor_reduce(gm[:], gc[:, :, 2:4], AX_X, ALU.max))
            link(v.tensor_tensor(gc[:, :, 4:5], gc[:, :, 2:3], gc[:, :, 3:4], ALU.is_ge))
            link(v.tensor_scalar(gc[:, :, 5:6], gc[:, :, 4:5], -1.0, 1.0, ALU.mult, ALU.add))
            ing = gd[:].rearrange("p n (g e) -> p n g e", g=2)
            link(v.tensor_copy(ing, gc[:, :, 4:6][:, :, :, None].broadcast_to([128, NT, 2, 4])))
            gview = gate[:].rearrange("p n (g e) -> p n g e", g=2)
            link(v.tensor_reduce(gc[:, :, 6:8], gview, AX_X, ALU.max))
            link(v.tensor_tensor(ga[:].rearrange("p n (g e) -> p n g e", g=2), gview,
                                 gc[:, :, 6:8][:, :, :, None].broadcast_to([128, NT, 2, 4]), ALU.subtract))
            link(v.tensor_copy(gb_[:], gd[:]))
            v.tensor_copy(gate[:, :, 0:1], ga[:, :, 0:1]).then_inc(s["s5g_d"], 1)
            v.wait_ge(s["s5g_e2"], 1)
            link(v.tensor_tensor(gd[:], gd[:], gb_[:], ALU.mult))
            link(v.tensor_reduce(gs[:], gd[:], AX_X, ALU.add))
            link(v.reciprocal(gs[:], gs[:]))
            link(v.tensor_tensor(gate[:], gd[:], over(gs), ALU.mult))
            link(v.tensor_tensor(gate[:], gate[:], over(gm), ALU.mult))
            first_max(link, gate[:], gb_[:], ga[:])
            link(v.scalar_tensor_tensor(out=gc[:], in0=gb_[:], scalar=-2.0, in1=gate[:], op0=ALU.mult, op1=ALU.add))
            first_max(link, gc[:], gd[:], ga[:])
            link(v.tensor_tensor(gb_[:], gb_[:], gd[:], ALU.add))
            link(v.tensor_tensor(gate[:], gate[:], gb_[:], ALU.mult))

            with v.Fori(0, B) as b:
                link, count = chain(v, "f_vec")
                v.wait_ge(s["f_th"], b + 1)
                a_ps = PS[:, 0:2, :].rearrange("p n (m t) -> p (n m) t", m=2)
                b_ps = PS[:, 2:4, :].rearrange("p n (m t) -> p (n m) t", m=2)
                link(v.scalar_tensor_tensor(out=th, in0=th, scalar=1.0, in1=a_ps, op0=ALU.add, op1=ALU.mult), b)
                v.wait_ge(s["f_hb"], b + 1)
                v.scalar_tensor_tensor(out=hg, in0=th, scalar=0.5, in1=b_ps, op0=ALU.mult, op1=ALU.mult).then_inc(s["f_g"], 1)
                v.wait_ge(s["f_ghi"], b + 1)
                v.tensor_tensor(hT_lo, hg, hT_hi.bitcast(F32), ALU.subtract).then_inc(s["f_glo"], 1)
                for c in range(C):
                    v.wait_ge(s["f_ex"], 2 * b + c + 1)
                    if c or not False:
                        v.wait_ge(s["f_ad"], 0 + 4 * b + 2 * c) if c else None
                    v.tensor_tensor(prod, PS[:, 4:6, :].rearrange("p n (m d) -> p (n m) d", m=4),
                                    gateb[:, b, c, :][:, :, None].broadcast_to([128, E, D]), ALU.mult).then_inc(s["f_pr"], 1)
                    v.wait_ge(s["f_ad"], 4 * b + 2 * c + 2)
                    last = v.tensor_tensor(Xb[:, b, c, :], Xb[:, b, c, :], acc2[:, 0, :], ALU.add)
                    last.then_inc(s["f_fr"], 1)
                    v.wait_ge(s["f_fr"], 6 * b + 3 * c + 1)
                    v.tensor_tensor(Xb[:, b, c, :], Xb[:, b, c, :], acc2[:, 1, :], ALU.add).then_inc(s["f_fr"], 1)
                    v.wait_ge(s["f_fr"], 6 * b + 3 * c + 2)
                    v.tensor_tensor(Xb[:, b, c, :], Xb[:, b, c, :], PS[:, 6, 128 * c:128 * c + 128], ALU.add).then_inc(s["f_fr"], 1)
                    v.wait_ge(s["f_fr"], 6 * b + 3 * c + 3)
                v.tensor_copy(rstd[:, 0:1], veps[:, 0:1]).then_inc(s["f_y"], 1)

        @block.tensor
        def _(pe):
            pe.wait_ge(s["ld_w0"], 16 * 7)

            def transposes(bank, src, sem_name):
                for c in range(C):
                    last = pe.transpose(PS[:, bank, 128 * c:128 * c + 128], src[:, c, :], ident[:])
                last.then_inc(s[sem_name], 1)

            with pe.Fori(0, B) as b:
                pe.wait_ge(s["s1_xn"], b + 1)
                transposes(0, xn, "s1_xT")
                pe.wait_ge(s["s1_xTs"], b + 1)
                for n in range(2):
                    last = pe.matmul(PS[:, 1, S * n:S * n + S], wqkv[:, D * n:D * n + D], xT[:], start=True, stop=True)
                last.then_inc(s["s1_qk"], 1)
                for c in range(C):
                    last = pe.matmul(PS[:, 2, 128 * c:128 * c + 128], xT[:, 128 * c:128 * c + 128], wqkv[:, 2 * D:3 * D],
                                     start=True, stop=True)
                last.then_inc(s["s1_v"], 1)
                pe.wait_ge(s["s1_phi"], b + 1)
                pe.wait_ge(s["s1_vs"], b + 1)
                pe.transpose(PS[:, 2, 0:128], qk[:, 1, 0:128], ident[:]).then_inc(s["s1_kT"], 1)
                pe.wait_ge(s["s1_k0"], b + 1)
                pe.matmul(PS[:, 2, 128:272], k0[:], v9[:, 0, :, :].rearrange("p h d -> p (h d)"), start=True, stop=True).then_inc(s["s1_st"], 1)
                pe.wait_ge(s["s1_blk"], b + 1)
                for c in range(C):
                    if c:
                        pe.wait_ge(s["s1_sm"], b * C + c)
                    for g in range(4):
                        last = pe.matmul(PS[:, 3 + g, :].rearrange("p (j t) -> p j t", j=4),
                                         qk[32 * g:32 * g + 32, 1, 128 * c:128 * c + 128],
                                         qblk[32 * g:32 * g + 32, :, 128 * c:128 * c + 128], start=True, stop=True)
                    last.then_inc(s["s1_sc"], 1)
                    pe.wait_ge(s["s1_sm"], b * C + c + 1)
                    if c:
                        pe.wait_ge(s["s1_o"], b * C + c)
                        pe.wait_ge(s["s1_stm"], b + 1)
                        pe.matmul(PS[:, 7, 0:144], qk[:, 0, 128:256], state[:].rearrange("p h d -> p (h d)"),
                                  start=True, stop=False, skip_group_check=True)
                    for h in range(LH):
                        last = pe.matmul(PS[:, 7, 9 * h:9 * h + 9], sm[:, h, :], v9[:, c, h, :], start=(c == 0), stop=True,
                                         skip_group_check=True)
                    last.then_inc(s["s1_pv"], 1)
                pe.wait_ge(s["s1_o"], C * b + C)
                transposes(0, o0, "s1_oT")
                pe.wait_ge(s["s1_oTs"], b + 1)
                for c in range(C):
                    last = pe.matmul(PS[:, 1, 128 * c:128 * c + 128], oT[:, 128 * c:128 * c + 128], wo0[:], start=True, stop=True)
                last.then_inc(s["s1_pr"], 1)
                pe.wait_ge(s["s1_xn1"], b + 1)
                transposes(0, xn, "s1_x1T")
                pe.wait_ge(s["s1_x1s"], 2 * b + 2)
                for c in range(C):
                    last = pe.matmul(PS[:, 7, 256 + E * c:256 + E * c + E], xT[:, 128 * c:128 * c + 128], wg0[:], start=True, stop=True)
                last.then_inc(s["s1_lg"], 1)

            pe.wait_ge(s["s2_rt"], 1)
            for c in range(C):
                last = pe.transpose(PS[0:B * E, 0, 128 * c:128 * c + 128], route[:, c, :, :].rearrange("p b e -> p (b e)"), ident[:])
            last.then_inc(s["s2_rT"], 1)

            pe.wait_ge(s["ld_w1"], 16 * 12)
            pe.wait_ge(s["w_split"], len(cut))
            pe.wait_ge(s["w_hi"], len(cut) + 1)
            pe.wait_ge(s["s2_dma"], 16 * B)
            with pe.Fori(0, B) as b:
                for half in range(2):
                    last = pe.matmul(PS[:, 0, S * half:S * half + S], w1a[:, half, :], x1T[:, b, :], start=True, stop=True)
                last.then_inc(s["s3_h"], 1)
                for half in range(2):
                    last = pe.matmul(PS[:, 1, S * half:S * half + S], expand[:, half, :], sele[:, b, :], start=True, stop=True)
                last.then_inc(s["s3_m"], 1)
                pe.wait_ge(s["s3_hm"], b + 1)
                pe.wait_ge(s["s3_selc"], b + 1)
                for c in range(C):
                    t = slice(128 * c, 128 * c + 128)
                    for half in range(2):
                        pe.matmul(PS[:, 2, t], hm[:, half, t], w2a[:, half, :], start=(half == 0), stop=False)
                    last = pe.matmul(PS[:, 2, t], selc[:, t], b2a[:], start=False, stop=True)
                last.then_inc(s["s3_o"], 1)
                pe.wait_ge(s["s3_xn"], b + 1)
                transposes(3, xn, "s3_xT")
                pe.wait_ge(s["s3_hi"], b + 1)
                pe.wait_ge(s["s3_lo"], b + 1)
                mm3(pe, PS[:, 4, 0:S], (wd_hi[:], wd_lo[:]), (x2_hi[:, b, :], x2_lo[:, b, :])).then_inc(s["s3_lat"], 1)
                pe.wait_ge(s["s3_llo"], b + 1)

            def proj(k, p, b):
                if not (isinstance(k, int) and k < 1):
                    pe.wait_ge(s["a_qlo"], k)
                    pe.wait_ge(s["a_klo"], k)
                w = slice(128 * p, 128 * p + 128)
                mm3(pe, PS[:, 0, 0:S], (wq_hi[:, w], wq_lo[:, w]), (x2_hi[:, b, :], x2_lo[:, b, :]))
                mm3(pe, PS[:, 0, S:2 * S], (wk_hi[:, w], wk_lo[:, w]), (lat_hi[:, b, :], lat_lo[:, b, :])).then_inc(s["a_proj"], 1)

            def values(b, g):
                n = 4 * b + g
                if g:
                    pe.wait_ge(s["a_vs"], n)
                t, w = slice(128 * (g // 2), 128 * (g // 2) + 128), slice(512 * (g % 2), 512 * (g % 2) + 512)
                mm3(pe, PS[:, 0, :], (ls_hi[:, t], ls_lo[:, t]), (wv_hi[:, w], wv_lo[:, w])).then_inc(s["a_v"], 1)

            def scores(k, p):
                pe.wait_ge(s["a_qlo"], k + 1)
                pe.wait_ge(s["a_klo"], k + 1)
                if not (isinstance(k, int) and k < 1):
                    pe.wait_ge(s["a_max"], 2 * k)
                for h in range(2):
                    r = slice(64 * h, 64 * h + 64)
                    for c in range(C):
                        t = slice(128 * c, 128 * c + 128)
                        dst = PS[:, 1 + h, 0:128] if c == 0 else PS[:, 1 + h, 128:384]
                        mm3(pe, dst, (q_hi[r, p, t], q_lo[r, p, t]), (k_hi[r, p, 0:128 * c + 128], k_lo[r, p, 0:128 * c + 128]),
                            stop=False, skip=True)
                        last = pe.matmul(PS[:, 1 + h, 256 * c:256 * c + 128], identb[:], maskneg[:], start=False, stop=True,
                                         skip_group_check=True)
                last.then_inc(s["a_s"], 1)

            def turn_max(k, p):
                if not (isinstance(k, int) and k < 2):
                    pe.wait_ge(s["a_exp"], k - 1)
                elif k == 1:
                    pe.wait_ge(s["a_cs"], 1)
                pe.wait_ge(s["a_max"], 2 * k + 2)
                for c in range(C):
                    last = pe.transpose(PS[0:2, 3 + c, 384:512], negm[:, p % 2, c, :], ident[:])
                last.then_inc(s["a_c"], 1)

            def scores_t(k, p, final=False):
                pe.wait_ge(s["a_cs"], k + 1 if final else k + 2)
                if not (isinstance(k, int) and k < 1):
                    pe.wait_ge(s["a_exp"], k)
                for h in range(2):
                    r = slice(64 * h, 64 * h + 64)
                    for c in range(C):
                        t, kt = slice(128 * c, S), slice(128 * c, 128 * c + 128)
                        dst = PS[:, 3 + h, 256 * c:256 + 128 * c]
                        mm3(pe, dst, (k_hi[r, p, kt], k_lo[r, p, kt]), (q_hi[r, p, t], q_lo[r, p, t]), stop=False)
                        last = pe.matmul(dst, sel2r[:, h, :], negc[:, p % 2, t], start=False, stop=True)
                last.then_inc(s["a_st"], 1)

            def attend(k, p, b, par):
                pe.wait_ge(s["a_msk"], k + 1)
                pe.wait_ge(s["a_vs"], 4 * b + 4)
                if not (isinstance(k, int) and k < 1):
                    pe.wait_ge(s["a_yn"], k)
                for c in range(C):
                    for h in range(2):
                        dst = PS[:, 5, 65 * (2 * c + h):65 * (2 * c + h) + 65]
                        for kt in range(c + 1):
                            last = pe.matmul(dst, pT[:, p % 2, h, 256 * kt + 128 * (c - kt):256 * kt + 128 * (c - kt) + 128],
                                             v65[:, par, kt, 2 * p + h, :], start=(kt == 0), stop=(kt == c))
                last.then_inc(s["a_y"], 1)

            def turn_y(k, p):
                pe.wait_ge(s["a_yn"], k + 1)
                if not (isinstance(k, int) and k < 1):
                    pe.wait_ge(s["a_ylo"], k)
                for c in range(C):
                    last = pe.transpose(PS[:, 6, 128 * c:128 * c + 128], yn[:, p % 2, c, :, :].rearrange("p h d -> p (h d)"), ident[:])
                last.then_inc(s["a_yT"], 1)

            def project(k, p, b):
                pe.wait_ge(s["a_ylo"], k + 1)
                if p == 0 and not (isinstance(b, int) and b == 0):
                    pe.wait_ge(s["a_x"], b)
                w = slice(128 * p, 128 * p + 128)
                for c in range(C):
                    t = slice(128 * c, 128 * c + 128)
                    last = mm3(pe, PS[:, 7, t], (y_hi[:, t], y_lo[:, t]), (wo_hi[:, w], wo_lo[:, w]),
                               start=(p == 0 and c == 0), stop=(p == NP - 1), skip=True)
                last.then_inc(s["a_o"], 1)

            def body(b, first, last):
                if not last:
                    pe.wait_ge(s["a_ls"], 2 * b + 2)
                    if not first:
                        pe.wait_ge(s["a_qlo"], NP * b)
                        pe.wait_ge(s["a_klo"], NP * b)
                    for g in range(4):
                        values(b, g)
                    pe.wait_ge(s["a_vs"], 4 * b + 4)
                for p in range(NP if not last else LAG + 1):
                    if not last:
                        proj(NP * b + p, p, b)
                    for lag, stage in ((2, turn_max), (4, attend), (1, scores), (5, turn_y), (3, scores_t), (6, project)):
                        kk = p - lag
                        if (first and kk < 0) or (last and kk >= 0):
                            continue
                        bb = b - 1 if kk < 0 else b
                        k = NP * b + kk
                        if stage is attend:
                            stage(k, kk % NP, bb, bb % 2)
                        elif stage is project:
                            stage(k, kk % NP, bb)
                        elif stage is scores_t:
                            stage(k, kk % NP, final=last and kk == -1)
                        else:
                            stage(k, kk % NP)
            body(0, True, False)
            with pe.Fori(1, B) as b:
                body(b, False, False)
            body(B, False, True)

            with pe.Fori(0, B) as b:
                pe.wait_ge(s["s5_xn"], b + 1)
                transposes(0, xn, "s5_xT")
                pe.wait_ge(s["s5_xTs"], b + 1)
                for c in range(C):
                    last = pe.matmul(PS[:, 1, 10 * c:10 * c + 10], xT[:, 128 * c:128 * c + 128], wg1[:], start=True, stop=True)
                last.then_inc(s["s5_lg"], 1)
                pe.wait_ge(s["s5_lo"], b + 1)
                pe.wait_ge(s["s5_lgs"], 2 * b + 2)
            with pe.Fori(0, B) as b:
                x3 = (x3_hi[:, b, :], x3_lo[:, b, :])
                for n in range(4):
                    for m in range(2):
                        o = 512 * (n % 2) + 256 * (n // 2) + 128 * m
                        last = mm3(pe, PS[:, n, S * m:S * m + S], (wh_hi[:, o:o + 128], wh_lo[:, o:o + 128]), x3)
                    if n == 1:
                        last.then_inc(s["f_ha"], 1)
                last.then_inc(s["f_hb"], 1)
                pe.wait_ge(s["f_glo"], b + 1)
                for c in range(C):
                    t = slice(128 * c, 128 * c + 128)
                    if c:
                        pe.wait_ge(s["f_pr"], 2 * b + c)
                    for n in range(2):
                        for m in range(2):
                            last = mm3(pe, PS[:, 4 + n, :], (hT_hi[:, 2 + m, t], hT_lo[:, 2 + m, t]),
                                       (we_hi[:, 1024 * m + 512 * n:1024 * m + 512 * n + 512], we_lo[:, 1024 * m + 512 * n:1024 * m + 512 * n + 512]),
                                       start=(m == 0), stop=(m == 1))
                    if c == 0:
                        for c2 in range(C):
                            t2 = slice(128 * c2, 128 * c2 + 128)
                            for m in range(2):
                                last = mm3(pe, PS[:, 6, t2], (hT_hi[:, m, t2], hT_lo[:, m, t2]),
                                           (wf_hi[:, 128 * m:128 * m + 128], wf_lo[:, 128 * m:128 * m + 128]), start=(m == 0), stop=(m == 1))
                    last.then_inc(s["f_ex"], 1)
                pe.wait_ge(s["f_y"], b + 1)


_INS = ["x", "wqkv0", "wout0", "wgate0", "bgate0", "w1_0", "b1_0", "w2_0", "b2_0", "wdown", "wkup", "wvup",
        "wq1", "wout1", "win1", "w1_1", "wff1", "wexp1", "wgate1", "bgate1", "c_ident", "c_identb", "c_causal",
        "c_maskneg", "c_mask4", "c_block", "c_expand", "c_sel2", "c_desc"]


def kernel(**inputs):
    import ml_dtypes
    import numpy as np
    import concourse.bacc as _bacc
    from concourse.bass_utils import run_bass_kernel_spmd as _run

    i = {k: np.asarray(a) for k, a in inputs.items()}
    HDIM = NH * HD
    p = np.arange(128)
    j = np.arange(128)
    a = {
        "x": i["L0_attn_x"].reshape(NT, 128, D).transpose(1, 0, 2),
        "wqkv0": i["L0_attn_w_qkv"].T, "wout0": i["L0_attn_w_out"].T,
        "wgate0": i["L0_ffn_w_gate_w"], "bgate0": np.broadcast_to(i["L0_ffn_w_gate_b"], (128, E)),
        "w1_0": i["L0_ffn_W1"].reshape(2, 4, D, SUB).transpose(2, 0, 1, 3).reshape(128, 2, 128),
        "b1_0": i["L0_ffn_b1"].reshape(2, 128).T,
        "w2_0": i["L0_ffn_W2"].reshape(2, 128, D).transpose(1, 0, 2),
        "b2_0": i["L0_ffn_b2"],
        "wdown": i["L1_attn_w_kv_down"],
        "wkup": i["L1_attn_w_kv_up"][:, :HDIM], "wvup": i["L1_attn_w_kv_up"][:, HDIM:],
        "wq1": i["L1_attn_w_q"],
        "wout1": i["L1_attn_w_out"].reshape(NP, 128, D).transpose(1, 0, 2).reshape(128, NP * D),
        "win1": i["L1_ffn_w_in"].T, "w1_1": i["L1_ffn_w1"].T,
        "wff1": i["L1_ffn_w_out"].T.reshape(2, 128, D).transpose(1, 0, 2).reshape(128, 2 * D),
        "wexp1": i["L1_ffn_w2"].transpose(2, 0, 1).reshape(2, 128, E, D).transpose(1, 0, 2, 3).reshape(128, 2 * E * D),
        "wgate1": np.concatenate([i["L1_ffn_wg"], i["L1_ffn_we"]]).T,
        "bgate1": np.broadcast_to(np.concatenate([i["L1_ffn_gb"], i["L1_ffn_eb"]]), (128, 10)),
        "c_ident": np.eye(128, dtype=np.float32),
        "c_identb": np.eye(128, dtype=ml_dtypes.bfloat16),
        "c_causal": (j[None, :] >= p[:, None]).astype(np.float32),
        "c_maskneg": np.where(j[None, :] > p[:, None], -1e30, 0.0).astype(ml_dtypes.bfloat16),
        "c_mask4": ((p[:, None] // LD) % 4 == np.arange(4)).astype(np.float32),
        "c_block": np.broadcast_to(((p[:, None] // LD) == np.arange(LH))[:, :, None], (128, LH, LD + 1)).astype(np.float32),
        "c_expand": (np.arange(E)[:, None, None] == 4 * np.arange(2)[None, :, None] + j // SUB).astype(ml_dtypes.bfloat16),
        "c_sel2": np.broadcast_to(np.eye(2, dtype=np.float32)[:, :, None], (2, 2, 128)),
        "c_desc": np.broadcast_to(np.arange(E, 0, -1, dtype=np.float32), (128, E)),
    }
    nc = _bacc.Bacc("TRN2", target_bir_lowering=False, num_devices=1)
    arrays, args = {}, []
    for name in _INS:
        arr = np.ascontiguousarray(a[name])
        arrays[f"in_{name}"] = arr
        args.append(nc.dram_tensor(f"in_{name}", arr.shape, mybir.dt.from_np(arr.dtype), kind="ExternalInput").ap())
    args.append(nc.dram_tensor("out_0", (128, B, C, D), F32, kind="ExternalOutput").ap())
    build(nc, *args)
    r = _run(nc, [arrays], core_ids=[0])
    return r.results[0]["out_0"].transpose(1, 2, 0, 3).reshape(B, S, D)
```

```python
from contextlib import ExitStack

import concourse.bass as bass
from concourse import mybir

F32 = mybir.dt.float32
F32R = mybir.dt.float32r
BF16 = mybir.dt.bfloat16
ALU = mybir.AluOpType
ACT = mybir.ActivationFunctionType
AX_X = mybir.AxisListType.X

B, S, D = 8, 256, 128
C = S // 128
NT = B * C
LH, LD = 16, 8
E = 8
SUB = 32
K_TOP = S // 2
NH, HD = 16, 64
NP = NH // 2
HID = 256
LN_EPS = 1e-5
EPS = 1e-6
NV = 4 * C
KV = LH * (LD + 1) * LD
CUTS = dict(down=128, kup=NH * HD, vup=NH * HD, q=NH * HD, out=NP * D, hid=1024, exp=2048, ffn=256)
CHUNK = sum(CUTS.values()) // NT
NK = B * NP
LAST_LAG = 10


def build(nc, x_in, wqkv0, wout0, wgate0, bgate0, w1_0, b1_0, w2_0, b2_0, wcut, wgate1, bgate1,
          c_ident, c_identb, c_causal, c_maskneg, c_expand, c_sel2, c_desc, out):
    with ExitStack() as ctx:
        def sb(name, shape, dt=F32):
            return ctx.enter_context(nc.sbuf_tensor(name, shape, dt))

        def sem(name):
            return ctx.enter_context(nc.semaphore(name))

        X = sb("X", [128, NT, D])
        wqkv = sb("wqkv", [128, 3 * D])
        wo0 = sb("wo0", [128, D])
        wg0 = sb("wg0", [128, E])
        bg0 = sb("bg0", [128, E])
        w1a = sb("w1a", [128, 2, 128])
        b1a = sb("b1a", [128, 2])
        w2a = sb("w2a", [128, 2, D])
        b2a = sb("b2a", [E, D])
        wstage = sb("wstage", [128, 2, CHUNK])
        whi, wlo = (sb(n, [128, NT * CHUNK], F32R) for n in ("whi", "wlo"))
        at, parts = 0, {}
        for name, cols in CUTS.items():
            parts[name] = (whi[:, at:at + cols], wlo[:, at:at + cols])
            at += cols
        whic, wloc = (w[:, :].rearrange("p (k c) -> p k c", k=NT) for w in (whi, wlo))
        (wd_hi, wd_lo), (wk_hi, wk_lo), (wv_hi, wv_lo), (wq_hi, wq_lo) = (parts[n] for n in ("down", "kup", "vup", "q"))
        (wo_hi, wo_lo), (wh_hi, wh_lo), (we_hi, we_lo), (wf_hi, wf_lo) = (parts[n] for n in ("out", "hid", "exp", "ffn"))
        wg1 = sb("wg1", [128, 10])
        bg1 = sb("bg1", [128, 10])
        ident = sb("ident", [128, 128])
        identb = sb("identb", [128, 128], BF16)
        causal = sb("causal", [128, 128])
        maskneg = sb("maskneg", [128, 128], BF16)
        ones = sb("ones", [128, 128])
        expand = sb("expand", [E, 2, 128], BF16)
        sel2 = sb("sel2", [2, 2, 128])
        sel2r = sb("sel2r", [2, 2, 128], F32R)
        desc = sb("desc", [128, E])

        stats = sb("stats", [128, NT, 6])
        mv = sb("mv", [128, NT, 2])
        veps = sb("veps", [128, NT])
        rstd = sb("rstd", [128, NT])
        neghalf = sb("neghalf", [128, NT])
        rstd3 = rstd[:, :, None]
        xn = sb("xn", [128, C, D])
        xT = sb("xT", [128, S])
        oT = sb("oT", [128, S])
        early = sb("early", [128, 2 * C * NH * (HD + 1)])
        mid = sb("mid", [128, 2 * 2 * 512])
        kv = early[:, 0:3 * KV].rearrange("p (n a) -> p n a", n=3)
        qk = early[:, 3 * KV:3 * KV + C * 2 * D].rearrange("p (c a) -> p c a", c=C)
        nd = early[:, 3 * KV + C * 2 * D:3 * KV + C * 2 * D + KV // LD]
        v9 = sb("v9", [128, C, LD + 1, LH])
        neg = sb("neg", [128, 2 * D])
        ex = sb("ex", [128, C, 2 * D])
        mul = sb("mul", [128, KV])
        den0 = sb("den0", [128, LH])
        o0 = sb("o0", [128, C, D])
        x1T = early[:, 0:B * S].rearrange("p (b t) -> p b t", b=B)
        gate = sb("gate", [128, NT, E])
        ga, gb_, gc, gd = (sb(f"g{i}", [128, NT, E]) for i in range(4))
        gm = sb("gm", [128, NT, 1])
        gs = sb("gs", [128, NT, 1])
        dsum = sb("dsum", [128, C * E])
        route = sb("route", [128, C, B, E])
        rank = [sb(f"rank{i}", [B * E, S]) for i in range(2)]
        top8 = sb("top8", [B * E, 8])
        selb = sb("selb", [B * E, S], BF16)
        sele = sb("sele", [E, B, S], BF16)
        selc = sb("selc", [E, S])
        hs = mid[:, 4 * S:6 * S].rearrange("p (n t) -> p n t", n=2)
        hm = mid[:, 6 * S:8 * S].rearrange("p (n t) -> p n t", n=2)
        x2_hi, x2_lo = sb("x2_hi", [128, B, S], F32R), sb("x2_lo", [128, B, S], F32R)
        lat_hi, lat_lo = sb("lat_hi", [128, B, S], F32R), sb("lat_lo", [128, B, S], F32R)
        ls_hi, ls_lo = sb("ls_hi", [128, S], F32R), sb("ls_lo", [128, S], F32R)
        kk2 = sb("kk2", [128, 4, 2, S], F32R)
        qq2 = sb("qq2", [128, 4, 2, S], F32R)
        ql = sb("ql", [64, 4, 2, S], F32R)
        v65 = early[:, :].rearrange("p (n c h d) -> p n c h d", n=2, c=C, h=NH)
        negm = sb("negm", [128, 2, C, 2])
        negc = sb("negc", [2, 2, 384], F32R)
        pT = mid[:, :].rearrange("p (n h t) -> p n h t", n=2, h=2)
        rden = sb("rden", [128, 2, C, 2, 1])
        yn = sb("yn", [128, 2, C, 2, HD])
        y_hi, y_lo = sb("y_hi", [128, S], F32R), sb("y_lo", [128, S], F32R)
        x3_hi, x3_lo = x2_hi, x2_lo
        prod = early[:, 0:2048].rearrange("p (c e d) -> p c e d", c=C, e=E)
        th = early[:, 2080:3104].rearrange("p (n t) -> p n t", n=4)
        hg = early[:, 3104:4128].rearrange("p (n t) -> p n t", n=4)
        hT_hi, hT_lo = (r[:, :, :, :].rearrange("p (n a) h t -> p n (a h) t", n=2) for r in (kk2, qq2))
        sums = mid[:, :].rearrange("p (c a) -> p c a", c=C)
        acc4 = sums[:, :, 0:512].rearrange("p c (e d) -> p c e d", e=4)
        acc2 = sums[:, :, 512:768].rearrange("p c (e d) -> p c e d", e=2)
        acc1 = sums[:, :, 768:896]
        PS = ctx.enter_context(nc.psum_tensor("PS", [128, 8, 512], F32))

        block = ctx.enter_context(nc.Block())

        names = """ld_x0 ld_x1 ld_x2 ld_x3 ld_w0 ld_w1 ld_st0 ld_st1 ones w_split w_hi out_done
            s1_va s1_rs s3_va s3_rs nh s1_xn s1_xn1 s1_xT s1_xTs s1_qkv s1_rel s1_exp s1_vs s1_phi s1_kv s1_pre s1_mul
            s1_red s1_o s1_oT s1_oTs s1_pr s1_res s1_x1T s1_x1s s1_lg s1_lgs s1_vec
            s2_vec s2_d s2_e s2_rt s2_rT s2_rTs s2_sel s2_dma
            s3_selc s3_h s3_g s3_m s3_hm s3_o s3_xn s3_xT s3_hi s3_lo s3_lat s3_lhi s3_llo s3_vec
            a_proj a_hi a_lo a_s a_max a_c a_cs a_st a_exp a_msk a_y a_rec a_yn a_yT a_yhi a_ylo
            a_o a_ot a_to a_x a_ls a_v a_vs a3_va a3_rs a3_vec a3_xn a3_xT a3_hi a3_xs a3_lo a3_lg a3_lgs
            s5g_vec s5g_d s5g_e s5g_e2
            f_ha f_hb f_th f_th2 f_g f_ghi f_glo f_sh f_ex f_pr f_ad f_s1 f_y f_r1""".split()
        s = {n: sem(n) for n in names}

        apart_regs = []

        def wait_apart(eng, *waits):
            values = []
            for _, value in waits:
                if not isinstance(value, int):
                    own = eng.alloc_register(f"apart{len(apart_regs)}")
                    apart_regs.append(own)
                    eng.reg_mov(own, value)
                    value = own
                values.append(value)
            eng.wait_ge(s["ld_x0"], 16)
            for (name, _), value in zip(waits, values):
                eng.wait_ge(s[name], value)

        def chain(eng, name, base=0):
            count = [0]

            def link(ins, start=None, apart=False):
                count[0] += 1
                ins.then_inc(s[name], 1)
                value = (0 if start is None else start) + base + count[0]
                if apart:
                    wait_apart(eng, (name, value))
                else:
                    eng.wait_ge(s[name], value)
            return link, count

        def pipeline(eng, stages, per, total, peel, tail, last):
            def steps(b, count=per):
                for p in range(count):
                    for lag, stage in stages:
                        k = per * b + (p - lag)
                        if isinstance(k, int) and not 0 <= k < total:
                            continue
                        stage(k, (p - lag) % per, b + (p - lag) // per)
            blocks = total // per
            for b in range(peel):
                steps(b)
            with eng.Fori(peel, blocks - tail) as b:
                steps(b)
            for b in range(blocks - tail, blocks):
                steps(b)
            steps(blocks, last)

        def tiles(eng, stages):
            pipeline(eng, stages, C, NT, 3, 1, 4)

        def pairs(eng, stages):
            pipeline(eng, stages, NP, NK, 2, 1, LAST_LAG)

        def sequences(eng, stages):
            pipeline(eng, stages, 2, B, 2, 0, 1)

        def from_(k, n):
            return not isinstance(k, int) or k >= n

        def upto(n, most):
            return min(n, most) if isinstance(n, int) else n

        def mm3(pe, dst, w, m, start=True, stop=True, skip=False):
            pe.matmul(dst, w[0], m[1], start=start, stop=False, skip_group_check=skip)
            pe.matmul(dst, w[1], m[0], start=False, stop=False, skip_group_check=skip)
            return pe.matmul(dst, w[0], m[0], start=False, stop=stop, skip_group_check=skip)

        @block.sync
        def _(sp):
            for n in range(4):
                sp.dma_start(X[:, 4 * n:4 * n + 4, :], x_in[:, 4 * n:4 * n + 4, :]).then_inc(s[f"ld_x{n}"], 16)
                if n == 0:
                    for dst, src in ((ident, c_ident), (wqkv, wqkv0)):
                        sp.dma_start(dst[:], src).then_inc(s["ld_w0"], 16)
            for dst, src in ((causal, c_causal), (wo0, wout0), (wg0, wgate0)):
                sp.dma_start(dst[:], src).then_inc(s["ld_w0"], 16)
            for n in range(2):
                sp.dma_start(wstage[:, n, :], wcut[:, n, :]).then_inc(s[f"ld_st{n}"], 16)
            for dst, src in ((bg0, bgate0), (w1a, w1_0), (b1a, b1_0), (w2a, w2_0), (b2a, b2_0),
                             (expand, c_expand), (identb, c_identb), (maskneg, c_maskneg),
                             (sel2, c_sel2), (desc, c_desc), (wg1, wgate1), (bg1, bgate1)):
                sp.dma_start(dst[:], src).then_inc(s["ld_w1"], 16)
            with sp.Fori(1, B) as b:
                for c in range(C):
                    sp.wait_ge(s["w_split"], C * b + (c - 1))
                    sp.dma_start(wstage[:, c, :], wcut[:, C * b + c, :]).then_inc(s[f"ld_st{c}"], 16)
            sp.wait_ge(s["s2_sel"], 1)
            for b in range(B):
                sp.dma_start(sele[:, b, :], selb[E * b:E * b + E, :]).then_inc(s["s2_dma"], 16)
            with sp.Fori(0, B) as b:
                sp.wait_ge(s["f_y"], b + 1)
                sp.dma_start(out[:, b, :, :], X[:, :, :].rearrange("p (b c) d -> p b c d", c=C)[:, b, :, :]).then_inc(s["out_done"], 16)
            sp.wait_ge(s["out_done"], 16 * B)

        Xb = X[:, :, :].rearrange("p (b c) d -> p b c d", c=C)
        gcb = gc[:, :, :].rearrange("p (b c) e -> p b c e", c=C)
        gateb = gate[:, :, :].rearrange("p (b c) e -> p b c e", c=C)

        @block.gpsimd
        def _(pool):
            pool.memset(v9[:, :, LD, :], 1.0)
            pool.memset(ones[:], 1.0).then_inc(s["ones"], 1)
            pool.memset(neghalf[:], -0.5).then_inc(s["nh"], 1)
            pool.wait_ge(s["nh"], 1)

            def root(stage, n, tiles=C):
                pool.wait_ge(s[stage + "_va"], n)
                pool.tensor_tensor(rstd[:, 0:tiles], veps[:, 0:tiles], neghalf[:, 0:tiles], ALU.pow).then_inc(s[stage + "_rs"], 1)

            def key_values(k, c, b):
                if c == 0 and from_(k, 4):
                    pool.wait_ge(s["s1_pre"], k - 2)
                if c == 1 and from_(k, 2):
                    pool.wait_ge(s["s1_pre"], k - 1)
                pool.wait_ge(s["s1_vs"], k + 1)
                pool.wait_ge(s["s1_phi"], k + 1)
                slot = kv[:, b % 2, :] if c == 0 else kv[:, 2, :]
                pool.tensor_tensor(slot.rearrange("p (e h d) -> p e h d", e=LD + 1, h=LH),
                                   v9[:, c, :, :][:, :, :, None].broadcast_to([128, LD + 1, LH, LD]),
                                   qk[:, c, D:2 * D].rearrange("p (h d) -> p h d", h=LH)[:, None, :, :].broadcast_to([128, LD + 1, LH, LD]),
                                   ALU.mult).then_inc(s["s1_kv"], 1)

            def cut_low(k, c, b):
                pool.wait_ge(s["w_hi"], k + 1)
                pool.tensor_tensor(wloc[:, k, :], wstage[:, c, :], whic[:, k, :].bitcast(F32), ALU.subtract).then_inc(s["w_split"], 1)

            root("s1", 1, NT)
            tiles(pool, ((1, key_values), (1, cut_low)))
            root("s1", 2, NT)
            pool.wait_ge(s["ld_w1"], 16 * 12)
            pool.tensor_copy(sel2r[:], sel2[:]).then_inc(s["w_split"], 1)
            pool.wait_ge(s["s2_dma"], 16 * B)
            with pool.Fori(0, B) as b:
                pool.tensor_copy(selc[:], sele[:, b, :]).then_inc(s["s3_selc"], 1)
                pool.wait_ge(s["s3_o"], b + 1)
                root("s3", b + 1)

            pool.wait_ge(s["s3_h"], B)
            pool.memset(v65[:, :, :, :, HD:HD + 1], 1.0).then_inc(s["ones"], 1)

            def causal_zeros(k, p, b):
                wait_apart(pool, ("a_exp", k + 1))
                blk = pT[:, p % 2, :, :].rearrange("s h (b t) -> s (h b) t", t=256)[:, :, 0:128]
                pool.affine_select(out=blk, in_=blk, compare_op=ALU.is_ge, fill=0.0, base=0,
                                   pattern=[[0, 4], [1, 128]], channel_multiplier=-1).then_inc(s["a_msk"], 1)

            def latents(b):
                pool.tensor_copy(ls_hi[:], lat_hi[:, b, :])
                pool.tensor_copy(ls_lo[:], lat_lo[:, b, :]).then_inc(s["a_ls"], 1)

            def next_latents(k, p, b):
                if p == 0 and not (isinstance(b, int) and b + 1 >= B):
                    wait_apart(pool, ("a_v", NV * (b + 1)))
                    latents(b + 1)

            def root3(k, p, b):
                if p == NP - 1:
                    root("a3", b + 1)

            pool.wait_ge(s["s3_llo"], B)
            latents(0)
            pairs(pool, ((0, next_latents), (3, causal_zeros), (7, root3)))

            with pool.Fori(0, B) as b:
                for c in range(C):
                    n = C * b + c
                    pool.wait_ge(s["f_pr"], 2 * n + 2)
                    pool.tensor_tensor(acc4[:, c], prod[:, c, 0:4, :], prod[:, c, 4:8, :], ALU.add).then_inc(s["f_ad"], 1)
                    pool.wait_ge(s["f_ad"], 2 * n + 1)
                    pool.tensor_tensor(acc2[:, c], acc4[:, c, 0:2, :], acc4[:, c, 2:4, :], ALU.add).then_inc(s["f_ad"], 1)
                    pool.wait_ge(s["f_ad"], 2 * n + 2)
                    pool.tensor_tensor(acc1[:, c], acc2[:, c, 0, :], acc2[:, c, 1, :], ALU.add).then_inc(s["f_s1"], 1)

        @block.scalar
        def _(act):
            def turned_output(k, c, b):
                act.wait_ge(s["s1_oT"], k + 1)
                if from_(k, 2):
                    act.wait_ge(s["s1_pr"], k - 1)
                act.copy(oT[:, 128 * c:128 * c + 128], PS[:, 6, 128:256]).then_inc(s["s1_oTs"], 1)

            def turned_tokens(k, c, b):
                act.wait_ge(s["s1_xT"], k + 1)
                if from_(k, 2):
                    act.wait_ge(s["s1_qkv"], k - 1)
                act.copy(xT[:, 128 * c:128 * c + 128], PS[:, 6, 0:128]).then_inc(s["s1_xTs"], 1)

            def exponentials(k, c, b):
                act.wait_ge(s["s1_qkv"], k + 1)
                act.activation(neg[:], PS[:, 7, 0:2 * D], ACT.Relu, scale=-1.0).then_inc(s["s1_rel"], 1)
                if from_(k, 2):
                    act.wait_ge(s["s1_kv"], k - 1)
                act.copy(v9[:, c, 0:LD, :], PS[:, 7, 2 * D:3 * D].rearrange("p (h e) -> p e h", h=LH)).then_inc(s["s1_vs"], 1)
                if from_(k, 2):
                    act.wait_ge(s["s1_phi"], k - 1)
                act.wait_ge(s["s1_rel"], k + 1)
                act.activation(ex[:, c, :], neg[:], ACT.Exp, scale=-1.0).then_inc(s["s1_exp"], 1)

            def cut_high(k, c, b):
                act.wait_ge(s[f"ld_st{c}"], 16 * (b + 1))
                act.copy(whic[:, k, :], wstage[:, c, :]).then_inc(s["w_hi"], 1)

            act.wait_ge(s["ones"], 1)
            tiles(act, ((4, turned_output), (1, exponentials), (1, cut_high), (0, turned_tokens)))

            def turned1(b, par, _):
                act.wait_ge(s["s1_x1T"], b + 1)
                if from_(b, 2):
                    act.wait_ge(s["s1_lg"], b - 1)
                act.copy((xT, oT)[par][:], PS[:, par, 0:S]).then_inc(s["s1_x1s"], 1)
                act.copy(x1T[:, b, :], PS[:, par, 0:S]).then_inc(s["s1_x1s"], 1)

            def logits1(b, par, _):
                act.wait_ge(s["s1_lg"], b + 1)
                act.copy(gateb[:, b, :, :], PS[:, 2 + par, 0:C * E].rearrange("p (c e) -> p c e", c=C)).then_inc(s["s1_lgs"], 1)

            sequences(act, ((0, turned1), (1, logits1)))
            act.wait_ge(s["s2_d"], 1)
            act.activation(gb_[:], ga[:], ACT.Exp).then_inc(s["s2_e"], 1)
            act.wait_ge(s["ld_w1"], 16 * 12)
            with act.Fori(0, B) as b:
                act.wait_ge(s["s3_h"], b + 1)
                for half in range(2):
                    act.activation(hs[:, half, :], PS[:, 0, S * half:S * half + S], ACT.Gelu,
                                   bias=b1a[:, half:half + 1]).then_inc(s["s3_g"], 1)
                act.wait_ge(s["s3_xT"], b + 1)
                act.copy(x2_hi[:, b, :], PS[:, 3, 0:S]).then_inc(s["s3_hi"], 1)
                act.wait_ge(s["s3_lat"], b + 1)
                act.copy(lat_hi[:, b, :], PS[:, 4, 0:S]).then_inc(s["s3_lhi"], 1)

            act.wait_ge(s["ones"], 2)

            def high_parts(k, p, b):
                act.wait_ge(s["a_proj"], k + 1)
                if from_(k, 4):
                    act.wait_ge(s["a_st"], k - 3)
                for h in range(2):
                    for half in range(2):
                        last = act.activation(qq2[64 * half:64 * half + 64, p % 4, h, :], PS[64 * h:64 * h + 64, 0, 0:S], ACT.Copy,
                                              scale=float(HD) ** -0.5)
                for h in range(2):
                    last = act.copy(kk2[0:64, p % 4, h, :], PS[64 * h:64 * h + 64, 0, S:2 * S])
                last.then_inc(s["a_hi"], 1)

            def maxima(k, p, b):
                act.wait_ge(s["a_c"], k + 1)
                if from_(k, 2):
                    act.wait_ge(s["a_st"], k - 1)
                act.copy(negc[:, p % 2, 0:256].rearrange("h (c t) -> h c t", c=C), PS[0:2, 3:5, 384:512])
                act.copy(negc[:, p % 2, 256:384], PS[0:2, 4, 384:512]).then_inc(s["a_cs"], 1)

            def exps(k, p, b):
                act.wait_ge(s["a_st"], k + 1)
                if from_(k, 2):
                    act.wait_ge(s["a_y"], k - 1)
                act.activation(pT[:, p % 2, :, 0:384], PS[:, 3:5, 0:384], ACT.Exp).then_inc(s["a_exp"], 1)

            def keep_values(b, g):
                act.wait_ge(s["a_v"], NV * b + g + 1)
                if from_(b, 2):
                    act.wait_ge(s["a_y"], NP * (b - 2) + 2 * (g // 2) + 2)
                h0 = 4 * (g // 2)
                act.copy(v65[:, b % 2, g % 2, h0:h0 + 4, 0:HD],
                         PS[:, 6, 0:S].rearrange("p (h d) -> p h d", h=4)).then_inc(s["a_vs"], 1)

            def next_values(k, p, b):
                if not (isinstance(b, int) and b + 1 >= B):
                    keep_values(b + 1, p)

            def turned3(k, p, b):
                if p == NP - 1:
                    act.wait_ge(s["a3_xT"], b + 1)
                    if from_(b, 1):
                        act.wait_ge(s["a3_lg"], b)
                    act.copy(xT[:], PS[:, 6, 0:S]).then_inc(s["a3_xs"], 1)
                    act.copy(x3_hi[:, b, :], PS[:, 6, 0:S]).then_inc(s["a3_hi"], 1)

            def logits3(k, p, b):
                if p == NP - 1:
                    act.wait_ge(s["a3_lg"], b + 1)
                    lg = PS[:, 6, 0:C * 10].rearrange("p (c e) -> p c e", c=C)
                    act.copy(gateb[:, b, :, :], lg[:, :, 2:10])
                    act.copy(gcb[:, b, :, 0:2], lg[:, :, 0:2]).then_inc(s["a3_lgs"], 1)

            for g in range(NV):
                keep_values(0, g)
            pairs(act, ((0, high_parts), (2, maxima), (0, next_values), (9, turned3), (10, logits3), (3, exps)))

            act.wait_ge(s["s5g_d"], 1)
            act.activation(gb_[:], ga[:], ACT.Exp).then_inc(s["s5g_e"], 1)
            act.wait_ge(s["s5g_d"], 2)
            act.activation(gd[:], ga[:], ACT.Exp).then_inc(s["s5g_e2"], 1)

            def gated(b, par):
                act.wait_ge(s["f_ha"], b + 1)
                if from_(b, 1):
                    act.wait_ge(s["f_g"], b)
                act.activation(th, PS[:, 0:2, :].rearrange("p n (m t) -> p (n m) t", m=2), ACT.Tanh, scale=0.5).then_inc(s["f_th"], 1)
                act.wait_ge(s["f_g"], b + 1)
                if from_(b, 2):
                    act.wait_ge(s["f_sh"], b - 1)
                act.copy(hT_hi[:, par], hg).then_inc(s["f_ghi"], 1)
            gated(0, 0)
            gated(1, 1)
            with act.Fori(1, B // 2) as i:
                gated(2 * i, 0)
                gated(2 * i + 1, 1)

        @block.vector
        def _(v):
            def moments_all(n, x_ready):
                for k in range(NT):
                    if x_ready:
                        x_ready(k)
                    last = v.bn_stats(stats[:, k, :], X[:, k, :])
                last.then_inc(s["s1_vec"], 1)
                v.wait_ge(s["s1_vec"], 2 * n - 1)
                for k in range(NT):
                    last = v.bn_aggr(mv[:, k, :], stats[:, k, :])
                last.then_inc(s["s1_vec"], 1)
                v.wait_ge(s["s1_vec"], 2 * n)
                v.tensor_scalar(veps[:], mv[:, :, 1], LN_EPS, None, ALU.add).then_inc(s["s1_va"], 1)
                v.wait_ge(s["s1_rs"], n)

            def moments(b, link, start, stage):
                for c in range(C):
                    last = v.bn_stats(stats[:, c, :], Xb[:, b, c, :])
                link(last, start, apart=True)
                for c in range(C):
                    last = v.bn_aggr(mv[:, c, :], stats[:, c, :])
                link(last, start)
                v.tensor_scalar(veps[:, 0:C], mv[:, 0:C, 1], LN_EPS, None, ALU.add).then_inc(s[stage + "_va"], 1)

            def normalised(b, stage, n):
                v.wait_ge(s[stage + "_rs"], n)
                for c in range(C):
                    last = v.tensor_scalar(xn[:, c, :], Xb[:, b, c, :], mv[:, c, 0:1], rstd[:, c:c + 1],
                                           ALU.subtract, ALU.mult)
                return last

            def layernorm(b, link, start, stage, n):
                moments(b, link, start, stage)
                return normalised(b, stage, n)

            def part_ready(k):
                if k % 4 == 0:
                    v.wait_ge(s[f"ld_x{k // 4}"], 16)
            moments_all(1, part_ready)

            def apply1(k, c, b):
                if from_(k, 2):
                    v.wait_ge(s["s1_xT"], k - 1)
                v.tensor_scalar(xn[:, c, :], X[:, k, :], mv[:, k, 0:1], rstd3[:, k, :],
                                ALU.subtract, ALU.mult).then_inc(s["s1_xn"], 1)

            def features(k, c, b):
                if from_(k, 2):
                    v.wait_ge(s["s1_kv"], k - 1)
                    v.wait_ge(s["s1_mul"], k - 1)
                v.wait_ge(s["s1_exp"], k + 1)
                v.scalar_tensor_tensor(out=qk[:, c, :], in0=PS[:, 7, 0:2 * D], scalar=0.0,
                                       in1=ex[:, c, :], op0=ALU.max, op1=ALU.add).then_inc(s["s1_phi"], 1)

            def times_queries(k, c, b):
                v.wait_ge(s["s1_pre"], k + 1)
                v.tensor_tensor(mul[:].rearrange("p (g e a) -> p g e a", g=3, e=3),
                                PS[:, 3 * c:3 * c + 3, 0:3 * D].rearrange("p g (e a) -> p g e a", e=3),
                                qk[:, c, 0:D][:, None, None, :].broadcast_to([128, 3, 3, D]), ALU.mult).then_inc(s["s1_mul"], 1)

            def attention(k, c, b):
                v.wait_ge(s["s1_mul"], k + 1)
                v.tensor_reduce(nd, mul[:].rearrange("p (n d) -> p n d", d=LD), AX_X, ALU.add).then_inc(s["s1_red"], 1)
                v.wait_ge(s["s1_red"], 3 * k + 1)
                v.tensor_scalar(den0[:], nd[:, LH * LD:LH * LD + LH], EPS, None, ALU.max).then_inc(s["s1_red"], 1)
                v.wait_ge(s["s1_red"], 3 * k + 2)
                v.reciprocal(den0[:], den0[:]).then_inc(s["s1_red"], 1)
                v.wait_ge(s["s1_red"], 3 * k + 3)
                if from_(k, 2):
                    v.wait_ge(s["s1_oT"], k - 1)
                v.tensor_tensor(o0[:, c, :].rearrange("p (h e) -> p e h", h=LH),
                                nd[:, 0:LH * LD].rearrange("p (e h) -> p e h", e=LD),
                                den0[:][:, None, :].broadcast_to([128, LD, LH]), ALU.mult).then_inc(s["s1_o"], 1)

            def residual1(k, c, b):
                v.wait_ge(s["s1_pr"], k + 1)
                v.tensor_tensor(X[:, k, :], X[:, k, :], PS[:, 3 * c + 2, 3 * D:4 * D], ALU.add).then_inc(s["s1_res"], 1)

            tiles(v, ((0, apply1), (3, times_queries), (4, residual1), (1, features), (3, attention)))
            v.wait_ge(s["s1_res"], NT)
            moments_all(2, None)

            def apply1b(b, par, _):
                if from_(b, 2):
                    v.wait_ge(s["s1_x1T"], b - 1)
                for c in range(C):
                    k = C * b + c
                    last = v.tensor_scalar((xn, o0)[par][:, c, :], X[:, k, :], mv[:, k, 0:1], rstd3[:, k, :],
                                           ALU.subtract, ALU.mult)
                last.then_inc(s["s1_xn1"], 1)
            sequences(v, ((0, apply1b),))

            link, _ = chain(v, "s2_vec")
            v.wait_ge(s["s1_lgs"], B)
            v.wait_ge(s["ld_w1"], 16 * 12)
            wideE = [128, NT, E]

            def over(t):
                return t[:].broadcast_to(wideE)
            descb = desc[:, None, :].broadcast_to(wideE)

            def first_max(link, vals, onehot, scratch):
                link(v.tensor_reduce(gm[:], vals, AX_X, ALU.max))
                link(v.tensor_tensor(scratch, vals, over(gm), ALU.is_equal))
                link(v.tensor_tensor(scratch, scratch, descb, ALU.mult))
                link(v.tensor_reduce(gs[:], scratch, AX_X, ALU.max))
                link(v.tensor_tensor(onehot, scratch, over(gs), ALU.is_equal))

            link(v.tensor_tensor(gate[:], gate[:], bg0[:, None, :].broadcast_to(wideE), ALU.add))
            link(v.tensor_reduce(gm[:], gate[:], AX_X, ALU.max))
            v.tensor_tensor(ga[:], gate[:], over(gm), ALU.subtract).then_inc(s["s2_d"], 1)
            v.wait_ge(s["s2_e"], 1)
            link(v.tensor_reduce(gs[:], gb_[:], AX_X, ALU.add))
            link(v.reciprocal(gs[:], gs[:]))
            link(v.tensor_tensor(gate[:], gb_[:], over(gs), ALU.mult))
            first_max(link, gate[:], gb_[:], ga[:])
            link(v.scalar_tensor_tensor(out=gc[:], in0=gb_[:], scalar=-2.0, in1=gate[:], op0=ALU.mult, op1=ALU.add))
            first_max(link, gc[:], gd[:], ga[:])
            link(v.tensor_tensor(gb_[:], gb_[:], gd[:], ALU.add))
            link(v.tensor_tensor(gate[:], gate[:], gb_[:], ALU.mult))
            link(v.tensor_reduce(dsum[:], gate[:].rearrange("p (b c) e -> p (c e) b", c=C), AX_X, ALU.add))
            link(v.tensor_scalar(dsum[:], dsum[:], EPS, None, ALU.add))
            link(v.reciprocal(dsum[:], dsum[:]))
            link(v.tensor_tensor(route[:], gate[:].rearrange("p (b c) e -> p c b e", c=C),
                                 dsum[:].rearrange("p (c e) -> p c e", c=C)[:, :, None, :].broadcast_to([128, C, B, E]), ALU.mult))
            v.tensor_scalar(route[:], route[:], float(B), None, ALU.mult).then_inc(s["s2_rt"], 1)
            v.wait_ge(s["s2_rT"], 1)
            v.wait_ge(s["s1_x1s"], 2 * B)
            link(v.tensor_copy(rank[0][:], PS[0:B * E, 0, 0:S]))
            for r in range(K_TOP // 8):
                link(v.max(top8[:], rank[r % 2][:]))
                link(v.match_replace(rank[(r + 1) % 2][:], top8[:], rank[r % 2][:], -1.0))
            v.tensor_scalar(selb[:], rank[(K_TOP // 8) % 2][:], 0.0, None, ALU.is_lt).then_inc(s["s2_sel"], 1)

            V3 = 3
            with v.Fori(0, B) as b:
                link, count = chain(v, "s3_vec")
                st = b * V3
                v.wait_ge(s["s3_g"], 2 * b + 2)
                v.wait_ge(s["s3_m"], b + 1)
                v.tensor_tensor(hm, PS[:, 1, :].rearrange("p (n t) -> p n t", n=2), hs, ALU.mult).then_inc(s["s3_hm"], 1)
                v.wait_ge(s["s3_o"], b + 1)
                link(v.tensor_tensor(Xb[:, b, :, :], Xb[:, b, :, :], PS[:, 2, 0:S].rearrange("p (c d) -> p c d", c=C), ALU.add), st, apart=True)
                layernorm(b, link, st, "s3", b + 1).then_inc(s["s3_xn"], 1)
                v.wait_ge(s["s3_hi"], b + 1)
                v.tensor_tensor(x2_lo[:, b, :], PS[:, 3, 0:S], x2_hi[:, b, :].bitcast(F32), ALU.subtract).then_inc(s["s3_lo"], 1)
                v.wait_ge(s["s3_lhi"], b + 1)
                v.tensor_tensor(lat_lo[:, b, :], PS[:, 4, 0:S], lat_hi[:, b, :].bitcast(F32), ALU.subtract).then_inc(s["s3_llo"], 1)
                assert count[0] == V3

            def low_parts(k, p, b):
                v.wait_ge(s["a_hi"], k + 1)
                for h in range(2):
                    ps = PS[64 * h:64 * h + 64, 0, :]
                    v.tensor_tensor(kk2[64:128, p % 4, h, :], ps[:, S:2 * S], kk2[0:64, p % 4, h, :].bitcast(F32), ALU.subtract)
                    last = v.scalar_tensor_tensor(out=ql[:, p % 4, h, :], in0=ps[:, 0:S], scalar=float(HD) ** -0.5,
                                                  in1=qq2[0:64, p % 4, h, :].bitcast(F32), op0=ALU.mult, op1=ALU.subtract)
                last.then_inc(s["a_lo"], 1)

            def row_max(k, p, b):
                v.wait_ge(s["a_s"], k + 1)
                if from_(k, 2):
                    v.wait_ge(s["a_c"], k - 1)
                v.tensor_reduce(negm[:, p % 2, 0, :], PS[:, 1:3, 0:128], AX_X, ALU.max, negate=True)
                v.tensor_reduce(negm[:, p % 2, 1, :], PS[:, 1:3, 128:384], AX_X, ALU.max, negate=True).then_inc(s["a_max"], 1)

            def normalise(k, p, b):
                v.wait_ge(s["a_y"], k + 1)
                if from_(k, 2):
                    v.wait_ge(s["a_yT"], k - 1)
                y = PS[:, 5, 0:C * 2 * (HD + 1)].rearrange("p (c h d) -> p c h d", c=C, h=2)
                v.reciprocal(rden[:, p % 2], y[:, :, :, HD:HD + 1]).then_inc(s["a_rec"], 1)
                v.wait_ge(s["a_rec"], k + 1)
                v.tensor_tensor(yn[:, p % 2], y[:, :, :, 0:HD], rden[:, p % 2].broadcast_to([128, C, 2, HD]),
                                ALU.mult).then_inc(s["a_yn"], 1)

            def turned_y(k, p, b):
                v.wait_ge(s["a_yT"], k + 1)
                if from_(k, 1):
                    v.wait_ge(s["a_o"], k)
                ps = PS[:, 6, S:2 * S]
                v.tensor_copy(y_hi[:], ps).then_inc(s["a_yhi"], 1)
                v.wait_ge(s["a_yhi"], k + 1)
                v.tensor_tensor(y_lo[:], ps, y_hi[:].bitcast(F32), ALU.subtract).then_inc(s["a_ylo"], 1)

            def output(k, p, b):
                if p == NP - 1:
                    v.wait_ge(s["a_o"], k + 1)
                    v.tensor_copy(oT[:], PS[:, 7, 0:S]).then_inc(s["a_ot"], 1)

            def residual(k, p, b):
                if p == NP - 1:
                    v.wait_ge(s["a_to"], b + 1)
                    v.tensor_tensor(Xb[:, b, :, :], Xb[:, b, :, :], PS[:, 7, S:2 * S].rearrange("p (c d) -> p c d", c=C), ALU.add).then_inc(s["a_x"], 1)

            def norm3(k, p, b):
                if p == NP - 1:
                    link, count = chain(v, "a3_vec")
                    wait_apart(v, ("a_x", b + 1))
                    moments(b, link, b * 2, "a3")

            def apply3(k, p, b):
                if p == NP - 1:
                    normalised(b, "a3", b + 1).then_inc(s["a3_xn"], 1)

            def low3(k, p, b):
                if p == NP - 1:
                    v.wait_ge(s["a3_hi"], b + 1)
                    v.tensor_tensor(x3_lo[:, b, :], PS[:, 6, 0:S], x3_hi[:, b, :].bitcast(F32), ALU.subtract).then_inc(s["a3_lo"], 1)

            pairs(v, ((5, turned_y), (6, output), (0, low_parts), (1, row_max), (9, low3), (4, normalise), (6, residual), (7, norm3), (8, apply3)))

            v.wait_ge(s["a3_lgs"], B)
            link, _ = chain(v, "s5g_vec")
            link(v.tensor_tensor(gc[:, :, 0:2], gc[:, :, 0:2], bg1[:, None, 0:2].broadcast_to([128, NT, 2]), ALU.add))
            link(v.tensor_tensor(gate[:], gate[:], bg1[:, None, 2:10].broadcast_to(wideE), ALU.add))
            link(v.tensor_reduce(gm[:], gc[:, :, 0:2], AX_X, ALU.max))
            link(v.memset(ga[:], 0.0))
            v.tensor_tensor(ga[:, :, 0:2], gc[:, :, 0:2], gm[:].broadcast_to([128, NT, 2]), ALU.subtract).then_inc(s["s5g_d"], 1)
            v.wait_ge(s["s5g_e"], 1)
            g01 = gb_[:, :, 0:2]
            link(v.tensor_reduce(gs[:], g01, AX_X, ALU.add))
            link(v.reciprocal(gs[:], gs[:]))
            link(v.tensor_tensor(gc[:, :, 2:4], g01, gs[:].broadcast_to([128, NT, 2]), ALU.mult))
            link(v.tensor_reduce(gm[:], gc[:, :, 2:4], AX_X, ALU.max))
            link(v.tensor_tensor(gc[:, :, 4:5], gc[:, :, 2:3], gc[:, :, 3:4], ALU.is_ge))
            link(v.tensor_scalar(gc[:, :, 5:6], gc[:, :, 4:5], -1.0, 1.0, ALU.mult, ALU.add))
            ing = gd[:].rearrange("p n (g e) -> p n g e", g=2)
            link(v.tensor_copy(ing, gc[:, :, 4:6][:, :, :, None].broadcast_to([128, NT, 2, 4])))
            gview = gate[:].rearrange("p n (g e) -> p n g e", g=2)
            link(v.tensor_reduce(gc[:, :, 6:8], gview, AX_X, ALU.max))
            link(v.tensor_tensor(ga[:].rearrange("p n (g e) -> p n g e", g=2), gview,
                                 gc[:, :, 6:8][:, :, :, None].broadcast_to([128, NT, 2, 4]), ALU.subtract))
            link(v.tensor_copy(gb_[:], gd[:]))
            v.tensor_copy(gate[:, :, 0:1], ga[:, :, 0:1]).then_inc(s["s5g_d"], 1)
            v.wait_ge(s["s5g_e2"], 1)
            link(v.tensor_tensor(gd[:], gd[:], gb_[:], ALU.mult))
            link(v.tensor_reduce(gs[:], gd[:], AX_X, ALU.add))
            link(v.reciprocal(gs[:], gs[:]))
            link(v.tensor_tensor(gate[:], gd[:], over(gs), ALU.mult))
            link(v.tensor_tensor(gate[:], gate[:], over(gm), ALU.mult))
            first_max(link, gate[:], gb_[:], ga[:])
            link(v.scalar_tensor_tensor(out=gc[:], in0=gb_[:], scalar=-2.0, in1=gate[:], op0=ALU.mult, op1=ALU.add))
            first_max(link, gc[:], gd[:], ga[:])
            link(v.tensor_tensor(gb_[:], gb_[:], gd[:], ALU.add))
            link(v.tensor_tensor(gate[:], gate[:], gb_[:], ALU.mult))

            def hidden(b, par):
                a_ps = PS[:, 0:2, :].rearrange("p n (m t) -> p (n m) t", m=2)
                b_ps = PS[:, 2:4, :].rearrange("p n (m t) -> p (n m) t", m=2)
                v.wait_ge(s["f_th"], b + 1)
                v.scalar_tensor_tensor(out=th, in0=th, scalar=1.0, in1=a_ps, op0=ALU.add, op1=ALU.mult).then_inc(s["f_th2"], 1)
                v.wait_ge(s["f_hb"], b + 1)
                if from_(b, 1):
                    v.wait_ge(s["f_ghi"], b)
                v.wait_ge(s["f_th2"], b + 1)
                v.scalar_tensor_tensor(out=hg, in0=th, scalar=0.5, in1=b_ps, op0=ALU.mult, op1=ALU.mult).then_inc(s["f_g"], 1)

            def hidden_lo(b, par):
                v.wait_ge(s["f_ghi"], b + 1)
                v.tensor_tensor(hT_lo[:, par], hg, hT_hi[:, par].bitcast(F32), ALU.subtract).then_inc(s["f_glo"], 1)

            def weigh(b, c, n):
                k = 4 * b + 2 * c + n
                if n == 0 and from_(b, 1):
                    v.wait_ge(s["f_ad"], 2 * (C * (b - 1) + c) + 2)
                v.wait_ge(s["f_ex"], k + 1)
                v.tensor_tensor(prod[:, c, 4 * n:4 * n + 4, :], PS[:, 4 + n, :].rearrange("p (m d) -> p m d", m=4),
                                gateb[:, b, c, 4 * n:4 * n + 4][:, :, None].broadcast_to([128, 4, D]), ALU.mult).then_inc(s["f_pr"], 1)

            def final(b):
                v.wait_ge(s["f_s1"], C * b + C)
                v.wait_ge(s["f_sh"], b + 1)
                v.tensor_tensor(Xb[:, b, :, :], Xb[:, b, :, :], PS[:, 6, 0:S].rearrange("p (c d) -> p c d", c=C), ALU.add).then_inc(s["f_r1"], 1)
                v.wait_ge(s["f_r1"], b + 1)
                v.tensor_tensor(Xb[:, b, :, :], Xb[:, b, :, :], acc1, ALU.add).then_inc(s["f_y"], 1)

            def ffn(b, par, more=True):
                weigh(b, 0, 0)
                if more:
                    hidden(b + 1, 1 - par)
                weigh(b, 0, 1)
                if more:
                    hidden_lo(b + 1, 1 - par)
                weigh(b, 1, 0)
                weigh(b, 1, 1)
                final(b)
            hidden(0, 0)
            hidden_lo(0, 0)
            ffn(0, 0)
            with v.Fori(0, B // 2 - 1) as i:
                ffn(2 * i + 1, 1)
                ffn(2 * i + 2, 0)
            ffn(B - 1, 1, more=False)

        @block.tensor
        def _(pe):
            def transposes(bank, src, sem_name):
                for c in range(C):
                    last = pe.transpose(PS[:, bank, 128 * c:128 * c + 128], src[:, c, :], ident[:])
                last.then_inc(s[sem_name], 1)

            def turn_output(k, c, b):
                pe.wait_ge(s["s1_o"], k + 1)
                pe.wait_ge(s["s1_xTs"], upto(k + 4, NT))
                if from_(k, 1):
                    pe.wait_ge(s["s1_oTs"], k)
                pe.transpose(PS[:, 6, 128:256], o0[:, c, :], ident[:]).then_inc(s["s1_oT"], 1)

            def turn_tokens(k, c, b):
                pe.wait_ge(s["s1_xn"], k + 1)
                if from_(k, 1):
                    pe.wait_ge(s["s1_xTs"], k)
                if from_(k, 4):
                    pe.wait_ge(s["s1_oTs"], k - 3)
                pe.transpose(PS[:, 6, 0:128], xn[:, c, :], ident[:]).then_inc(s["s1_xT"], 1)

            def project1(k, c, b):
                pe.wait_ge(s["s1_xTs"], k + 1)
                if from_(k, 1):
                    pe.wait_ge(s["s1_phi"], k)
                pe.matmul(PS[:, 7, 0:3 * D], xT[:, 128 * c:128 * c + 128], wqkv[:], start=True, stop=True).then_inc(s["s1_qkv"], 1)

            def project_output(k, c, b):
                pe.wait_ge(s["s1_oTs"], k + 1)
                pe.matmul(PS[:, 3 * c + 2, 3 * D:4 * D], oT[:, 128 * c:128 * c + 128], wo0[:], start=True, stop=True).then_inc(s["s1_pr"], 1)

            def states(k, c, b):
                pe.wait_ge(s["s1_kv"], k + 1)
                if from_(k, 2):
                    pe.wait_ge(s["s1_mul"], k - 1)
                for g in range(3):
                    if g == 2 and from_(k, 2):
                        pe.wait_ge(s["s1_res"], k - 1)
                    w, dst = slice(3 * D * g, 3 * D * g + 3 * D), PS[:, 3 * c + g, 0:3 * D]
                    if c == 0:
                        last = pe.matmul(dst, causal[:], kv[:, b % 2, w], start=True, stop=True)
                    else:
                        pe.matmul(dst, causal[:], kv[:, 2, w], start=True, stop=False)
                        last = pe.matmul(dst, ones[:], kv[:, b % 2, w], start=False, stop=True)
                last.then_inc(s["s1_pre"], 1)

            pe.wait_ge(s["ld_w0"], 16 * 5)
            pe.wait_ge(s["ones"], 1)
            tiles(pe, ((4, turn_output), (1, project1), (4, project_output), (2, states), (0, turn_tokens)))

            def turn1(b, par, _):
                pe.wait_ge(s["s1_xn1"], b + 1)
                if from_(b, 2):
                    pe.wait_ge(s["s1_x1s"], 2 * b - 2)
                for c in range(C):
                    last = pe.transpose(PS[:, par, 128 * c:128 * c + 128], (xn, o0)[par][:, c, :], ident[:])
                last.then_inc(s["s1_x1T"], 1)

            def logits1(b, par, _):
                pe.wait_ge(s["s1_x1s"], 2 * b + 1)
                if from_(b, 2):
                    pe.wait_ge(s["s1_lgs"], b - 1)
                for c in range(C):
                    last = pe.matmul(PS[:, 2 + par, E * c:E * c + E], (xT, oT)[par][:, 128 * c:128 * c + 128], wg0[:], start=True, stop=True)
                last.then_inc(s["s1_lg"], 1)

            sequences(pe, ((0, turn1), (1, logits1)))

            pe.wait_ge(s["s2_rt"], 1)
            for c in range(C):
                last = pe.transpose(PS[0:B * E, 0, 128 * c:128 * c + 128], route[:, c, :, :].rearrange("p b e -> p (b e)"), ident[:])
            last.then_inc(s["s2_rT"], 1)

            pe.wait_ge(s["ld_w1"], 16 * 12)
            pe.wait_ge(s["w_split"], NT + 1)
            pe.wait_ge(s["s2_dma"], 16 * B)
            with pe.Fori(0, B) as b:
                for half in range(2):
                    last = pe.matmul(PS[:, 0, S * half:S * half + S], w1a[:, half, :], x1T[:, b, :], start=True, stop=True)
                last.then_inc(s["s3_h"], 1)
                for half in range(2):
                    last = pe.matmul(PS[:, 1, S * half:S * half + S], expand[:, half, :], sele[:, b, :], start=True, stop=True)
                last.then_inc(s["s3_m"], 1)
                pe.wait_ge(s["s3_hm"], b + 1)
                pe.wait_ge(s["s3_selc"], b + 1)
                for c in range(C):
                    t = slice(128 * c, 128 * c + 128)
                    for half in range(2):
                        pe.matmul(PS[:, 2, t], hm[:, half, t], w2a[:, half, :], start=(half == 0), stop=False)
                    last = pe.matmul(PS[:, 2, t], selc[:, t], b2a[:], start=False, stop=True)
                last.then_inc(s["s3_o"], 1)
                pe.wait_ge(s["s3_xn"], b + 1)
                transposes(3, xn, "s3_xT")
                pe.wait_ge(s["s3_hi"], b + 1)
                pe.wait_ge(s["s3_lo"], b + 1)
                mm3(pe, PS[:, 4, 0:S], (wd_hi, wd_lo), (x2_hi[:, b, :], x2_lo[:, b, :])).then_inc(s["s3_lat"], 1)
                pe.wait_ge(s["s3_llo"], b + 1)

            def turn_max(k, p, b):
                if from_(k, 2):
                    pe.wait_ge(s["a_exp"], k - 1)
                elif k == 1:
                    pe.wait_ge(s["a_cs"], 1)
                pe.wait_ge(s["a_max"], k + 1)
                for c in range(C):
                    last = pe.transpose(PS[0:2, 3 + c, 384:512], negm[:, p % 2, c, :], ident[:])
                last.then_inc(s["a_c"], 1)

            def turn_y(k, p, b):
                pe.wait_ge(s["a_yn"], k + 1)
                pe.wait_ge(s["a_vs"], upto(k + 5 + NV, B * NV))
                if p == 4 and from_(b, 1):
                    pe.wait_ge(s["a3_hi"], b)
                    pe.wait_ge(s["a3_lo"], b)
                if p == 5 and from_(b, 1):
                    pe.wait_ge(s["a3_lgs"], b)
                for c in range(C):
                    last = pe.transpose(PS[:, 6, S + 128 * c:S + 128 * c + 128], yn[:, p % 2, c, :, :].rearrange("p h d -> p (h d)"), ident[:])
                last.then_inc(s["a_yT"], 1)

            def project(k, p, b):
                if from_(k, 1):
                    pe.wait_ge(s["a_lo"], k)
                w = slice(128 * p, 128 * p + 128)
                mm3(pe, PS[:, 0, 0:S], (wq_hi[:, w], wq_lo[:, w]), (x2_hi[:, b, :], x2_lo[:, b, :]))
                mm3(pe, PS[:, 0, S:2 * S], (wk_hi[:, w], wk_lo[:, w]), (lat_hi[:, b, :], lat_lo[:, b, :])).then_inc(s["a_proj"], 1)

            def attend(k, p, b):
                pe.wait_ge(s["a_msk"], k + 1)
                pe.wait_ge(s["a_vs"], NV * (b + 1))
                if from_(k, 1):
                    pe.wait_ge(s["a_yn"], k)
                for c in range(C):
                    for h in range(2):
                        dst = PS[:, 5, 65 * (2 * c + h):65 * (2 * c + h) + 65]
                        for kt in range(c + 1):
                            last = pe.matmul(dst, pT[:, p % 2, h, 128 * (c + kt):128 * (c + kt) + 128],
                                             v65[:, b % 2, kt, 2 * p + h, :], start=(kt == 0), stop=(kt == c))
                last.then_inc(s["a_y"], 1)

            def scores(k, p, b):
                pe.wait_ge(s["a_lo"], k + 1)
                if from_(k, 1):
                    pe.wait_ge(s["a_max"], k)
                for h in range(2):
                    for c in range(C):
                        pe.matmul(PS[:, 1 + h, 128 * c:128 + 256 * c],
                                  qq2[:, p % 4, h, 128 * c:128 * c + 128], kk2[:, p % 4, h, 0:128 * c + 128],
                                  start=True, stop=False, skip_group_check=True)
                        last = pe.matmul(PS[:, 1 + h, 256 * c:256 * c + 128], identb[:], maskneg[:], start=False, stop=True,
                                         skip_group_check=True)
                last.then_inc(s["a_s"], 1)

            def values(b, g, *read):
                pe.wait_ge(s["a_ls"], b + 1)
                if read:
                    pe.wait_ge(s[read[0]], read[1])
                t, w = slice(128 * (g % 2), 128 * (g % 2) + 128), slice(S * (g // 2), S * (g // 2) + S)
                mm3(pe, PS[:, 6, 0:S], (ls_hi[:, t], ls_lo[:, t]), (wv_hi[:, w], wv_lo[:, w])).then_inc(s["a_v"], 1)

            def next_values(k, p, b, early=True):
                if early == (p > 0) and not (isinstance(b, int) and b + 1 >= B):
                    values(b + 1, p, *(("a_ylo", k - 4) if from_(k, 5) else ("a_vs", NV + k)))

            def first_values(k, p, b):
                next_values(k, p, b, early=False)

            def scores_t(k, p, b):
                pe.wait_ge(s["a_cs"], upto(k + 2, NK))
                if from_(k, 1):
                    pe.wait_ge(s["a_exp"], k)
                for h in range(2):
                    pe.matmul(PS[:, 3 + h, 0:384], sel2r[:, h, :], negc[:, p % 2, :], start=True, stop=False, skip_group_check=True)
                    for c in range(C):
                        t, kt = slice(128 * c, S), slice(128 * c, 128 * c + 128)
                        dst = PS[:, 3 + h, 256 * c:256 + 128 * c]
                        pe.matmul(dst, kk2[0:64, p % 4, h, kt], ql[:, p % 4, h, t], start=False, stop=False, skip_group_check=True)
                        last = pe.matmul(dst, kk2[:, p % 4, h, kt], qq2[:, p % 4, h, t], start=False, stop=True, skip_group_check=True)
                last.then_inc(s["a_st"], 1)

            def add_output(k, p, b):
                pe.wait_ge(s["a_ylo"], k + 1)
                if p == 0 and from_(b, 1):
                    pe.wait_ge(s["a_x"], b)
                w = slice(128 * p, 128 * p + 128)
                mm3(pe, PS[:, 7, 0:S], (wo_hi[:, w], wo_lo[:, w]), (y_hi[:], y_lo[:]),
                    start=(p == 0), stop=(p == NP - 1), skip=True).then_inc(s["a_o"], 1)

            def turn_output(k, p, b):
                if p == NP - 1:
                    pe.wait_ge(s["a_ot"], b + 1)
                    for c in range(C):
                        last = pe.transpose(PS[:, 7, S + 128 * c:S + 128 * c + 128], oT[:, 128 * c:128 * c + 128], ident[:])
                    last.then_inc(s["a_to"], 1)

            def turn3(k, p, b):
                if p == NP - 1:
                    pe.wait_ge(s["a3_xn"], b + 1)
                    pe.wait_ge(s["a_vs"], upto(k + 10 + NV, B * NV))
                    pe.wait_ge(s["a_ylo"], upto(k + 5, NK))
                    transposes(6, xn, "a3_xT")

            def logits3(k, p, b):
                if p == NP - 1:
                    pe.wait_ge(s["a3_xs"], b + 1)
                    pe.wait_ge(s["a_vs"], upto(k + 11 + NV, B * NV))
                    pe.wait_ge(s["a3_lo"], b + 1)
                    pe.wait_ge(s["a_ylo"], upto(k + 6, NK))
                    for c in range(C):
                        last = pe.matmul(PS[:, 6, 10 * c:10 * c + 10], xT[:, 128 * c:128 * c + 128], wg1[:], start=True, stop=True)
                    last.then_inc(s["a3_lg"], 1)

            for g in range(NV):
                values(0, g, *(("a_vs", g) if g else ()))
            pairs(pe, ((0, project), (5, turn_y), (1, scores), (2, turn_max), (0, next_values), (4, attend), (0, first_values), (9, turn3),
                       (10, logits3), (6, turn_output), (3, scores_t), (5, add_output)))

            pe.wait_ge(s["a3_lo"], B)
            pe.wait_ge(s["a3_lgs"], B)

            def hidden(b, par):
                if from_(b, 1):
                    pe.wait_ge(s["f_g"], b)
                x3 = (x3_hi[:, b, :], x3_lo[:, b, :])
                for n in range(4):
                    for m in range(2):
                        o = 512 * (n % 2) + 256 * (n // 2) + 128 * m
                        last = mm3(pe, PS[:, n, S * m:S * m + S], (wh_hi[:, o:o + 128], wh_lo[:, o:o + 128]), x3)
                    if n == 1:
                        last.then_inc(s["f_ha"], 1)
                last.then_inc(s["f_hb"], 1)

            def outputs(b, par):
                pe.wait_ge(s["f_glo"], b + 1)
                for c in range(C):
                    t = slice(128 * c, 128 * c + 128)
                    for n in range(2):
                        k = 4 * b + 2 * c + n
                        if from_(k, 2):
                            pe.wait_ge(s["f_pr"], k - 1)
                        for m in range(2):
                            w = slice(1024 * m + 512 * n, 1024 * m + 512 * n + 512)
                            last = mm3(pe, PS[:, 4 + n, :], (hT_hi[:, par, 2 + m, t], hT_lo[:, par, 2 + m, t]), (we_hi[:, w], we_lo[:, w]),
                                       start=(m == 0), stop=(m == 1))
                        last.then_inc(s["f_ex"], 1)
                if from_(b, 1):
                    pe.wait_ge(s["f_y"], b)
                for c in range(C):
                    t = slice(128 * c, 128 * c + 128)
                    for m in range(2):
                        last = mm3(pe, PS[:, 6, t], (hT_hi[:, par, m, t], hT_lo[:, par, m, t]),
                                   (wf_hi[:, 128 * m:128 * m + 128], wf_lo[:, 128 * m:128 * m + 128]), start=(m == 0), stop=(m == 1))
                last.then_inc(s["f_sh"], 1)

            hidden(0, 0)
            hidden(1, 1)
            outputs(0, 0)
            with pe.Fori(0, B // 2 - 1) as i:
                hidden(2 * i + 2, 0)
                outputs(2 * i + 1, 1)
                hidden(2 * i + 3, 1)
                outputs(2 * i + 2, 0)
            outputs(B - 1, 1)


_INS = ["x", "wqkv0", "wout0", "wgate0", "bgate0", "w1_0", "b1_0", "w2_0", "b2_0", "wcut", "wgate1", "bgate1",
        "c_ident", "c_identb", "c_causal", "c_maskneg", "c_expand", "c_sel2", "c_desc"]


def kernel(**inputs):
    import ml_dtypes
    import numpy as np
    import concourse.bacc as _bacc
    from concourse.bass_utils import run_bass_kernel_spmd as _run

    i = {k: np.asarray(a) for k, a in inputs.items()}
    HDIM = NH * HD
    p = np.arange(128)
    j = np.arange(128)
    a = {
        "x": i["L0_attn_x"].reshape(NT, 128, D).transpose(1, 0, 2),
        "wqkv0": i["L0_attn_w_qkv"].T, "wout0": i["L0_attn_w_out"].T,
        "wgate0": i["L0_ffn_w_gate_w"], "bgate0": np.broadcast_to(i["L0_ffn_w_gate_b"], (128, E)),
        "w1_0": i["L0_ffn_W1"].reshape(2, 4, D, SUB).transpose(2, 0, 1, 3).reshape(128, 2, 128),
        "b1_0": i["L0_ffn_b1"].reshape(2, 128).T,
        "w2_0": i["L0_ffn_W2"].reshape(2, 128, D).transpose(1, 0, 2),
        "b2_0": i["L0_ffn_b2"],
        "wcut": np.concatenate([
            i["L1_attn_w_kv_down"], i["L1_attn_w_kv_up"][:, :HDIM], i["L1_attn_w_kv_up"][:, HDIM:], i["L1_attn_w_q"],
            i["L1_attn_w_out"].reshape(NP, 128, D).transpose(1, 0, 2).reshape(128, NP * D),
            i["L1_ffn_w_in"].T, i["L1_ffn_w1"].T,
            i["L1_ffn_w2"].transpose(2, 0, 1).reshape(2, 128, E, D).transpose(1, 0, 2, 3).reshape(128, 2 * E * D),
            i["L1_ffn_w_out"].T.reshape(2, 128, D).transpose(1, 0, 2).reshape(128, 2 * D)], axis=1).reshape(128, NT, CHUNK),
        "wgate1": np.concatenate([i["L1_ffn_wg"], i["L1_ffn_we"]]).T,
        "bgate1": np.broadcast_to(np.concatenate([i["L1_ffn_gb"], i["L1_ffn_eb"]]), (128, 10)),
        "c_ident": np.eye(128, dtype=np.float32),
        "c_identb": np.eye(128, dtype=ml_dtypes.bfloat16),
        "c_causal": (j[None, :] >= p[:, None]).astype(np.float32),
        "c_maskneg": np.where(j[None, :] > p[:, None], -1e30, 0.0).astype(ml_dtypes.bfloat16),
        "c_expand": (np.arange(E)[:, None, None] == 4 * np.arange(2)[None, :, None] + j // SUB).astype(ml_dtypes.bfloat16),
        "c_sel2": np.broadcast_to(np.eye(2, dtype=np.float32)[:, :, None], (2, 2, 128)),
        "c_desc": np.broadcast_to(np.arange(E, 0, -1, dtype=np.float32), (128, E)),
    }
    nc = _bacc.Bacc("TRN2", target_bir_lowering=False, num_devices=1)
    arrays, args = {}, []
    for name in _INS:
        arr = np.ascontiguousarray(a[name])
        arrays[f"in_{name}"] = arr
        args.append(nc.dram_tensor(f"in_{name}", arr.shape, mybir.dt.from_np(arr.dtype), kind="ExternalInput").ap())
    args.append(nc.dram_tensor("out_0", (128, B, C, D), F32, kind="ExternalOutput").ap())
    build(nc, *args)
    r = _run(nc, [arrays], core_ids=[0])
    return r.results[0]["out_0"].transpose(1, 2, 0, 3).reshape(B, S, D)
```

```python
from contextlib import ExitStack

import concourse.bass as bass
from concourse import mybir

F32 = mybir.dt.float32
F32R = mybir.dt.float32r
BF16 = mybir.dt.bfloat16
ALU = mybir.AluOpType
ACT = mybir.ActivationFunctionType
AX_X = mybir.AxisListType.X

B, S, D = 8, 256, 128
C = S // 128
NT = B * C
LH, LD = 16, 8
E = 8
SUB = 32
K_TOP = S // 2
NH, HD = 16, 64
NP = NH // 2
LN_EPS = 1e-5
EPS = 1e-6
NV = 4 * C
KV = LH * (LD + 1) * LD
CUTS = dict(down=128, kup=NH * HD, vup=NH * HD, q=NH * HD, out=NP * D, hid=1024, exp=2048, ffn=256)
CHUNK = sum(CUTS.values()) // NT
PARTS = (slice(0, 4), slice(4, NT))
NK = B * NP
EXPERT_BANKS = (4, 5, 7, 4)
GATE = (slice(0, C * (B - 1)), slice(C * (B - 1), NT))
GATE_PARTS = (4, 6, 2, 5, 6, 7)
GATE_LINKS = sum(GATE_PARTS)
LAST_LAG = 10


def build(nc, x_in, wqkv0, wout0, wgate0, bgate0, w1_0, b1_0, w2_0, b2_0, wcut, wgate1, bgate1,
          c_ident, c_identb, c_causal, c_maskneg, c_expand, c_rows, c_sel2, c_desc, out):
    with ExitStack() as ctx:
        def sb(name, shape, dt=F32):
            return ctx.enter_context(nc.sbuf_tensor(name, shape, dt))

        def sem(name):
            return ctx.enter_context(nc.semaphore(name))

        X = sb("X", [128, NT, D])
        wqkv = sb("wqkv", [128, 3 * D])
        wo0 = sb("wo0", [128, D])
        wg0 = sb("wg0", [128, E])
        bg0 = sb("bg0", [128, E])
        w1a = sb("w1a", [128, 2, 128])
        b1a = sb("b1a", [128, 2])
        w2a = sb("w2a", [128, 2, D])
        b2a = sb("b2a", [B * E, D])
        wstage = sb("wstage", [128, 2, CHUNK])
        whi, wlo = (sb(n, [128, NT * CHUNK], F32R) for n in ("whi", "wlo"))
        at, parts = 0, {}
        for name, cols in CUTS.items():
            parts[name] = (whi[:, at:at + cols], wlo[:, at:at + cols])
            at += cols
        whic, wloc = (w[:, :].rearrange("p (k c) -> p k c", k=NT) for w in (whi, wlo))
        (wd_hi, wd_lo), (wk_hi, wk_lo), (wv_hi, wv_lo), (wq_hi, wq_lo) = (parts[n] for n in ("down", "kup", "vup", "q"))
        (wo_hi, wo_lo), (wh_hi, wh_lo), (we_hi, we_lo), (wf_hi, wf_lo) = (parts[n] for n in ("out", "hid", "exp", "ffn"))
        wg1 = sb("wg1", [128, 10])
        bg1 = sb("bg1", [128, 10])
        ident = sb("ident", [128, 128])
        identb = sb("identb", [128, 128], BF16)
        causal = sb("causal", [128, 128])
        maskneg = sb("maskneg", [128, 128], BF16)
        ones = sb("ones", [128, 128])
        expand = sb("expand", [B * E, B, 2 * 128], BF16)
        rows = sb("rows", [B * E, B])
        sel2 = sb("sel2", [66, 2, 1])
        desc = sb("desc", [128, E])

        stats = sb("stats", [128, NT, 6])
        mv = sb("mv", [128, NT, 2])
        veps = sb("veps", [128, NT])
        rstd = sb("rstd", [128, NT])
        neghalf = sb("neghalf", [128, NT])
        rstd3 = rstd[:, :, None]
        xn = sb("xn", [128, C, D])
        xT = sb("xT", [128, S])
        oT = sb("oT", [128, S])
        early = sb("early", [128, 2 * C * NH * (HD + 1)])
        mid = sb("mid", [128, 2 * 2 * 512])
        kv = early[:, 0:3 * KV].rearrange("p (n a) -> p n a", n=3)
        qk = early[:, 3 * KV:3 * KV + C * 2 * D].rearrange("p (c a) -> p c a", c=C)
        nd = early[:, 3 * KV + C * 2 * D:3 * KV + C * 2 * D + KV // LD]
        mul = mid[:, 0:KV]
        ex = mid[:, KV:KV + C * 2 * D].rearrange("p (c a) -> p c a", c=C)
        v9 = mid[:, KV + C * 2 * D:KV + C * 2 * D + C * (LD + 1) * LH].rearrange("p (c e h) -> p c e h", c=C, e=LD + 1)
        neg = sb("neg", [128, 2 * D])
        den0 = sb("den0", [128, LH])
        o0 = sb("o0", [128, C, D])
        x1T = mid[:, :].rearrange("p (b t) -> p b t", b=B)
        gate = sb("gate", [128, NT, E])
        ga, gb_, gc, gd = (sb(f"g{i}", [128, NT, E]) for i in range(4))
        gm = sb("gm", [128, NT, 1])
        gs = sb("gs", [128, NT, 1])
        dsum = sb("dsum", [128, C * E])
        route = sb("route", [128, C, B, E])
        rank = [sb(f"rank{i}", [B * E, S]) for i in range(2)]
        top8 = sb("top8", [B * E, 8])
        selb = sb("selb", [B * E, S], BF16)
        self32 = sb("self32", [B * E, S])
        hs = early[:, 0:B * 2 * S].rearrange("p (b n t) -> p b n t", b=B, n=2)
        hm = mid[:, 0:4 * S].rearrange("p (r n t) -> p r n t", r=2, n=2)
        b2b = mid[0:B * E, 4 * S:4 * S + B * D].rearrange("p (b d) -> p b d", b=B)
        x2_hi, x2_lo = sb("x2_hi", [128, B, S], F32R), sb("x2_lo", [128, B, S], F32R)
        lat_hi, lat_lo = sb("lat_hi", [128, B, S], F32R), sb("lat_lo", [128, B, S], F32R)
        ls_hi, ls_lo = sb("ls_hi", [128, S], F32R), sb("ls_lo", [128, S], F32R)
        kk2 = sb("kk2", [128, 4, 2, S], F32R)
        qq2 = sb("qq2", [128, 4, 2, S], F32R)
        k1 = sb("k1", [66, 4, 2, S], F32R)
        ql = sb("ql", [66, 4, 2, S], F32R)
        v65 = early[:, :].rearrange("p (n c h d) -> p n c h d", n=2, c=C, h=NH)
        negm = sb("negm", [128, 2, C, 2])
        pT = mid[:, :].rearrange("p (n h t) -> p n h t", n=2, h=2)
        rden = sb("rden", [128, 2, C, 2, 1])
        yn = sb("yn", [128, 2, C, 2, HD])
        y_hi, y_lo = sb("y_hi", [128, S], F32R), sb("y_lo", [128, S], F32R)
        x3_hi, x3_lo = x2_hi, x2_lo
        prod = early[:, 0:2048].rearrange("p (c e d) -> p c e d", c=C, e=E)
        th = early[:, 2080:3104].rearrange("p (n t) -> p n t", n=4)
        hg = early[:, 3104:4128].rearrange("p (n t) -> p n t", n=4)
        hT_hi, hT_lo = (r[:, :, :, :].rearrange("p (n a) h t -> p n (a h) t", n=2) for r in (kk2, qq2))
        sums = mid[:, :].rearrange("p (c a) -> p c a", c=C)
        acc4 = sums[:, :, 0:512].rearrange("p c (e d) -> p c e d", e=4)
        acc2 = sums[:, :, 512:768].rearrange("p c (e d) -> p c e d", e=2)
        acc1 = sums[:, :, 768:896]
        PS = ctx.enter_context(nc.psum_tensor("PS", [128, 8, 512], F32))

        block = ctx.enter_context(nc.Block())

        names = """ld_x0 ld_x1 ld_x2 ld_x3 ld_w0 ld_w1 ld_st0 ld_st1 ones w_split w_hi out_done
            s1_va s1_rs s3_va s3_rs s3_res nh s1_xn s1_xn1 s1_xT s1_xTs s1_qkv s1_rel s1_exp s1_vs s1_phi s1_kv s1_pre s1_mul
            s1_red s1_o s1_oT s1_oTs s1_pr s1_res s1_stat s1_x1T s1_x1s s1_lg s1_lgs s1_vec
            s2_vec s2_d s2_e s2_rt s2_rT s2_sel
            s3_b2 s3_h s3_g s3_m s3_hm s3_o s3_xn s3_xT s3_hi s3_lo s3_lat s3_lhi s3_llo s3_vec
            a_proj a_rows a_hi a_lo a_s a_max a_c a_cs a_st a_exp a_msk a_y a_rec a_yn a_yT a_yhi a_ylo
            a_o a_ot a_to a_x a_ls a_v a_vs a3_va a3_rs a3_vec a3_xn a3_xT a3_hi a3_xs a3_lo a3_lg a3_lgs
            s5g_vec s5g_d s5g_e
            f_ha f_hb f_th f_th2 f_g f_ghi f_glo f_sh f_ex f_pr f_ad f_s1 f_y f_r1""".split()
        s = {n: sem(n) for n in names}

        apart_regs = []

        def wait_apart(eng, *waits):
            values = []
            for _, value in waits:
                if not isinstance(value, int):
                    own = eng.alloc_register(f"apart{len(apart_regs)}")
                    apart_regs.append(own)
                    eng.reg_mov(own, value)
                    value = own
                values.append(value)
            eng.wait_ge(s["ld_x0"], 16)
            for (name, _), value in zip(waits, values):
                eng.wait_ge(s[name], value)

        def chain(eng, name, base=0):
            count = [0]

            def link(ins, start=None, apart=False):
                count[0] += 1
                ins.then_inc(s[name], 1)
                value = (0 if start is None else start) + base + count[0]
                if apart:
                    wait_apart(eng, (name, value))
                else:
                    eng.wait_ge(s[name], value)
            return link, count

        def pipeline(eng, stages, per, total, peel, tail, last):
            def steps(b, count=per):
                for p in range(count):
                    for lag, stage in stages:
                        k = per * b + (p - lag)
                        if isinstance(k, int) and not 0 <= k < total:
                            continue
                        stage(k, (p - lag) % per, b + (p - lag) // per)
            blocks = total // per
            for b in range(peel):
                steps(b)
            with eng.Fori(peel, blocks - tail) as b:
                steps(b)
            for b in range(blocks - tail, blocks):
                steps(b)
            steps(blocks, last)

        def tiles(eng, stages):
            pipeline(eng, stages, C, NT, 3, 1, 4)

        def pairs(eng, stages, tail=1):
            pipeline(eng, stages, NP, NK, 2, tail, LAST_LAG)

        def sequences(eng, stages):
            pipeline(eng, stages, 2, B, 2, 0, 1)

        def short(eng, stages):
            pipeline(eng, stages, 2, B, 2, 0, 3)

        def from_(k, n):
            return not isinstance(k, int) or k >= n

        def value_steps(p, b):
            if isinstance(b, int) and b == 0:
                return [(0, 4 * (p // 2) + p % 2, 2)] if p < 4 else [(1, 2 * (p - 4), 1), (1, 2 * (p - 4) + 1, 1)]
            return [] if isinstance(b, int) and b + 1 >= B else [(b + 1, p, 1)]

        def made(k):
            return min(2 * k, k + NV, B * NV) if isinstance(k, int) else k + NV

        def upto(n, most):
            return min(n, most) if isinstance(n, int) else n

        def mm3(pe, dst, w, m, start=True, stop=True, skip=False):
            pe.matmul(dst, w[0], m[1], start=start, stop=False, skip_group_check=skip)
            pe.matmul(dst, w[1], m[0], start=False, stop=False, skip_group_check=skip)
            return pe.matmul(dst, w[0], m[0], start=False, stop=stop, skip_group_check=skip)

        @block.sync
        def _(sp):
            for n in range(4):
                sp.dma_start(X[:, 4 * n:4 * n + 4, :], x_in[:, 4 * n:4 * n + 4, :]).then_inc(s[f"ld_x{n}"], 16)
                if n == 0:
                    for dst, src in ((ident, c_ident), (wqkv, wqkv0)):
                        sp.dma_start(dst[:], src).then_inc(s["ld_w0"], 16)
            for dst, src in ((causal, c_causal), (wo0, wout0), (wg0, wgate0)):
                sp.dma_start(dst[:], src).then_inc(s["ld_w0"], 16)
            for n in range(2):
                sp.dma_start(wstage[:, n, :], wcut[:, n, :]).then_inc(s[f"ld_st{n}"], 16)
            for dst, src in ((bg0, bgate0), (w1a, w1_0), (b1a, b1_0), (w2a, w2_0), (b2a, b2_0),
                             (expand, c_expand), (rows, c_rows), (identb, c_identb), (maskneg, c_maskneg),
                             (desc, c_desc), (wg1, wgate1), (bg1, bgate1)):
                sp.dma_start(dst[:], src).then_inc(s["ld_w1"], 16)
            sp.dma_start(sel2[64:66], c_sel2).then_inc(s["ld_w1"], 16)
            with sp.Fori(1, B) as b:
                for c in range(C):
                    sp.wait_ge(s["w_split"], C * b + (c - 1))
                    sp.dma_start(wstage[:, c, :], wcut[:, C * b + c, :]).then_inc(s[f"ld_st{c}"], 16)
            with sp.Fori(0, B) as b:
                sp.wait_ge(s["f_y"], b + 1)
                sp.dma_start(out[:, b, :, :], X[:, :, :].rearrange("p (b c) d -> p b c d", c=C)[:, b, :, :]).then_inc(s["out_done"], 16)
            sp.wait_ge(s["out_done"], 16 * B)

        Xb = X[:, :, :].rearrange("p (b c) d -> p b c d", c=C)
        gcb = gc[:, :, :].rearrange("p (b c) e -> p b c e", c=C)
        gateb = gate[:, :, :].rearrange("p (b c) e -> p b c e", c=C)

        @block.gpsimd
        def _(pool):
            pool.memset(v9[:, :, LD, :], 1.0)
            pool.memset(ones[:], 1.0).then_inc(s["ones"], 1)
            pool.memset(neghalf[:], -0.5).then_inc(s["nh"], 1)
            pool.wait_ge(s["nh"], 1)

            def root(stage, n, T=slice(0, C)):
                pool.wait_ge(s[stage + "_va"], n)
                pool.tensor_tensor(rstd[:, T], veps[:, T], neghalf[:, T], ALU.pow).then_inc(s[stage + "_rs"], 1)

            def key_values(k, c, b):
                if c == 0 and from_(k, 4):
                    pool.wait_ge(s["s1_pre"], k - 2)
                if c == 1 and from_(k, 2):
                    pool.wait_ge(s["s1_pre"], k - 1)
                pool.wait_ge(s["s1_vs"], k + 1)
                pool.wait_ge(s["s1_phi"], k + 1)
                slot = kv[:, b % 2, :] if c == 0 else kv[:, 2, :]
                pool.tensor_tensor(slot.rearrange("p (e h d) -> p e h d", e=LD + 1, h=LH),
                                   v9[:, c, :, :][:, :, :, None].broadcast_to([128, LD + 1, LH, LD]),
                                   qk[:, c, D:2 * D].rearrange("p (h d) -> p h d", h=LH)[:, None, :, :].broadcast_to([128, LD + 1, LH, LD]),
                                   ALU.mult).then_inc(s["s1_kv"], 1)

            def cut_low(k, c, b):
                pool.wait_ge(s["w_hi"], k + 1)
                pool.tensor_tensor(wloc[:, k, :], wstage[:, c, :], whic[:, k, :].bitcast(F32), ALU.subtract).then_inc(s["w_split"], 1)

            for part in range(2):
                root("s1", 1 + part, PARTS[part])
            tiles(pool, ((1, key_values), (1, cut_low)))
            for part in range(2):
                root("s1", 3 + part, PARTS[part])
            pool.wait_ge(s["ld_w1"], 16 * 13)
            pool.wait_ge(s["s3_h"], B)
            pool.tensor_tensor(b2b, b2a[:, None, :].broadcast_to([B * E, B, D]), rows[:, :, None].broadcast_to([B * E, B, D]),
                               ALU.mult).then_inc(s["s3_b2"], 1)

            def root_s3(b, par, _):
                root("s3", b + 1)
            short(pool, ((1, root_s3),))
            pool.wait_ge(s["s3_hm"], B)
            pool.memset(v65[:, :, :, :, HD:HD + 1], 1.0).then_inc(s["ones"], 1)

            def causal_zeros(k, p, b):
                wait_apart(pool, ("a_exp", k + 1))
                blk = pT[:, p % 2, :, :].rearrange("s h (b t) -> s (h b) t", t=256)[:, :, 0:128]
                pool.affine_select(out=blk, in_=blk, compare_op=ALU.is_ge, fill=0.0, base=0,
                                   pattern=[[0, 4], [1, 128]], channel_multiplier=-1).then_inc(s["a_msk"], 1)

            def latents(b):
                pool.tensor_copy(ls_hi[:], lat_hi[:, b, :])
                pool.tensor_copy(ls_lo[:], lat_lo[:, b, :]).then_inc(s["a_ls"], 1)

            def next_latents(k, p, b):
                for seq, g, wide in value_steps(p, b):
                    if g + 2 * wide - 1 == NV and not (isinstance(seq, int) and seq + 1 >= B):
                        wait_apart(pool, ("a_v", NV * (seq + 1)))
                        latents(seq + 1)

            def root3(k, p, b):
                if p == NP - 1:
                    root("a3", b + 1)

            pool.wait_ge(s["s3_llo"], B)
            latents(0)
            pairs(pool, ((0, next_latents), (3, causal_zeros), (7, root3)), tail=2)

            def add_experts(b):
                for c in range(C):
                    n = C * b + c
                    pool.wait_ge(s["f_pr"], 2 * n + 2)
                    pool.tensor_tensor(acc4[:, c], prod[:, c, 0:4, :], prod[:, c, 4:8, :], ALU.add).then_inc(s["f_ad"], 1)
                    pool.wait_ge(s["f_ad"], 2 * n + 1)
                    pool.tensor_tensor(acc2[:, c], acc4[:, c, 0:2, :], acc4[:, c, 2:4, :], ALU.add).then_inc(s["f_ad"], 1)
                    if c == 0 and from_(b, 1):
                        pool.wait_ge(s["f_y"], b)
                    pool.wait_ge(s["f_ad"], 2 * n + 2)
                    pool.tensor_tensor(acc1[:, c], acc2[:, c, 0, :], acc2[:, c, 1, :], ALU.add).then_inc(s["f_s1"], 1)
            add_experts(0)
            with pool.Fori(1, B) as b:
                add_experts(b)

        @block.scalar
        def _(act):
            def turned_output(k, c, b):
                act.wait_ge(s["s1_oT"], k + 1)
                if from_(k, 2):
                    act.wait_ge(s["s1_pr"], k - 1)
                act.copy(oT[:, 128 * c:128 * c + 128], PS[:, 6, 128:256]).then_inc(s["s1_oTs"], 1)

            def turned_tokens(k, c, b):
                act.wait_ge(s["s1_xT"], k + 1)
                if from_(k, 2):
                    act.wait_ge(s["s1_qkv"], k - 1)
                act.copy(xT[:, 128 * c:128 * c + 128], PS[:, 6, 0:128]).then_inc(s["s1_xTs"], 1)

            def exponentials(k, c, b):
                act.wait_ge(s["s1_qkv"], k + 1)
                act.activation(neg[:], PS[:, 7, 0:2 * D], ACT.Relu, scale=-1.0).then_inc(s["s1_rel"], 1)
                if from_(k, 2):
                    act.wait_ge(s["s1_kv"], k - 1)
                act.copy(v9[:, c, 0:LD, :], PS[:, 7, 2 * D:3 * D].rearrange("p (h e) -> p e h", h=LH)).then_inc(s["s1_vs"], 1)
                if from_(k, 2):
                    act.wait_ge(s["s1_phi"], k - 1)
                act.wait_ge(s["s1_rel"], k + 1)
                act.activation(ex[:, c, :], neg[:], ACT.Exp, scale=-1.0).then_inc(s["s1_exp"], 1)

            def cut_high(k, c, b):
                act.wait_ge(s[f"ld_st{c}"], 16 * (b + 1))
                act.copy(whic[:, k, :], wstage[:, c, :]).then_inc(s["w_hi"], 1)

            act.wait_ge(s["ones"], 1)
            tiles(act, ((4, turned_output), (1, exponentials), (1, cut_high), (0, turned_tokens)))

            def turned1(b, par, _):
                act.wait_ge(s["s1_x1T"], b + 1)
                if from_(b, 2):
                    act.wait_ge(s["s1_lg"], b - 1)
                act.copy((xT, oT)[par][:], PS[:, par, 0:S]).then_inc(s["s1_x1s"], 1)
                act.copy(x1T[:, b, :], PS[:, par, 0:S]).then_inc(s["s1_x1s"], 1)

            def logits1(b, par, _):
                act.wait_ge(s["s1_lg"], b + 1)
                act.copy(gateb[:, b, :, :], PS[:, 2 + par, 0:C * E].rearrange("p (c e) -> p c e", c=C)).then_inc(s["s1_lgs"], 1)

            sequences(act, ((0, turned1), (1, logits1)))
            act.wait_ge(s["s2_d"], 1)
            act.activation(gb_[:], ga[:], ACT.Exp).then_inc(s["s2_e"], 1)
            act.wait_ge(s["ld_w1"], 16 * 13)
            act.wait_ge(s["s1_o"], NT)

            def gelu(b, par, _):
                act.wait_ge(s["s3_h"], b + 1)
                for half in range(2):
                    last = act.activation(hs[:, b, half, :], PS[:, 4 + par, S * half:S * half + S], ACT.Gelu, bias=b1a[:, half:half + 1])
                last.then_inc(s["s3_g"], 1)
            sequences(act, ((0, gelu),))
            act.copy(k1[64:66], sel2[64:66][:, None, :, :].broadcast_to([2, 4, 2, S])).then_inc(s["a_rows"], 1)

            def high_tokens(b, par, _):
                act.wait_ge(s["s3_xT"], b + 1)
                act.copy(x2_hi[:, b, :], PS[:, 3, 0:S]).then_inc(s["s3_hi"], 1)

            def high_latents(b, par, _):
                act.wait_ge(s["s3_lat"], b + 1)
                act.copy(lat_hi[:, b, :], PS[:, 4, 0:S]).then_inc(s["s3_lhi"], 1)
            short(act, ((2, high_tokens), (3, high_latents)))

            act.wait_ge(s["ones"], 2)

            def high_parts(k, p, b):
                act.wait_ge(s["a_proj"], k + 1)
                if from_(k, 4):
                    act.wait_ge(s["a_st"], k - 3)
                for h in range(2):
                    for half in range(2):
                        last = act.activation(qq2[64 * half:64 * half + 64, p % 4, h, :], PS[64 * h:64 * h + 64, 0, 0:S], ACT.Copy,
                                              scale=float(HD) ** -0.5)
                for h in range(2):
                    act.copy(k1[0:64, p % 4, h, :], PS[64 * h:64 * h + 64, 0, S:2 * S])
                    last = act.copy(kk2[0:64, p % 4, h, :], PS[64 * h:64 * h + 64, 0, S:2 * S])
                last.then_inc(s["a_hi"], 1)

            def maxima(k, p, b):
                act.wait_ge(s["a_c"], k + 1)
                if from_(k, 4):
                    act.wait_ge(s["a_st"], k - 3)
                for h in range(2):
                    last = act.copy(ql[64:66, p % 4, h, :].rearrange("p (c t) -> p c t", c=C), PS[0:2, 3:5, 384:512])
                last.then_inc(s["a_cs"], 1)

            def exps(k, p, b):
                act.wait_ge(s["a_st"], k + 1)
                if from_(k, 2):
                    act.wait_ge(s["a_y"], k - 1)
                act.activation(pT[:, p % 2, :, 0:384], PS[:, 3:5, 0:384], ACT.Exp).then_inc(s["a_exp"], 1)

            def keep_values(b, g, wide, n):
                act.wait_ge(s["a_v"], n)
                if from_(b, 2):
                    act.wait_ge(s["a_y"], NP * (b - 2) + 2 * (g // 2) + 2)
                h0 = 4 * (g // 2)
                act.copy(v65[:, b % 2, g % 2, h0:h0 + 4 * wide, 0:HD],
                         PS[:, 6, 0:S * wide].rearrange("p (h d) -> p h d", h=4 * wide)).then_inc(s["a_vs"], wide)

            def next_values(k, p, b):
                for i, (seq, g, wide) in enumerate(value_steps(p, b)):
                    keep_values(seq, g, wide, made(k) + i + wide)

            def turned3(k, p, b):
                if p == NP - 1:
                    act.wait_ge(s["a3_xT"], b + 1)
                    if from_(b, 1):
                        act.wait_ge(s["a3_lg"], b)
                    act.copy(xT[:], PS[:, 6, 0:S]).then_inc(s["a3_xs"], 1)
                    act.copy(x3_hi[:, b, :], PS[:, 6, 0:S]).then_inc(s["a3_hi"], 1)

            def logits3(k, p, b):
                if p == NP - 1:
                    act.wait_ge(s["a3_lg"], b + 1)
                    lg = PS[:, 6, 0:C * 10].rearrange("p (c e) -> p c e", c=C)
                    act.copy(gateb[:, b, :, :], lg[:, :, 2:10])
                    act.copy(gcb[:, b, :, 0:2], lg[:, :, 0:2]).then_inc(s["a3_lgs"], 1)

            def gate_exp(n, i):
                act.wait_ge(s["s5g_d"], 2 * n + i + 1)
                act.activation((gb_, gd)[i][:, GATE[n], :], ga[:, GATE[n], :], ACT.Exp).then_inc(s["s5g_e"], 1)

            def tanh(b, par):
                act.wait_ge(s["f_ha"], b + 1)
                if from_(b, 1):
                    act.wait_ge(s["f_g"], b)
                act.activation(th, PS[:, 0:2, :].rearrange("p n (m t) -> p (n m) t", m=2), ACT.Tanh, scale=0.5).then_inc(s["f_th"], 1)

            def hidden_high(b, par):
                act.wait_ge(s["f_g"], b + 1)
                if from_(b, 2):
                    act.wait_ge(s["f_sh"], b - 1)
                act.copy(hT_hi[:, par], hg).then_inc(s["f_ghi"], 1)

            def beginning(step):
                def stage(k, p, b):
                    if isinstance(k, int) and k == NK - 1:
                        if step == 0:
                            act.wait_ge(s["a_y"], NK)
                            tanh(0, 0)
                        if step == 1:
                            gate_exp(0, 0)
                        if step == 2:
                            hidden_high(0, 0)
                        if step == 3:
                            gate_exp(0, 1)
                return stage

            pairs(act, ((0, high_parts), (2, maxima), (0, next_values), (6, beginning(0)), (7, beginning(1)), (8, beginning(2)),
                        (9, turned3), (10, logits3), (10, beginning(3)), (3, exps)))

            tanh(1, 1)
            hidden_high(1, 1)
            gate_exp(1, 0)
            gate_exp(1, 1)
            with act.Fori(1, B // 2) as i:
                for par in range(2):
                    tanh(2 * i + par, par)
                    hidden_high(2 * i + par, par)


        @block.vector
        def _(v):
            def statistics(k):
                return v.bn_stats(stats[:, k, :], X[:, k, :])

            def moments_all(n):
                for part, T in enumerate(PARTS):
                    if n == 1:
                        for k in range(T.start, T.stop):
                            if k % 4 == 0:
                                v.wait_ge(s[f"ld_x{k // 4}"], 16)
                            last = statistics(k)
                        last.then_inc(s["s1_vec"], 1)
                        v.wait_ge(s["s1_vec"], 2 * part + 1)
                    for k in range(T.start, T.stop):
                        last = v.bn_aggr(mv[:, k, :], stats[:, k, :])
                    last.then_inc(s["s1_vec"], 1)
                    v.wait_ge(s["s1_vec"], 2 * part + 2 if n == 1 else 5 + part)
                    v.tensor_scalar(veps[:, T], mv[:, T, 1], LN_EPS, None, ALU.add).then_inc(s["s1_va"], 1)

            def moments(b, link, start, stage):
                for c in range(C):
                    last = v.bn_stats(stats[:, c, :], Xb[:, b, c, :])
                link(last, start, apart=True)
                for c in range(C):
                    last = v.bn_aggr(mv[:, c, :], stats[:, c, :])
                link(last, start)
                v.tensor_scalar(veps[:, 0:C], mv[:, 0:C, 1], LN_EPS, None, ALU.add).then_inc(s[stage + "_va"], 1)

            def normalised(b, stage, n):
                v.wait_ge(s[stage + "_rs"], n)
                for c in range(C):
                    last = v.tensor_scalar(xn[:, c, :], Xb[:, b, c, :], mv[:, c, 0:1], rstd[:, c:c + 1],
                                           ALU.subtract, ALU.mult)
                return last

            def layernorm(b, link, start, stage, n):
                moments(b, link, start, stage)
                return normalised(b, stage, n)

            moments_all(1)

            def apply1(k, c, b):
                if isinstance(k, int) and k in (0, PARTS[1].start):
                    v.wait_ge(s["s1_rs"], 1 + k // PARTS[1].start)
                if from_(k, 2):
                    v.wait_ge(s["s1_xT"], k - 1)
                v.tensor_scalar(xn[:, c, :], X[:, k, :], mv[:, k, 0:1], rstd3[:, k, :],
                                ALU.subtract, ALU.mult).then_inc(s["s1_xn"], 1)

            def features(k, c, b):
                if from_(k, 2):
                    v.wait_ge(s["s1_kv"], k - 1)
                    v.wait_ge(s["s1_mul"], k - 1)
                v.wait_ge(s["s1_exp"], k + 1)
                v.scalar_tensor_tensor(out=qk[:, c, :], in0=PS[:, 7, 0:2 * D], scalar=0.0,
                                       in1=ex[:, c, :], op0=ALU.max, op1=ALU.add).then_inc(s["s1_phi"], 1)

            def times_queries(k, c, b):
                v.wait_ge(s["s1_pre"], k + 1)
                v.tensor_tensor(mul.rearrange("p (g e a) -> p g e a", g=3, e=3),
                                PS[:, 3 * c:3 * c + 3, 0:3 * D].rearrange("p g (e a) -> p g e a", e=3),
                                qk[:, c, 0:D][:, None, None, :].broadcast_to([128, 3, 3, D]), ALU.mult).then_inc(s["s1_mul"], 1)

            def sums(k, c, b):
                v.wait_ge(s["s1_mul"], k + 1)
                v.tensor_reduce(nd, mul.rearrange("p (n d) -> p n d", d=LD), AX_X, ALU.add).then_inc(s["s1_red"], 1)

            def attention(k, c, b):
                v.wait_ge(s["s1_red"], 3 * k + 1)
                v.tensor_scalar(den0[:], nd[:, LH * LD:LH * LD + LH], EPS, None, ALU.max).then_inc(s["s1_red"], 1)
                v.wait_ge(s["s1_red"], 3 * k + 2)
                v.reciprocal(den0[:], den0[:]).then_inc(s["s1_red"], 1)
                v.wait_ge(s["s1_red"], 3 * k + 3)
                if from_(k, 2):
                    v.wait_ge(s["s1_oT"], k - 1)
                v.tensor_tensor(o0[:, c, :].rearrange("p (h e) -> p e h", h=LH),
                                nd[:, 0:LH * LD].rearrange("p (e h) -> p e h", e=LD),
                                den0[:][:, None, :].broadcast_to([128, LD, LH]), ALU.mult).then_inc(s["s1_o"], 1)

            def residual1(k, c, b):
                v.wait_ge(s["s1_pr"], k + 1)
                v.wait_ge(s["s1_exp"], upto(k + 4, NT))
                v.tensor_tensor(X[:, k, :], X[:, k, :], PS[:, 7, 3 * D:4 * D], ALU.add).then_inc(s["s1_res"], 1)

            def statistics1(k, c, b):
                wait_apart(v, ("s1_res", k + 1))
                statistics(k).then_inc(s["s1_stat"], 1)

            tiles(v, ((0, apply1), (3, times_queries), (3, sums), (1, features), (3, attention), (4, residual1), (4, statistics1)))
            v.wait_ge(s["s1_stat"], NT)
            moments_all(2)

            def apply1b(b, par, _):
                if isinstance(b, int) and C * b in (0, PARTS[1].start):
                    v.wait_ge(s["s1_rs"], 3 + C * b // PARTS[1].start)
                if from_(b, 2):
                    v.wait_ge(s["s1_x1T"], b - 1)
                for c in range(C):
                    k = C * b + c
                    last = v.tensor_scalar((xn, o0)[par][:, c, :], X[:, k, :], mv[:, k, 0:1], rstd3[:, k, :],
                                           ALU.subtract, ALU.mult)
                last.then_inc(s["s1_xn1"], 1)
            sequences(v, ((0, apply1b),))

            link, _ = chain(v, "s2_vec")
            v.wait_ge(s["s1_lgs"], B)
            v.wait_ge(s["ld_w1"], 16 * 13)
            wideE = [128, NT, E]

            def over(t):
                return t[:].broadcast_to(wideE)
            descb = desc[:, None, :].broadcast_to(wideE)

            def first_max(link, vals, onehot, scratch):
                link(v.tensor_reduce(gm[:], vals, AX_X, ALU.max))
                link(v.tensor_tensor(scratch, vals, over(gm), ALU.is_equal))
                link(v.tensor_tensor(scratch, scratch, descb, ALU.mult))
                link(v.tensor_reduce(gs[:], scratch, AX_X, ALU.max))
                link(v.tensor_tensor(onehot, scratch, over(gs), ALU.is_equal))

            link(v.tensor_tensor(gate[:], gate[:], bg0[:, None, :].broadcast_to(wideE), ALU.add))
            link(v.tensor_reduce(gm[:], gate[:], AX_X, ALU.max))
            v.tensor_tensor(ga[:], gate[:], over(gm), ALU.subtract).then_inc(s["s2_d"], 1)
            v.wait_ge(s["s2_e"], 1)
            link(v.tensor_reduce(gs[:], gb_[:], AX_X, ALU.add))
            link(v.reciprocal(gs[:], gs[:]))
            link(v.tensor_tensor(gate[:], gb_[:], over(gs), ALU.mult))
            first_max(link, gate[:], gb_[:], ga[:])
            link(v.scalar_tensor_tensor(out=gc[:], in0=gb_[:], scalar=-2.0, in1=gate[:], op0=ALU.mult, op1=ALU.add))
            first_max(link, gc[:], gd[:], ga[:])
            link(v.tensor_tensor(gb_[:], gb_[:], gd[:], ALU.add))
            link(v.tensor_tensor(gate[:], gate[:], gb_[:], ALU.mult))
            link(v.tensor_reduce(dsum[:], gate[:].rearrange("p (b c) e -> p (c e) b", c=C), AX_X, ALU.add))
            link(v.tensor_scalar(dsum[:], dsum[:], EPS, None, ALU.add))
            link(v.reciprocal(dsum[:], dsum[:]))
            link(v.tensor_tensor(route[:], gate[:].rearrange("p (b c) e -> p c b e", c=C),
                                 dsum[:].rearrange("p (c e) -> p c e", c=C)[:, :, None, :].broadcast_to([128, C, B, E]), ALU.mult))
            v.tensor_scalar(route[:], route[:], float(B), None, ALU.mult).then_inc(s["s2_rt"], 1)
            v.wait_ge(s["s2_rT"], 1)
            v.wait_ge(s["s1_x1s"], 2 * B)
            link(v.tensor_copy(rank[0][:], PS[0:B * E, 0, 0:S]))
            for r in range(K_TOP // 8):
                link(v.max(top8[:], rank[r % 2][:]))
                link(v.match_replace(rank[(r + 1) % 2][:], top8[:], rank[r % 2][:], -1.0))
            v.tensor_scalar(selb[:], rank[(K_TOP // 8) % 2][:], 0.0, None, ALU.is_lt)
            v.tensor_scalar(self32[:], rank[(K_TOP // 8) % 2][:], 0.0, None, ALU.is_lt).then_inc(s["s2_sel"], 1)

            def choose(b, par, _):
                v.wait_ge(s["s3_g"], b + 1)
                if from_(b, 2):
                    v.wait_ge(s["s3_o"], b - 1)
                v.wait_ge(s["s3_m"], b + 1)
                v.tensor_tensor(hm[:, par], PS[:, par, :].rearrange("p (n t) -> p n t", n=2), hs[:, b], ALU.mult).then_inc(s["s3_hm"], 1)

            def residual_s3(b, par, _):
                v.wait_ge(s["s3_o"], b + 1)
                v.tensor_tensor(Xb[:, b, :, :], Xb[:, b, :, :], PS[:, 2, 0:S].rearrange("p (c d) -> p c d", c=C), ALU.add).then_inc(s["s3_res"], 1)

            def moments_s3(b, par, _):
                wait_apart(v, ("s3_res", b + 1))
                link, count = chain(v, "s3_vec")
                moments(b, link, b * 2, "s3")

            def apply_s3(b, par, _):
                if from_(b, 1):
                    v.wait_ge(s["s3_xT"], b)
                normalised(b, "s3", b + 1).then_inc(s["s3_xn"], 1)

            def low_tokens(b, par, _):
                v.wait_ge(s["s3_hi"], b + 1)
                v.tensor_tensor(x2_lo[:, b, :], PS[:, 3, 0:S], x2_hi[:, b, :].bitcast(F32), ALU.subtract).then_inc(s["s3_lo"], 1)

            def low_latents(b, par, _):
                v.wait_ge(s["s3_lhi"], b + 1)
                v.tensor_tensor(lat_lo[:, b, :], PS[:, 4, 0:S], lat_hi[:, b, :].bitcast(F32), ALU.subtract).then_inc(s["s3_llo"], 1)
            short(v, ((0, choose), (2, apply_s3), (1, residual_s3), (1, moments_s3), (2, low_tokens), (3, low_latents)))

            def low_parts(k, p, b):
                v.wait_ge(s["a_hi"], k + 1)
                for h in range(2):
                    ps = PS[64 * h:64 * h + 64, 0, :]
                    v.tensor_tensor(kk2[64:128, p % 4, h, :], ps[:, S:2 * S], kk2[0:64, p % 4, h, :].bitcast(F32), ALU.subtract)
                    last = v.scalar_tensor_tensor(out=ql[0:64, p % 4, h, :], in0=ps[:, 0:S], scalar=float(HD) ** -0.5,
                                                  in1=qq2[0:64, p % 4, h, :].bitcast(F32), op0=ALU.mult, op1=ALU.subtract)
                last.then_inc(s["a_lo"], 1)

            def row_max(k, p, b):
                v.wait_ge(s["a_s"], k + 1)
                if from_(k, 2):
                    v.wait_ge(s["a_c"], k - 1)
                v.tensor_reduce(negm[:, p % 2, 0, :], PS[:, 1:3, 256:384], AX_X, ALU.max, negate=True)
                v.tensor_reduce(negm[:, p % 2, 1, :], PS[:, 1:3, 0:256], AX_X, ALU.max, negate=True).then_inc(s["a_max"], 1)

            def normalise(k, p, b):
                v.wait_ge(s["a_y"], k + 1)
                if from_(k, 2):
                    v.wait_ge(s["a_yT"], k - 1)
                y = PS[:, 5, 0:C * 2 * (HD + 1)].rearrange("p (c h d) -> p c h d", c=C, h=2)
                v.reciprocal(rden[:, p % 2], y[:, :, :, HD:HD + 1]).then_inc(s["a_rec"], 1)
                v.wait_ge(s["a_rec"], k + 1)
                v.tensor_tensor(yn[:, p % 2], y[:, :, :, 0:HD], rden[:, p % 2].broadcast_to([128, C, 2, HD]),
                                ALU.mult).then_inc(s["a_yn"], 1)

            def turned_y(k, p, b):
                v.wait_ge(s["a_yT"], k + 1)
                if from_(k, 1):
                    v.wait_ge(s["a_o"], k)
                ps = PS[:, 6, S:2 * S]
                v.tensor_copy(y_hi[:], ps).then_inc(s["a_yhi"], 1)
                v.wait_ge(s["a_yhi"], k + 1)
                v.tensor_tensor(y_lo[:], ps, y_hi[:].bitcast(F32), ALU.subtract).then_inc(s["a_ylo"], 1)

            def output(k, p, b):
                if p == NP - 1:
                    v.wait_ge(s["a_o"], k + 1)
                    v.tensor_copy(oT[:], PS[:, 7, 0:S]).then_inc(s["a_ot"], 1)

            def residual(k, p, b):
                if p == NP - 1:
                    v.wait_ge(s["a_to"], b + 1)
                    v.tensor_tensor(Xb[:, b, :, :], Xb[:, b, :, :], PS[:, 7, S:2 * S].rearrange("p (c d) -> p c d", c=C), ALU.add).then_inc(s["a_x"], 1)

            def norm3(k, p, b):
                if p == NP - 1:
                    link, count = chain(v, "a3_vec")
                    wait_apart(v, ("a_x", b + 1))
                    moments(b, link, b * 2, "a3")

            def apply3(k, p, b):
                if p == NP - 1:
                    normalised(b, "a3", b + 1).then_inc(s["a3_xn"], 1)

            def low3(k, p, b):
                if p == NP - 1:
                    v.wait_ge(s["a3_hi"], b + 1)
                    v.tensor_tensor(x3_lo[:, b, :], PS[:, 6, 0:S], x3_hi[:, b, :].bitcast(F32), ALU.subtract).then_inc(s["a3_lo"], 1)

            a_ps, b_ps = (PS[:, 2 * n:2 * n + 2, :].rearrange("p n (m t) -> p (n m) t", m=2) for n in range(2))

            def hidden(b, par):
                v.wait_ge(s["f_th"], b + 1)
                v.scalar_tensor_tensor(out=th, in0=th, scalar=1.0, in1=a_ps, op0=ALU.add, op1=ALU.mult).then_inc(s["f_th2"], 1)

            def hidden_gated(b, par):
                v.wait_ge(s["f_hb"], b + 1)
                if from_(b, 1):
                    v.wait_ge(s["f_ghi"], b)
                v.wait_ge(s["f_th2"], b + 1)
                v.scalar_tensor_tensor(out=hg, in0=th, scalar=0.5, in1=b_ps, op0=ALU.mult, op1=ALU.mult).then_inc(s["f_g"], 1)

            def hidden_low(b, par):
                v.wait_ge(s["f_ghi"], b + 1)
                v.tensor_tensor(hT_lo[:, par], hg, hT_hi[:, par].bitcast(F32), ALU.subtract).then_inc(s["f_glo"], 1)

            def gate_part(n, part):
                T = GATE[n]
                nt = T.stop - T.start
                link, count = chain(v, "s5g_vec", n * GATE_LINKS + sum(GATE_PARTS[:part]))
                lg, groups, x, y, top, total = gate[:, T, :], gc[:, T, :], gb_[:, T, :], gd[:, T, :], gm[:, T, :], gs[:, T, :]
                less = ga[:, T, :]
                by_group = "p n (g e) -> p n g e"

                def over(a, *shape):
                    return a.broadcast_to([128, nt, *shape])

                def first_max(vals, onehot):
                    link(v.tensor_reduce(top, vals, AX_X, ALU.max))
                    link(v.tensor_tensor(less, vals, over(top, E), ALU.is_equal))
                    link(v.tensor_tensor(less, less, over(desc[:, None, :], E), ALU.mult))
                    link(v.tensor_reduce(total, less, AX_X, ALU.max))
                    link(v.tensor_tensor(onehot, less, over(total, E), ALU.is_equal))

                if part == 0:
                    link(v.tensor_tensor(groups[:, :, 0:2], groups[:, :, 0:2], over(bg1[:, None, 0:2], 2), ALU.add))
                    link(v.tensor_tensor(lg, lg, over(bg1[:, None, 2:10], E), ALU.add))
                    link(v.tensor_reduce(top, groups[:, :, 0:2], AX_X, ALU.max))
                    link(v.memset(less, 0.0))
                    v.tensor_tensor(less[:, :, 0:2], groups[:, :, 0:2], over(top, 2), ALU.subtract).then_inc(s["s5g_d"], 1)
                if part == 1:
                    v.wait_ge(s["s5g_e"], 2 * n + 1)
                    link(v.tensor_reduce(total, x[:, :, 0:2], AX_X, ALU.add))
                    link(v.reciprocal(total, total))
                    link(v.tensor_tensor(groups[:, :, 2:4], x[:, :, 0:2], over(total, 2), ALU.mult))
                    link(v.tensor_reduce(top, groups[:, :, 2:4], AX_X, ALU.max))
                    link(v.tensor_tensor(groups[:, :, 4:5], groups[:, :, 2:3], groups[:, :, 3:4], ALU.is_ge))
                    link(v.tensor_scalar(groups[:, :, 5:6], groups[:, :, 4:5], -1.0, 1.0, ALU.mult, ALU.add))
                if part == 2:
                    link(v.tensor_reduce(groups[:, :, 6:8], lg.rearrange(by_group, g=2), AX_X, ALU.max))
                    link(v.tensor_tensor(less.rearrange(by_group, g=2), lg.rearrange(by_group, g=2),
                                         over(groups[:, :, 6:8][:, :, :, None], 2, 4), ALU.subtract))
                    v.tensor_copy(x.rearrange(by_group, g=2), over(groups[:, :, 4:6][:, :, :, None], 2, 4)).then_inc(s["s5g_d"], 1)
                if part == 3:
                    v.wait_ge(s["s5g_e"], 2 * n + 2)
                    link(v.tensor_tensor(y, y, x, ALU.mult))
                    link(v.tensor_reduce(total, y, AX_X, ALU.add))
                    link(v.reciprocal(total, total))
                    link(v.tensor_tensor(lg, y, over(total, E), ALU.mult))
                    link(v.tensor_tensor(lg, lg, over(top, E), ALU.mult))
                if part == 4:
                    first_max(lg, x)
                    link(v.scalar_tensor_tensor(out=groups, in0=x, scalar=-2.0, in1=lg, op0=ALU.mult, op1=ALU.add))
                if part == 5:
                    first_max(groups, y)
                    link(v.tensor_tensor(x, x, y, ALU.add))
                    link(v.tensor_tensor(lg, lg, x, ALU.mult))
                assert count[0] == GATE_PARTS[part], count

            def beginning(step):
                def stage(k, p, b):
                    if isinstance(k, int) and k == NK - 1:
                        if step == 0:
                            v.wait_ge(s["a3_lgs"], B - 1)
                            gate_part(0, 0)
                            gate_part(0, 1)
                        if step == 1:
                            hidden(0, 0)
                            hidden_gated(0, 0)
                            gate_part(0, 2)
                        if step == 2:
                            hidden_low(0, 0)
                            for part in (3, 4, 5):
                                gate_part(0, part)
                return stage

            pairs(v, ((5, turned_y), (6, output), (1, row_max), (6, residual), (0, low_parts), (4, normalise), (7, norm3),
                      (7, beginning(0)), (8, apply3), (8, beginning(1)), (9, low3), (10, beginning(2))))

            def weigh(b, c, n):
                k = 4 * b + 2 * c + n
                if n == 0 and from_(b, 1):
                    v.wait_ge(s["f_ad"], 2 * (C * (b - 1) + c) + 2)
                v.wait_ge(s["f_ex"], k + 1)
                v.tensor_tensor(prod[:, c, 4 * n:4 * n + 4, :], PS[:, EXPERT_BANKS[2 * c + n], :].rearrange("p (m d) -> p m d", m=4),
                                gateb[:, b, c, 4 * n:4 * n + 4][:, :, None].broadcast_to([128, 4, D]), ALU.mult).then_inc(s["f_pr"], 1)

            def final(b):
                v.wait_ge(s["f_s1"], C * b + C)
                v.wait_ge(s["f_sh"], b + 1)
                v.tensor_tensor(Xb[:, b, :, :], Xb[:, b, :, :], PS[:, 6, 0:S].rearrange("p (c d) -> p c d", c=C), ALU.add).then_inc(s["f_r1"], 1)
                v.wait_ge(s["f_r1"], b + 1)
                v.tensor_tensor(Xb[:, b, :, :], Xb[:, b, :, :], acc1, ALU.add).then_inc(s["f_y"], 1)

            def ffn(b, par, more=True):
                weigh(b, 0, 0)
                if more:
                    hidden(b + 1, 1 - par)
                if from_(b, 1):
                    final(b - 1)
                weigh(b, 0, 1)
                if more:
                    hidden_gated(b + 1, 1 - par)
                weigh(b, 1, 0)
                if more:
                    hidden_low(b + 1, 1 - par)
                weigh(b, 1, 1)
            ffn(0, 0)
            v.wait_ge(s["a3_lgs"], B)
            for part in range(len(GATE_PARTS)):
                gate_part(1, part)
            with v.Fori(0, B // 2 - 1) as i:
                ffn(2 * i + 1, 1)
                ffn(2 * i + 2, 0)
            ffn(B - 1, 1, more=False)
            final(B - 1)

        @block.tensor
        def _(pe):
            def transposes(bank, src, sem_name):
                for c in range(C):
                    last = pe.transpose(PS[:, bank, 128 * c:128 * c + 128], src[:, c, :], ident[:])
                last.then_inc(s[sem_name], 1)

            def turn_output(k, c, b):
                pe.wait_ge(s["s1_o"], k + 1)
                pe.wait_ge(s["s1_xTs"], upto(k + 4, NT))
                if from_(k, 1):
                    pe.wait_ge(s["s1_oTs"], k)
                pe.transpose(PS[:, 6, 128:256], o0[:, c, :], ident[:]).then_inc(s["s1_oT"], 1)

            def turn_tokens(k, c, b):
                pe.wait_ge(s["s1_xn"], k + 1)
                if from_(k, 1):
                    pe.wait_ge(s["s1_xTs"], k)
                if from_(k, 4):
                    pe.wait_ge(s["s1_oTs"], k - 3)
                pe.transpose(PS[:, 6, 0:128], xn[:, c, :], ident[:]).then_inc(s["s1_xT"], 1)

            def project1(k, c, b):
                pe.wait_ge(s["s1_xTs"], k + 1)
                if from_(k, 1):
                    pe.wait_ge(s["s1_phi"], k)
                if from_(k, 4):
                    pe.wait_ge(s["s1_res"], k - 3)
                pe.matmul(PS[:, 7, 0:3 * D], xT[:, 128 * c:128 * c + 128], wqkv[:], start=True, stop=True).then_inc(s["s1_qkv"], 1)

            def project_output(k, c, b):
                pe.wait_ge(s["s1_oTs"], k + 1)
                pe.wait_ge(s["s1_phi"], upto(k + 3, NT))
                if from_(k, 1):
                    pe.wait_ge(s["s1_res"], k)
                pe.matmul(PS[:, 7, 3 * D:4 * D], oT[:, 128 * c:128 * c + 128], wo0[:], start=True, stop=True).then_inc(s["s1_pr"], 1)

            def states(k, c, b):
                pe.wait_ge(s["s1_kv"], k + 1)
                if from_(k, 2):
                    pe.wait_ge(s["s1_mul"], k - 1)
                for g in range(3):
                    w, dst = slice(3 * D * g, 3 * D * g + 3 * D), PS[:, 3 * c + g, 0:3 * D]
                    if c == 0:
                        last = pe.matmul(dst, causal[:], kv[:, b % 2, w], start=True, stop=True)
                    else:
                        last = pe.matmul(dst, causal[:], kv[:, 2, w], start=False, stop=True, skip_group_check=True)
                last.then_inc(s["s1_pre"], 1)

            def carry(k, c, b):
                if c == 1:
                    pe.wait_ge(s["s1_kv"], k)
                    if from_(k, 2):
                        pe.wait_ge(s["s1_mul"], k - 1)
                    for g in range(3):
                        pe.matmul(PS[:, 3 * c + g, 0:3 * D], ones[:], kv[:, b % 2, 3 * D * g:3 * D * g + 3 * D],
                                  start=True, stop=False, skip_group_check=True)

            pe.wait_ge(s["ld_w0"], 16 * 5)
            pe.wait_ge(s["ones"], 1)
            tiles(pe, ((4, turn_output), (4, project_output), (1, project1), (2, states), (0, turn_tokens), (1, carry)))

            def turn1(b, par, _):
                pe.wait_ge(s["s1_xn1"], b + 1)
                if from_(b, 2):
                    pe.wait_ge(s["s1_x1s"], 2 * b - 2)
                for c in range(C):
                    last = pe.transpose(PS[:, par, 128 * c:128 * c + 128], (xn, o0)[par][:, c, :], ident[:])
                last.then_inc(s["s1_x1T"], 1)

            def logits1(b, par, _):
                pe.wait_ge(s["s1_x1s"], 2 * b + 1)
                if from_(b, 2):
                    pe.wait_ge(s["s1_lgs"], b - 1)
                for c in range(C):
                    last = pe.matmul(PS[:, 2 + par, E * c:E * c + E], (xT, oT)[par][:, 128 * c:128 * c + 128], wg0[:], start=True, stop=True)
                last.then_inc(s["s1_lg"], 1)

            sequences(pe, ((0, turn1), (1, logits1)))

            def hidden0(b, par, _):
                if from_(b, 2):
                    pe.wait_ge(s["s3_g"], b - 1)
                for half in range(2):
                    last = pe.matmul(PS[:, 4 + par, S * half:S * half + S], w1a[:, half, :], x1T[:, b, :], start=True, stop=True)
                last.then_inc(s["s3_h"], 1)
            pe.wait_ge(s["ld_w1"], 16 * 13)

            def turn_route(b, par, _):
                if isinstance(b, int) and b == B // 2 - 1:
                    pe.wait_ge(s["s2_rt"], 1)
                    for c in range(C):
                        last = pe.transpose(PS[0:B * E, 0, 128 * c:128 * c + 128], route[:, c, :, :].rearrange("p b e -> p (b e)"), ident[:])
                    last.then_inc(s["s2_rT"], 1)
            sequences(pe, ((0, hidden0), (0, turn_route)))

            pe.wait_ge(s["w_split"], NT)
            pe.wait_ge(s["a_rows"], 1)
            pe.wait_ge(s["s3_b2"], 1)
            pe.wait_ge(s["s2_sel"], 1)

            def spread(b, par, _):
                if from_(b, 2):
                    pe.wait_ge(s["s3_hm"], b - 1)
                for half in range(2):
                    last = pe.matmul(PS[:, par, S * half:S * half + S], expand[:, b, 128 * half:128 * half + 128], selb[:], start=True, stop=True)
                last.then_inc(s["s3_m"], 1)

            def outputs0(b, par, _):
                pe.wait_ge(s["s3_hm"], b + 1)
                if from_(b, 1):
                    pe.wait_ge(s["s3_res"], b)
                for c in range(C):
                    t = slice(128 * c, 128 * c + 128)
                    for half in range(2):
                        pe.matmul(PS[:, 2, t], hm[:, par, half, t], w2a[:, half, :], start=(half == 0), stop=False)
                    last = pe.matmul(PS[:, 2, t], self32[:, t], b2b[:, b, :], start=False, stop=True)
                last.then_inc(s["s3_o"], 1)

            def turn_s3(b, par, _):
                pe.wait_ge(s["s3_xn"], b + 1)
                if from_(b, 1):
                    pe.wait_ge(s["s3_lo"], b)
                transposes(3, xn, "s3_xT")

            def latents0(b, par, _):
                pe.wait_ge(s["s3_lo"], b + 1)
                if from_(b, 1):
                    pe.wait_ge(s["s3_llo"], b)
                mm3(pe, PS[:, 4, 0:S], (wd_hi, wd_lo), (x2_hi[:, b, :], x2_lo[:, b, :])).then_inc(s["s3_lat"], 1)
            short(pe, ((0, spread), (1, outputs0), (2, turn_s3), (3, latents0)))
            pe.wait_ge(s["s3_llo"], B)

            def turn_max(k, p, b):
                if from_(k, 2):
                    pe.wait_ge(s["a_exp"], k - 1)
                elif k == 1:
                    pe.wait_ge(s["a_cs"], 1)
                pe.wait_ge(s["a_max"], k + 1)
                for c in range(C):
                    last = pe.transpose(PS[0:2, 3 + c, 384:512], negm[:, p % 2, c, :], ident[:])
                last.then_inc(s["a_c"], 1)

            def turn_y(k, p, b):
                pe.wait_ge(s["a_yn"], k + 1)
                pe.wait_ge(s["a_vs"], made(k + 5))
                if p == 4 and from_(b, 1):
                    pe.wait_ge(s["a3_hi"], b)
                    pe.wait_ge(s["a3_lo"], b)
                if p == 5 and from_(b, 1):
                    pe.wait_ge(s["a3_lgs"], b)
                for c in range(C):
                    last = pe.transpose(PS[:, 6, S + 128 * c:S + 128 * c + 128], yn[:, p % 2, c, :, :].rearrange("p h d -> p (h d)"), ident[:])
                last.then_inc(s["a_yT"], 1)

            def project(k, p, b):
                if from_(k, 1):
                    pe.wait_ge(s["a_lo"], k)
                w = slice(128 * p, 128 * p + 128)
                mm3(pe, PS[:, 0, 0:S], (wq_hi[:, w], wq_lo[:, w]), (x2_hi[:, b, :], x2_lo[:, b, :]))
                mm3(pe, PS[:, 0, S:2 * S], (wk_hi[:, w], wk_lo[:, w]), (lat_hi[:, b, :], lat_lo[:, b, :])).then_inc(s["a_proj"], 1)

            def attend(k, p, b):
                pe.wait_ge(s["a_msk"], k + 1)
                pe.wait_ge(s["a_vs"], NV * (b + 1))
                if from_(k, 1):
                    pe.wait_ge(s["a_yn"], k)
                for c in range(C):
                    for h in range(2):
                        dst = PS[:, 5, 65 * (2 * c + h):65 * (2 * c + h) + 65]
                        for kt in range(c + 1):
                            last = pe.matmul(dst, pT[:, p % 2, h, 128 * (c + kt):128 * (c + kt) + 128],
                                             v65[:, b % 2, kt, 2 * p + h, :], start=(kt == 0), stop=(kt == c))
                last.then_inc(s["a_y"], 1)

            def scores(k, p, b):
                pe.wait_ge(s["a_lo"], k + 1)
                if from_(k, 1):
                    pe.wait_ge(s["a_max"], k)
                for h in range(2):
                    pe.matmul(PS[:, 1 + h, 0:256], qq2[:, p % 4, h, 128:256], kk2[:, p % 4, h, :],
                              start=True, stop=False, skip_group_check=True)
                    pe.matmul(PS[:, 1 + h, 256:384], qq2[:, p % 4, h, 0:128], kk2[:, p % 4, h, 0:128],
                              start=False, stop=False, skip_group_check=True)
                    last = pe.matmul(PS[:, 1 + h, 128:384].rearrange("p (c t) -> p c t", c=C), identb[:],
                                     maskneg[:, None, :].broadcast_to([128, C, 128]), start=False, stop=True, skip_group_check=True)
                last.then_inc(s["a_s"], 1)

            def values(b, g, wide):
                pe.wait_ge(s["a_ls"], b + 1)
                t, w = slice(128 * (g % 2), 128 * (g % 2) + 128), slice(S * (g // 2), S * (g // 2 + wide))
                mm3(pe, PS[:, 6, 0:S * wide], (ls_hi[:, t], ls_lo[:, t]), (wv_hi[:, w], wv_lo[:, w])).then_inc(s["a_v"], wide)

            def next_values(k, p, b):
                for i, (seq, g, wide) in enumerate(value_steps(p, b)):
                    if i == 0 and from_(k, 5):
                        pe.wait_ge(s["a_ylo"], k - 4)
                    elif from_(k, 1) or i:
                        pe.wait_ge(s["a_vs"], made(k) + i)
                    values(seq, g, wide)

            def scores_t(k, p, b):
                pe.wait_ge(s["a_cs"], upto(k + 2, NK))
                if from_(k, 1):
                    pe.wait_ge(s["a_exp"], k)
                for h in range(2):
                    for c in range(C):
                        t, kt = slice(128 * c, S), slice(128 * c, 128 * c + 128)
                        dst = PS[:, 3 + h, 256 * c:256 + 128 * c]
                        pe.matmul(dst, k1[:, p % 4, h, kt], ql[:, p % 4, h, t], start=(c == 0), stop=False, skip_group_check=True)
                        last = pe.matmul(dst, kk2[:, p % 4, h, kt], qq2[:, p % 4, h, t], start=False, stop=True, skip_group_check=True)
                last.then_inc(s["a_st"], 1)

            def add_output(k, p, b):
                pe.wait_ge(s["a_ylo"], k + 1)
                if p == 0 and from_(b, 1):
                    pe.wait_ge(s["a_x"], b)
                w = slice(128 * p, 128 * p + 128)
                mm3(pe, PS[:, 7, 0:S], (wo_hi[:, w], wo_lo[:, w]), (y_hi[:], y_lo[:]),
                    start=(p == 0), stop=(p == NP - 1), skip=True).then_inc(s["a_o"], 1)

            def turn_output(k, p, b):
                if p == NP - 1:
                    pe.wait_ge(s["a_ot"], b + 1)
                    for c in range(C):
                        last = pe.transpose(PS[:, 7, S + 128 * c:S + 128 * c + 128], oT[:, 128 * c:128 * c + 128], ident[:])
                    last.then_inc(s["a_to"], 1)

            def turn3(k, p, b):
                if p == NP - 1:
                    pe.wait_ge(s["a3_xn"], b + 1)
                    pe.wait_ge(s["a_vs"], made(k + 10))
                    pe.wait_ge(s["a_ylo"], upto(k + 5, NK))
                    transposes(6, xn, "a3_xT")

            def logits3(k, p, b):
                if p == NP - 1:
                    pe.wait_ge(s["a3_xs"], b + 1)
                    pe.wait_ge(s["a_vs"], made(k + 11))
                    pe.wait_ge(s["a3_lo"], b + 1)
                    pe.wait_ge(s["a_ylo"], upto(k + 6, NK))
                    for c in range(C):
                        last = pe.matmul(PS[:, 6, 10 * c:10 * c + 10], xT[:, 128 * c:128 * c + 128], wg1[:], start=True, stop=True)
                    last.then_inc(s["a3_lg"], 1)

            def hidden(b, par):
                if from_(b, 1):
                    pe.wait_ge(s["f_g"], b)
                x3 = (x3_hi[:, b, :], x3_lo[:, b, :])
                for n in range(4):
                    for m in range(2):
                        o = 512 * (n % 2) + 256 * (n // 2) + 128 * m
                        last = mm3(pe, PS[:, n, S * m:S * m + S], (wh_hi[:, o:o + 128], wh_lo[:, o:o + 128]), x3)
                    if n == 1:
                        last.then_inc(s["f_ha"], 1)
                last.then_inc(s["f_hb"], 1)

            def begin_ffn(k, p, b):
                if isinstance(k, int) and k == NK - 1:
                    for name in ("a_lo", "a_max", "a_exp"):
                        pe.wait_ge(s[name], NK)
                    hidden(0, 0)

            def go_on_ffn(k, p, b):
                if isinstance(k, int) and k == NK - 1:
                    hidden(1, 1)

            pairs(pe, ((0, project), (5, turn_y), (2, turn_max), (1, scores), (6, turn_output), (4, attend), (0, next_values),
                       (9, turn3), (10, logits3), (3, scores_t), (5, add_output), (6, begin_ffn), (10, go_on_ffn)))

            pe.wait_ge(s["a3_lgs"], B)

            def outputs(b, par):
                pe.wait_ge(s["f_glo"], b + 1)
                for c in range(C):
                    t = slice(128 * c, 128 * c + 128)
                    for n in range(2):
                        k = 4 * b + 2 * c + n
                        if from_(k, 3):
                            pe.wait_ge(s["f_pr"], k if 2 * c + n == 0 else k - 2 if 2 * c + n == 3 else k - 3)
                        for m in range(2):
                            w = slice(1024 * m + 512 * n, 1024 * m + 512 * n + 512)
                            last = mm3(pe, PS[:, EXPERT_BANKS[2 * c + n], :], (hT_hi[:, par, 2 + m, t], hT_lo[:, par, 2 + m, t]), (we_hi[:, w], we_lo[:, w]),
                                       start=(m == 0), stop=(m == 1))
                        last.then_inc(s["f_ex"], 1)
                if from_(b, 1):
                    pe.wait_ge(s["f_y"], b)
                for c in range(C):
                    t = slice(128 * c, 128 * c + 128)
                    for m in range(2):
                        last = mm3(pe, PS[:, 6, t], (hT_hi[:, par, m, t], hT_lo[:, par, m, t]),
                                   (wf_hi[:, 128 * m:128 * m + 128], wf_lo[:, 128 * m:128 * m + 128]), start=(m == 0), stop=(m == 1))
                last.then_inc(s["f_sh"], 1)

            outputs(0, 0)
            with pe.Fori(0, B // 2 - 1) as i:
                hidden(2 * i + 2, 0)
                outputs(2 * i + 1, 1)
                hidden(2 * i + 3, 1)
                outputs(2 * i + 2, 0)
            outputs(B - 1, 1)


_INS = ["x", "wqkv0", "wout0", "wgate0", "bgate0", "w1_0", "b1_0", "w2_0", "b2_0", "wcut", "wgate1", "bgate1",
        "c_ident", "c_identb", "c_causal", "c_maskneg", "c_expand", "c_rows", "c_sel2", "c_desc"]


def kernel(**inputs):
    import ml_dtypes
    import numpy as np
    import concourse.bacc as _bacc
    from concourse.bass_utils import run_bass_kernel_spmd as _run

    i = {k: np.asarray(a) for k, a in inputs.items()}
    HDIM = NH * HD
    p = np.arange(128)
    j = np.arange(128)
    a = {
        "x": i["L0_attn_x"].reshape(NT, 128, D).transpose(1, 0, 2),
        "wqkv0": i["L0_attn_w_qkv"].T, "wout0": i["L0_attn_w_out"].T,
        "wgate0": i["L0_ffn_w_gate_w"], "bgate0": np.broadcast_to(i["L0_ffn_w_gate_b"], (128, E)),
        "w1_0": i["L0_ffn_W1"].reshape(2, 4, D, SUB).transpose(2, 0, 1, 3).reshape(128, 2, 128),
        "b1_0": i["L0_ffn_b1"].reshape(2, 128).T,
        "w2_0": i["L0_ffn_W2"].reshape(2, 128, D).transpose(1, 0, 2),
        "b2_0": np.broadcast_to(i["L0_ffn_b2"], (B, E, D)).reshape(B * E, D),
        "wcut": np.concatenate([
            i["L1_attn_w_kv_down"], i["L1_attn_w_kv_up"][:, :HDIM], i["L1_attn_w_kv_up"][:, HDIM:], i["L1_attn_w_q"],
            i["L1_attn_w_out"].reshape(NP, 128, D).transpose(1, 0, 2).reshape(128, NP * D),
            i["L1_ffn_w_in"].T, i["L1_ffn_w1"].T,
            i["L1_ffn_w2"].transpose(2, 0, 1).reshape(2, 128, E, D).transpose(1, 0, 2, 3).reshape(128, 2 * E * D),
            i["L1_ffn_w_out"].T.reshape(2, 128, D).transpose(1, 0, 2).reshape(128, 2 * D)], axis=1).reshape(128, NT, CHUNK),
        "wgate1": np.concatenate([i["L1_ffn_wg"], i["L1_ffn_we"]]).T,
        "bgate1": np.broadcast_to(np.concatenate([i["L1_ffn_gb"], i["L1_ffn_eb"]]), (128, 10)),
        "c_ident": np.eye(128, dtype=np.float32),
        "c_identb": np.eye(128, dtype=ml_dtypes.bfloat16),
        "c_causal": (j[None, :] >= p[:, None]).astype(np.float32),
        "c_maskneg": np.where(j[None, :] > p[:, None], -1e30, 0.0).astype(ml_dtypes.bfloat16),
        "c_expand": np.array([[[r == E * b + h // SUB for h in range(E * SUB)] for b in range(B)] for r in range(B * E)]).astype(ml_dtypes.bfloat16),
        "c_rows": (np.arange(B * E)[:, None] // E == np.arange(B)).astype(np.float32),
        "c_sel2": np.eye(2, dtype=np.float32)[:, :, None],
        "c_desc": np.broadcast_to(np.arange(E, 0, -1, dtype=np.float32), (128, E)),
    }
    nc = _bacc.Bacc("TRN2", target_bir_lowering=False, num_devices=1)
    arrays, args = {}, []
    for name in _INS:
        arr = np.ascontiguousarray(a[name])
        arrays[f"in_{name}"] = arr
        args.append(nc.dram_tensor(f"in_{name}", arr.shape, mybir.dt.from_np(arr.dtype), kind="ExternalInput").ap())
    args.append(nc.dram_tensor("out_0", (128, B, C, D), F32, kind="ExternalOutput").ap())
    build(nc, *args)
    r = _run(nc, [arrays], core_ids=[0])
    return r.results[0]["out_0"].transpose(1, 2, 0, 3).reshape(B, S, D)
```
